# Optimizing a Trainium2 kernel written in Bass

```python
import numpy as np
import jax
import jax.numpy as jnp

def _softmax(x, axis=-1):
    return jax.nn.softmax(x, axis=axis)

def _gelu(x):
    return jax.nn.gelu(x, approximate=True)

def _silu(x):
    return jax.nn.silu(x)

def _sigmoid(x):
    return jax.nn.sigmoid(x)

def _layernorm(x, axis=-1, eps=1e-05):
    m = jnp.mean(x, axis=axis, keepdims=True)
    v = jnp.var(x, axis=axis, keepdims=True)
    return (x - m) / jnp.sqrt(v + eps)

def _scatter_add(tgt, idx, src, axis=0):
    return tgt.at[idx].add(src)

def _segment_sum(src, seg, n):
    return jax.ops.segment_sum(src, seg, n)
kernel_name = 'mk_gnn_preln_d4_gnn_r32_e06255'

def setup_inputs(seed: int=0):
    np.random.seed(seed)
    _w = jnp.asarray

    def _rec_inputs():
        import jax
        import jax.numpy as jnp
        _gk = jax.random.key(seed)
        x = -0.0003713 + 1 * jax.random.normal(jax.random.fold_in(_gk, 1), (3125, 128), jnp.float32)
        _s = jax.random.randint(jax.random.fold_in(_gk, 2), (50000,), 0, 3125, jnp.int32)
        _d = jax.random.randint(jax.random.fold_in(_gk, 3), (50000,), 0, 3125, jnp.int32)
        _loop = jnp.arange(3125, dtype=jnp.int32)
        src = jnp.concatenate([_s, _d, _loop])
        dst = jnp.concatenate([_d, _s, _loop])
        _o = jnp.argsort(dst, stable=True)
        src = src[_o]
        dst = dst[_o]
        edge_type_9 = jax.random.randint(jax.random.fold_in(_gk, 12), (103125,), 0, 9, jnp.int32)
        return (x, src, dst, edge_type_9)
    x, src, dst, edge_type_9 = _rec_inputs()

    def _L0_gnn_setup():
        import jax, jax.numpy as jnp
        import numpy as np
        N = 3125
        E = 50000
        IN = 128
        H = 4
        C = 32
        OUT = H * C
        NEG_SLOPE = 0.2
        LN_EPS = 1e-05
        SM_EPS = 1e-16
        key = jax.random.key(seed)
        ks = jax.random.split(key, 6)
        x = jax.random.normal(ks[0], (N, IN), dtype=jnp.float32)
        edge_index = jax.random.randint(ks[1], (2, E), 0, N, dtype=jnp.int64)
        W = jax.random.normal(ks[2], (IN, OUT), dtype=jnp.float32) * 0.05
        a_src = jax.random.normal(ks[3], (H, C), dtype=jnp.float32) * 0.05
        a_dst = jax.random.normal(ks[4], (H, C), dtype=jnp.float32) * 0.05
        bias = jnp.zeros((OUT,), dtype=jnp.float32)
        gamma = jnp.ones((OUT,), dtype=jnp.float32)
        beta = jnp.zeros((OUT,), dtype=jnp.float32)
        return {'x': x, 'edge_index': edge_index, 'W': W, 'a_src': a_src, 'a_dst': a_dst, 'bias': bias, 'gamma': gamma, 'beta': beta}
    _L0_gnn_all = _L0_gnn_setup()
    _L0_gnn_in = {k: v for k, v in _L0_gnn_all.items() if k in ('W', 'a_src', 'a_dst', 'bias', 'gamma', 'beta')}
    del _L0_gnn_all

    def _L1_gnn_setup():
        import jax, jax.numpy as jnp
        import numpy as np
        NUM_EDGE_TYPES = 8
        HIDDEN = 128
        N_NODES = 50000
        N_EDGES = 18750

        def _gru_cell(x, h, W_ih, W_hh, b_ih, b_hh):
            H = h.shape[-1]
            gi = x @ W_ih.T + b_ih
            gh = h @ W_hh.T + b_hh
            i_r, i_z, i_n = (gi[:, :H], gi[:, H:2 * H], gi[:, 2 * H:])
            h_r, h_z, h_n = (gh[:, :H], gh[:, H:2 * H], gh[:, 2 * H:])
            r = jax.nn.sigmoid(i_r + h_r)
            z = jax.nn.sigmoid(i_z + h_z)
            n = jnp.tanh(i_n + r * h_n)
            return (1.0 - z) * n + z * h
        key = jax.random.key(seed)
        ks = jax.random.split(key, 10)
        H = HIDDEN
        h = jax.random.normal(ks[0], (N_NODES, H), dtype=jnp.float32)
        edge_index = jax.random.randint(ks[1], (2, N_EDGES), 0, N_NODES, dtype=jnp.int32)
        edge_type = jax.random.randint(ks[2], (N_EDGES,), 0, NUM_EDGE_TYPES + 1, dtype=jnp.int32)
        s = 1.0 / np.sqrt(H)
        W_msg = jax.random.uniform(ks[3], (H, H), jnp.float32, -s, s)
        b_msg = jax.random.uniform(ks[4], (H,), jnp.float32, -s, s)
        edge_embed = jax.random.normal(ks[5], (NUM_EDGE_TYPES + 1, H), dtype=jnp.float32)
        W_ih = jax.random.uniform(ks[6], (3 * H, H), jnp.float32, -s, s)
        W_hh = jax.random.uniform(ks[7], (3 * H, H), jnp.float32, -s, s)
        b_ih = jax.random.uniform(ks[8], (3 * H,), jnp.float32, -s, s)
        b_hh = jax.random.uniform(ks[9], (3 * H,), jnp.float32, -s, s)
        return {'h': h, 'edge_index': edge_index, 'edge_type': edge_type, 'num_nodes': N_NODES, 'W_msg': W_msg, 'b_msg': b_msg, 'edge_embed': edge_embed, 'W_ih': W_ih, 'W_hh': W_hh, 'b_ih': b_ih, 'b_hh': b_hh}
    _L1_gnn_all = _L1_gnn_setup()
    _L1_gnn_in = {k: v for k, v in _L1_gnn_all.items() if k in ('W_msg', 'b_msg', 'edge_embed', 'W_ih', 'W_hh', 'b_ih', 'b_hh')}
    del _L1_gnn_all

    def _L2_gnn_setup():
        import jax, jax.numpy as jnp
        import numpy as np
        N_NODES = 50000
        N_EDGES = 18750
        D_IN = 128
        D_OUT = 128
        BN_EPS = 1e-05

        def batchnorm(h, gamma, beta):
            mean = jnp.mean(h, axis=0)
            var = jnp.var(h, axis=0)
            return (h - mean) * jax.lax.rsqrt(var + BN_EPS) * gamma + beta
        key = jax.random.key(seed)
        ks = jax.random.split(key, 6)
        x = jax.random.normal(ks[0], (N_NODES, D_IN), dtype=jnp.float32)
        edge_index = jax.random.randint(ks[1], (2, N_EDGES), 0, N_NODES, dtype=jnp.int64)
        s_in = 1.0 / np.sqrt(D_IN)
        s_out = 1.0 / np.sqrt(D_OUT)
        return {'x': x, 'edge_index': edge_index, 'W_mlp': jax.random.normal(ks[2], (D_IN, D_OUT), dtype=jnp.float32) * s_in, 'b_mlp': jax.random.normal(ks[3], (D_OUT,), dtype=jnp.float32) * s_in, 'gamma1': jnp.ones((D_OUT,), dtype=jnp.float32), 'beta1': jnp.zeros((D_OUT,), dtype=jnp.float32), 'W_conv': jax.random.normal(ks[4], (D_OUT, D_OUT), dtype=jnp.float32) * s_out, 'b_conv': jax.random.normal(ks[5], (D_OUT,), dtype=jnp.float32) * s_out, 'gamma2': jnp.ones((D_OUT,), dtype=jnp.float32), 'beta2': jnp.zeros((D_OUT,), dtype=jnp.float32)}
    _L2_gnn_all = _L2_gnn_setup()
    _L2_gnn_in = {k: v for k, v in _L2_gnn_all.items() if k in ('W_mlp', 'b_mlp', 'gamma1', 'beta1', 'W_conv', 'b_conv', 'gamma2', 'beta2')}
    del _L2_gnn_all

    def _L3_gnn_setup():
        import jax, jax.numpy as jnp
        import numpy as np
        N = 3125
        E = 25000
        D_IN, D_H, D_OUT = (128, 128, 128)
        key = jax.random.key(seed)
        ks = jax.random.split(key, 8)
        x = jax.random.normal(ks[0], (N, D_IN), dtype=jnp.float32)
        edge_index = jax.random.randint(ks[1], (2, E), 0, N, dtype=jnp.int64)
        s = 1.0 / np.sqrt(D_IN)
        W1 = jax.random.uniform(ks[2], (D_H, D_IN), minval=-s, maxval=s, dtype=jnp.float32)
        b1 = jax.random.uniform(ks[3], (D_H,), minval=-s, maxval=s, dtype=jnp.float32)
        sh = 1.0 / np.sqrt(D_H)
        W2 = jax.random.uniform(ks[4], (D_H, D_H), minval=-sh, maxval=sh, dtype=jnp.float32)
        b2 = jax.random.uniform(ks[5], (D_H,), minval=-sh, maxval=sh, dtype=jnp.float32)
        W3 = jax.random.uniform(ks[6], (D_OUT, D_H), minval=-sh, maxval=sh, dtype=jnp.float32)
        b3 = jax.random.uniform(ks[7], (D_OUT,), minval=-sh, maxval=sh, dtype=jnp.float32)
        return {'x': x, 'edge_index': edge_index, 'W1': W1, 'b1': b1, 'W2': W2, 'b2': b2, 'W3': W3, 'b3': b3}
    _L3_gnn_all = _L3_gnn_setup()
    _L3_gnn_in = {k: v for k, v in _L3_gnn_all.items() if k in ('W1', 'b1', 'W2', 'b2', 'W3', 'b3')}
    del _L3_gnn_all
    return {'x': x, 'src': src, 'dst': dst, 'edge_type_9': edge_type_9, 'L0_gnn_W': _L0_gnn_in['W'], 'L0_gnn_a_src': _L0_gnn_in['a_src'], 'L0_gnn_a_dst': _L0_gnn_in['a_dst'], 'L0_gnn_bias': _L0_gnn_in['bias'], 'L0_gnn_gamma': _L0_gnn_in['gamma'], 'L0_gnn_beta': _L0_gnn_in['beta'], 'L1_gnn_W_msg': _L1_gnn_in['W_msg'], 'L1_gnn_b_msg': _L1_gnn_in['b_msg'], 'L1_gnn_edge_embed': _L1_gnn_in['edge_embed'], 'L1_gnn_W_ih': _L1_gnn_in['W_ih'], 'L1_gnn_W_hh': _L1_gnn_in['W_hh'], 'L1_gnn_b_ih': _L1_gnn_in['b_ih'], 'L1_gnn_b_hh': _L1_gnn_in['b_hh'], 'L2_gnn_W_mlp': _L2_gnn_in['W_mlp'], 'L2_gnn_b_mlp': _L2_gnn_in['b_mlp'], 'L2_gnn_gamma1': _L2_gnn_in['gamma1'], 'L2_gnn_beta1': _L2_gnn_in['beta1'], 'L2_gnn_W_conv': _L2_gnn_in['W_conv'], 'L2_gnn_b_conv': _L2_gnn_in['b_conv'], 'L2_gnn_gamma2': _L2_gnn_in['gamma2'], 'L2_gnn_beta2': _L2_gnn_in['beta2'], 'L3_gnn_W1': _L3_gnn_in['W1'], 'L3_gnn_b1': _L3_gnn_in['b1'], 'L3_gnn_W2': _L3_gnn_in['W2'], 'L3_gnn_b2': _L3_gnn_in['b2'], 'L3_gnn_W3': _L3_gnn_in['W3'], 'L3_gnn_b3': _L3_gnn_in['b3']}

def reference(x, src, dst, edge_type_9, L0_gnn_W, L0_gnn_a_src, L0_gnn_a_dst, L0_gnn_bias, L0_gnn_gamma, L0_gnn_beta, L1_gnn_W_msg, L1_gnn_b_msg, L1_gnn_edge_embed, L1_gnn_W_ih, L1_gnn_W_hh, L1_gnn_b_ih, L1_gnn_b_hh, L2_gnn_W_mlp, L2_gnn_b_mlp, L2_gnn_gamma1, L2_gnn_beta1, L2_gnn_W_conv, L2_gnn_b_conv, L2_gnn_gamma2, L2_gnn_beta2, L3_gnn_W1, L3_gnn_b1, L3_gnn_W2, L3_gnn_b2, L3_gnn_W3, L3_gnn_b3):
    import jax
    import jax.numpy as jnp

    def _L0_gnn_ref(x, edge_index, W, a_src, a_dst, bias, gamma, beta):
        import jax, jax.numpy as jnp
        import numpy as np
        N = 3125
        E = 50000
        IN = 128
        H = 4
        C = 32
        OUT = H * C
        NEG_SLOPE = 0.2
        LN_EPS = 1e-05
        SM_EPS = 1e-16
        n = x.shape[0]
        loops = jnp.arange(n, dtype=edge_index.dtype)
        src = jnp.concatenate([edge_index[0], loops])
        dst = jnp.concatenate([edge_index[1], loops])
        h = (x @ W).reshape(n, H, C)
        alpha_src = jnp.sum(h * a_src, axis=-1)
        alpha_dst = jnp.sum(h * a_dst, axis=-1)
        e = jax.nn.leaky_relu(alpha_src[src] + alpha_dst[dst], NEG_SLOPE)
        emax = jax.ops.segment_max(e, dst, num_segments=n)
        emax = jnp.where(jnp.isfinite(emax), emax, 0.0)
        ee = jnp.exp(e - emax[dst])
        denom = jax.ops.segment_sum(ee, dst, num_segments=n)
        alpha = ee / (denom[dst] + SM_EPS)
        msg = h[src] * alpha[:, :, None]
        out = jax.ops.segment_sum(msg, dst, num_segments=n).reshape(n, OUT) + bias
        mu = jnp.mean(out, axis=-1, keepdims=True)
        var = jnp.var(out, axis=-1, keepdims=True)
        out = (out - mu) * jax.lax.rsqrt(var + LN_EPS) * gamma + beta
        return jax.nn.relu(out)

    def _L1_gnn_ref(h, edge_index, edge_type, num_nodes, W_msg, b_msg, edge_embed, W_ih, W_hh, b_ih, b_hh):
        import jax, jax.numpy as jnp
        import numpy as np
        NUM_EDGE_TYPES = 8
        HIDDEN = 128
        N_NODES = 50000
        N_EDGES = 18750

        def _gru_cell(x, h, W_ih, W_hh, b_ih, b_hh):
            H = h.shape[-1]
            gi = x @ W_ih.T + b_ih
            gh = h @ W_hh.T + b_hh
            i_r, i_z, i_n = (gi[:, :H], gi[:, H:2 * H], gi[:, 2 * H:])
            h_r, h_z, h_n = (gh[:, :H], gh[:, H:2 * H], gh[:, 2 * H:])
            r = jax.nn.sigmoid(i_r + h_r)
            z = jax.nn.sigmoid(i_z + h_z)
            n = jnp.tanh(i_n + r * h_n)
            return (1.0 - z) * n + z * h
        src = edge_index[0]
        dst = edge_index[1]
        src_h = h[src] @ W_msg.T + b_msg
        emb = edge_embed[jnp.clip(edge_type, 0, NUM_EDGE_TYPES)]
        msg = src_h + emb
        messages = jax.ops.segment_sum(msg, dst, num_segments=num_nodes)
        h_new = _gru_cell(messages, h[:num_nodes], W_ih, W_hh, b_ih, b_hh)
        result = jnp.zeros_like(h).at[:num_nodes].set(h_new)
        return result

    def _L2_gnn_ref(x, edge_index, W_mlp, b_mlp, gamma1, beta1, W_conv, b_conv, gamma2, beta2):
        import jax, jax.numpy as jnp
        import numpy as np
        N_NODES = 50000
        N_EDGES = 18750
        D_IN = 128
        D_OUT = 128
        BN_EPS = 1e-05

        def batchnorm(h, gamma, beta):
            mean = jnp.mean(h, axis=0)
            var = jnp.var(h, axis=0)
            return (h - mean) * jax.lax.rsqrt(var + BN_EPS) * gamma + beta
        N = x.shape[0]
        h = x @ W_mlp + b_mlp
        h = jax.nn.relu(batchnorm(h, gamma1, beta1))
        loops = jnp.arange(N, dtype=edge_index.dtype)
        src = jnp.concatenate([edge_index[0], loops])
        dst = jnp.concatenate([edge_index[1], loops])
        h = h @ W_conv
        ones = jnp.ones(dst.shape[0], dtype=h.dtype)
        deg = jax.ops.segment_sum(ones, dst, num_segments=N)
        dinv = jnp.where(deg > 0, jax.lax.rsqrt(deg), 0.0)
        norm = dinv[src] * dinv[dst]
        msgs = norm[:, None] * h[src]
        out = jax.ops.segment_sum(msgs, dst, num_segments=N) + b_conv
        return jax.nn.relu(batchnorm(out, gamma2, beta2))

    def _L3_gnn_ref(x, edge_index, W1, b1, W2, b2, W3, b3):
        import jax, jax.numpy as jnp
        import numpy as np
        N = 3125
        E = 25000
        D_IN, D_H, D_OUT = (128, 128, 128)
        row, col = (edge_index[0], edge_index[1])
        n = x.shape[0]
        deg = jnp.clip(jax.ops.segment_sum(jnp.ones_like(row, dtype=x.dtype), row, num_segments=n), 1.0)

        def mp(h):
            agg = jax.ops.segment_sum(h[col], row, num_segments=n)
            return jax.nn.relu(agg / deg[:, None])
        h = mp(x @ W1.T + b1)
        h = mp(h @ W2.T + b2)
        return h @ W3.T + b3
    edge_index = jnp.stack([src, dst])
    h = jnp.maximum(_layernorm(x, axis=-1), 0.0)
    x = x + _L0_gnn_ref(h, edge_index, L0_gnn_W, L0_gnn_a_src, L0_gnn_a_dst, L0_gnn_bias, L0_gnn_gamma, L0_gnn_beta)
    h = jnp.maximum(_layernorm(x, axis=-1), 0.0)
    x = x + _L1_gnn_ref(h, edge_index, edge_type_9, 3125, L1_gnn_W_msg, L1_gnn_b_msg, L1_gnn_edge_embed, L1_gnn_W_ih, L1_gnn_W_hh, L1_gnn_b_ih, L1_gnn_b_hh)
    h = jnp.maximum(_layernorm(x, axis=-1), 0.0)
    x = x + _L2_gnn_ref(h, edge_index, L2_gnn_W_mlp, L2_gnn_b_mlp, L2_gnn_gamma1, L2_gnn_beta1, L2_gnn_W_conv, L2_gnn_b_conv, L2_gnn_gamma2, L2_gnn_beta2)
    h = jnp.maximum(_layernorm(x, axis=-1), 0.0)
    x = x + _L3_gnn_ref(h, edge_index, L3_gnn_W1, L3_gnn_b1, L3_gnn_W2, L3_gnn_b2, L3_gnn_W3, L3_gnn_b3)
    return x

_drawn_inputs = setup_inputs


def setup_inputs(seed=0):
    import zlib

    import numpy as np

    out = dict(_drawn_inputs(seed))
    spreads = {'L0_gnn_bias': (0.0, 0.1),
     'L0_gnn_gamma': (1.0, 0.2),
     'L0_gnn_beta': (0.0, 0.1),
     'L2_gnn_gamma1': (1.0, 0.2),
     'L2_gnn_beta1': (0.0, 0.1),
     'L2_gnn_gamma2': (1.0, 0.2),
     'L2_gnn_beta2': (0.0, 0.1)}
    factors = {'L0_gnn_a_dst': 8.0,
     'L1_gnn_b_ih': 8.0,
     'L1_gnn_b_hh': 8.0,
     'L2_gnn_b_mlp': 8.0,
     'L2_gnn_b_conv': 8.0,
     'L3_gnn_W1': 2.766,
     'L3_gnn_b1': 8.0,
     'L3_gnn_b2': 5.177}
    for name, (base, spread) in spreads.items():
        noise = np.random.default_rng([zlib.crc32(name.encode()), seed]).standard_normal(out[name].shape)
        drawn = base * np.exp(spread * noise) if base else spread * noise
        out[name] = jnp.asarray(drawn.astype(out[name].dtype))
    for name, factor in factors.items():
        out[name] = (out[name] * factor).astype(out[name].dtype)
    return out
```

```python
import numpy as np
import concourse.bass as bass
from concourse import mybir
from contextlib import ExitStack

F32 = mybir.dt.float32
BF16 = mybir.dt.bfloat16
I32 = mybir.dt.int32
I16 = mybir.dt.int16
ALU = mybir.AluOpType
ACT = mybir.ActivationFunctionType
AX = mybir.AxisListType

P = 128
N, D, E = 3125, 128, 103125
H, C = 4, 32
NTYPE = 9
ET = 125
NE = E // ET
EP, EJ = 75, 11
Q = 4
R = 784
S = Q * R
GD = P // Q
NG = S // GD
U = 3
PADE = 4
NT = 25
SP_ = NT * P
TAIL = N - (NT - 1) * P
STAIL = S - (NT - 1) * P
CW = 512
NC7 = 7
CHUNKS = [(c * CW, min(CW, S - c * CW)) for c in range(NC7)]
TG = 5
EPS = 1e-5
BIG = 1e30
TINY = 2.0 ** -60
SLOPE = 0.2
BF16_MAX_COUNT = 256.0
NEG_HUGE = -3.0e38


def gnn_program(nc, t, out, dbg):
    ctx = ExitStack()
    with ctx:
        def sb(name, shape, dt):
            return ctx.enter_context(nc.sbuf_tensor(name, shape, dt))

        def sem(name):
            return ctx.enter_context(nc.semaphore(name))

        scratch = "ExternalOutput" if dbg else "Internal"

        def dram(name, shape, dt):
            return nc.dram_tensor(name, shape, dt, kind=scratch).ap()

        count32 = dram("count32", (NG * P, R), F32)
        count16 = dram("count16", (NG * P, R), BF16)
        turned16 = dram("turned16", (S, S), BF16)
        bounds_d = dram("bounds_d", (2, NE), F32)
        win_d = dram("win_d", (NG, 2), I32)
        types_d = dram("types_d", (NTYPE, S), F32)
        hn_d = dram("hn_d", (SP_, D), F32)
        rows32 = count32.rearrange("(d q) r -> d (q r)", q=Q)
        rows16 = count16.rearrange("(d q) r -> d (q r)", q=Q)

        AW = 38400
        arena = sb("arena", [P, AW], F32)

        def ar(a, shape, dt=F32, parts=P, pb=0):
            n = int(np.prod(shape)) * mybir.dt.size(dt)
            assert n % 4 == 0 and a + n // 4 <= AW, (a, shape)
            v = arena[pb:pb + parts, a:a + n // 4]
            if dt != F32:
                v = v.bitcast(dt)
            if len(shape) == 2:
                v = v.rearrange("p (a b) -> p a b", b=shape[1])
            if len(shape) == 3:
                v = v.rearrange("p (a b c) -> p a b c", b=shape[1], c=shape[2])
            return v

        e_int = ar(12800, [3, EJ * ET], I32, EP)
        e_f = ar(16928, [3, EJ * ET], F32, EP)
        e_t = ar(21056, [EJ * ET], F32, EP)
        e_key = ar(22432, [EJ * ET], F32, EP)
        key = ar(23808, [NE + PADE], F32, ET)
        rem = ar(24640, [NE + PADE], F32, ET)
        typ = ar(25472, [NE + PADE], F32, ET)
        Y = ar(26304, [NE + PADE + 1, NTYPE + 1], BF16, ET)
        A = [ar(30460 + 64 * i, [P], BF16, ET) for i in range(U)]
        B = [ar(30656 + 392 * i, [R], BF16, ET) for i in range(U)]
        stage32 = [ar(31840 + 784 * i, [R]) for i in range(2)]
        stage16 = [ar(33408 + 392 * i, [R], BF16) for i in range(2)]
        ovf_junk = [ar(34592 + 392 * i, [R], BF16) for i in range(2)]
        tb = ar(0, [2, NE + 1], F32, NG)
        cov = ar(1700, [NE + 1], F32, NG)
        iota_t = ar(2600, [NE + 1], F32, NG)
        iota_i = ar(3500, [NE + 1], I32, NG)
        iota128 = ar(4400, [P], I16, ET)
        iota_g = ar(4500, [P], I16, ET)
        iotaR = ar(4600, [R], I16, ET)
        T32 = ar(32000, [NTYPE, NG], F32, GD)
        T98 = ar(33000, [NTYPE, GD], F32, NG)
        WAb = ar(19200, [H, P])
        as_bc = ar(0, [H, SP_])
        Cb = [ar(12800 + 3200 * i, [SP_]) for i in range(2)]
        L = ar(19200, [SP_])
        nm = [ar(22400 + 1600 * i, [SP_], BF16) for i in range(2)]
        u = [ar(25600 + 3200 * i, [SP_]) for i in range(2)]
        acc = ar(32000, [SP_])
        junk = ar(35200, [SP_], BF16)
        A3 = ar(36800, [SP_], BF16)
        hT0 = ar(12800, [SP_])
        Z3 = ar(16000, [SP_])
        Z3b = ar(25600, [SP_], BF16)
        Z3c = ar(27200, [SP_])
        stg16 = [ar(1600 * i, [SP_], BF16) for i in range(2)]
        stageT = [ar(3200 + 3200 * i, [NT, 2 * P], BF16) for i in range(2)]
        ring = [ar(9600 + 1568 * i, [S], BF16) for i in range(4)]
        G = ar(15872, [NT, 3, D], BF16)
        FA, FB, FC = ar(20672, [SP_]), ar(23872, [SP_]), ar(27072, [SP_])
        rest = FC.rearrange("p (t d) -> p t d", d=D)
        att_o = rest
        gr, gz, gn = (ar(30272 + CW * i, [CW]) for i in range(3))
        DB = ar(0, [SP_])
        TT = ar(35200, [SP_], F32, NTYPE)

        nb = sb("nb", [P, NT, H * (C + 1)], F32)
        hn = nb[:, :, 0:D]
        haug = sb("haug", [P, NT, H, C + 1], F32)
        x = haug[:, :, :, :].rearrange("p t h c -> p (t h c)")[:, 0:NT * D].rearrange("p (t d) -> p t d", d=D)
        PT = [sb(f"PT{i}", [P, TG * P], F32) for i in range(2)]
        aggS = [sb(f"aggS{i}", [C + 1, H * P], F32) for i in range(2)]
        ident = sb("ident", [P, P], F32)
        identb = sb("identb", [P, P], BF16)
        ones = sb("ones", [P, P], F32)
        onesb = sb("onesb", [P, P], BF16)
        qsum = sb("qsum", [P, GD], F32)
        Wraw = ar(12800, [10, D])
        WT = sb("WT", [P, 12, D], F32)
        WW = sb("WW", [P, D + 2 * H], F32)
        wa_t = sb("wa_t", [P, D], F32)
        vec = sb("vec", [P, 8, D], F32)
        col = sb("col", [P, 24], F32)
        embx = sb("embx", [NTYPE, D], F32)
        bmsg9 = sb("bmsg9", [NTYPE, D], F32)
        Traw = sb("Traw", [P, NG, NTYPE], F32)
        asd = sb("asd", [P, NT, 2 * H], F32)
        ad8 = sb("ad8", [P, NT * H], F32)
        mx = sb("mx", [P, 2, 3, H], F32)
        wins = sb("wins", [1, NG * 2], I32)
        win = sb("win", [NG, 2], F32)
        win_i = sb("win_i", [NG, 2], I32)
        tlo = sb("tlo", [EP, 2, EJ], F32)
        grp_i = sb("grp_i", [NG, 1], I32)
        tiny = sb("tiny", [P, 1], F32)
        neg1 = sb("neg1", [P, 4], F32)
        grp = sb("grp", [NG, 2], F32)
        it9 = sb("it9", [ET, NTYPE], F32)
        it9i = sb("it9i", [ET, NTYPE], I32)
        ovf = sb("ovf", [P, NG], F32)
        flag_f = sb("flag_f", [P, 2], F32)
        flag_i = sb("flag_i", [1, 2], I32)
        bn6 = sb("bn6", [P, NT, 6], F32)
        mv = sb("mv", [P, NT, 2], F32)
        rstd = sb("rstd", [P, NT], F32)
        rden = sb("rden", [P, NT, H], F32)
        dinv = sb("dinv", [P, NT], F32)
        rdeg = sb("rdeg", [P, NT], F32)
        mhalf = sb("mhalf", [P, NT], F32)
        masks = sb("masks", [P, H], F32)

        ps = ctx.enter_context(nc.psum_tensor("ps", [P, 8, CW], F32))
        psf = ps[:, :, :].rearrange("p a b -> p (a b)")


        v, a, gp, pt, sy = nc.vector, nc.scalar, nc.gpsimd, nc.tensor, nc.sync
        s_chain = {e: sem("chain_" + e) for e in ("dve", "act", "pool")}
        chain = {e: 0 for e in s_chain}

        def link(eng, which, ins):
            chain[which] += 1
            ins.then_inc(s_chain[which], 1)
            eng.wait_ge(s_chain[which], chain[which])

        NPASS = NG // 2

        def halves(x):
            return x.rearrange("p (h n) -> p h n", h=2)

        def phase_counts():
            edges_in, consts, split_ready, cols_out, cols_in = sem("edges_in"), sem("consts"), sem("split_ready"), sem("cols_out"), sem("cols_in")
            bounds_ready, bounds_st, bounds_in = sem("bounds_ready"), sem("bounds_st"), sem("bounds_in")
            win_ready, win_st, win_in = sem("win_ready"), sem("win_st"), sem("win_in")
            hot = [sem(f"hot{i}") for i in range(U)]
            hot_used = [sem(f"hot_used{i}") for i in range(U)]
            group_done = [sem(f"group_done{i}") for i in range(2)]
            staged = [sem(f"staged{i}") for i in range(2)]
            stored = [sem(f"stored{i}") for i in range(2)]
            with nc.Block() as block:
                @block.sync
                def _(sp):
                    for k, n in enumerate(("src", "dst", "edge_type_9")):
                        sp.dma_start(e_int[:, k, :], t[n].rearrange("(p e) -> p e", p=EP)).then_inc(edges_in, 16)
                    sp.wait_ge(bounds_ready, 1)
                    sp.dma_start(bounds_d.rearrange("k (p j) -> p k j", p=EP), tlo[:, :, :]).then_inc(bounds_st, 16)
                    sp.wait_ge(bounds_st, 16)
                    sp.dma_start(tb[:, :, 0:NE], bounds_d.partition_broadcast(NG)).then_inc(bounds_in, 16)
                    sp.wait_ge(win_ready, 1)
                    sp.dma_start(win_d, win_i[:, :]).then_inc(win_st, 16)
                    sp.wait_ge(win_st, 16)
                    sp.dma_start(wins[0:1, :], win_d.rearrange("(o g) k -> o (g k)", o=1)).then_inc(win_in, 16)
                    with sp.Fori(0, NPASS) as m:
                        for b in range(2):
                            rows = bass.ds((m * 2 + b) * P, P)
                            sp.wait_ge(staged[b], m + 2)
                            for dst, st in ((count32, stage32), (count16, stage16)):
                                sp.dma_start(dst[rows, :], st[b]).then_inc(stored[b], 16)
                    for b in range(2):
                        sp.wait_ge(stored[b], 32 * (NPASS + 1))

                @block.gpsimd
                def _(pool):
                    link(pool, "pool", gp.memset(ones[:, :], 1.0))
                    gp.affine_select(out=ident[:, :], in_=ones[:, :], compare_op=ALU.is_equal, fill=0.0, base=0,
                                     pattern=[[-1, P]], channel_multiplier=1)
                    gp.memset(onesb[:, :], 1.0)
                    gp.iota(iota_i[:, 0:NE], [[1, NE]], base=0, channel_multiplier=0)
                    gp.iota(grp_i[:, :], [[1, 1]], base=0, channel_multiplier=GD)
                    gp.iota(it9i[:, :], [[1, NTYPE]], base=0, channel_multiplier=0)
                    gp.iota(iota_g, [[1, P]], base=-P, channel_multiplier=0)
                    gp.iota(iotaR, [[1, R]], base=0, channel_multiplier=0).then_inc(consts, 1)

                @block.tensor
                def _(pe):
                    for i in range(U):
                        pe.sem_inc(hot_used[i], 1)
                    pe.wait_ge(consts, 1)
                    pe.wait_ge(split_ready, 1)
                    k = 0
                    for src in (e_key, e_f[:, 0, :], e_f[:, 2, :]):
                        for j0, j1 in ((0, 6), (6, EJ)):
                            for j in range(j0, j1):
                                last = pt.transpose(ps[0:ET, k, (j - j0) * EP:(j - j0 + 1) * EP],
                                                    src[:, j * ET:(j + 1) * ET], ident[0:EP, 0:EP])
                            last.then_inc(cols_out, 1)
                            k += 1
                    pe.wait_ge(cols_in, k)
                    pe.wait_ge(win_in, 16)
                    turn_reg = pe.alloc_register("pe_turn")
                    pe.reg_mov(turn_reg, 1)

                    def turn(t0, b, first, last, m=None):
                        n = pe.snap(turn_reg)
                        if first:
                            pe.wait_ge(staged[b], m + 1)
                        for i in range(U):
                            pe.wait_ge(hot[i], n)
                            start, stop = first and i == 0, last and i == U - 1
                            for h in range(2):
                                pt.matmul(ps[:, 3 * b + h, 0:R // 2], A[i], B[i][:, h * (R // 2):(h + 1) * (R // 2)],
                                          start=start, stop=stop)
                            pt.matmul(ps[:, 3 * b + 2, 0:NTYPE], A[i], Y[:, bass.ds(t0 + i, 1), 0:NTYPE],
                                      start=start, stop=stop).then_inc(hot_used[i], 1)
                        pe.reg_add(turn_reg, turn_reg, 1)

                    with pe.Fori(0, NPASS) as m:
                        for b in range(2):
                            lo = pe.value_load(wins[0:1, bass.ds((m * 2 + b) * 2, 1)], min_val=0, max_val=NE - 3 * U + 1)
                            hi = pe.value_load(wins[0:1, bass.ds((m * 2 + b) * 2 + 1, 1)], min_val=3 * U, max_val=NE + U - 1)
                            turn(lo, b, True, False, m)
                            with pe.Fori(lo + U, hi - U, U) as tt:
                                turn(tt, b, False, False)
                            turn(hi - U, b, False, True)
                            pt.matmul(ps[0:1, 7, 0:1], onesb[:, 0:1], onesb[:, 0:1], start=True, stop=True).then_inc(group_done[b], 1)

                @block.scalar
                def _(act):
                    for b in range(2):
                        act.sem_inc(staged[b], 1)
                        act.sem_inc(stored[b], 32)
                    with act.Fori(0, NPASS) as m:
                        for b in range(2):
                            act.wait_ge(group_done[b], m + 1)
                            act.wait_ge(stored[b], m * 32 + 32)
                            counts = ps[:, 3 * b:3 * b + 2, 0:R // 2]
                            a.activation(halves(stage32[b]), counts, ACT.Copy)
                            a.activation(halves(stage16[b]), counts, ACT.Copy)
                            a.activation(halves(ovf_junk[b]), counts, ACT.Relu, bias=neg1[:, 0:1],
                                         accum_out=ovf[:, bass.ds(m * 2 + b, 1)])
                            a.activation(Traw[:, bass.ds(m * 2 + b, 1), :].rearrange("p o k -> p (o k)"), ps[:, 3 * b + 2, 0:NTYPE],
                                         ACT.Copy).then_inc(staged[b], 1)

                @block.vector
                def _(dve):
                    dve.wait_ge(edges_in, 48)
                    link(dve, "dve", v.tensor_copy(e_f, e_int))
                    v.tensor_reduce(tlo[:, 0, :], e_f[:, 1, :].rearrange("p (j e) -> p j e", j=EJ), AX.X, ALU.min)
                    v.tensor_reduce(tlo[:, 1, :], e_f[:, 1, :].rearrange("p (j e) -> p j e", j=EJ), AX.X, ALU.max).then_inc(bounds_ready, 1)
                    link(dve, "dve", v.tensor_scalar(e_t, e_f[:, 0, :], float(R), None, ALU.is_ge))
                    for k in (2, 3):
                        link(dve, "dve", v.tensor_scalar(e_key, e_f[:, 0, :], float(k * R), None, ALU.is_ge))
                        link(dve, "dve", v.tensor_tensor(e_t, e_t, e_key, ALU.add))
                    link(dve, "dve", v.scalar_tensor_tensor(e_f[:, 0, :], e_t, -float(R), e_f[:, 0, :], ALU.mult, ALU.add))
                    link(dve, "dve", v.scalar_tensor_tensor(e_key, e_f[:, 1, :], float(Q), e_t, ALU.mult, ALU.add))
                    v.tensor_scalar(e_f[:, 2, :], e_f[:, 2, :], 0.0, float(NTYPE - 1), ALU.max, ALU.min).then_inc(split_ready, 1)
                    v.memset(neg1[:, 0:1], -BF16_MAX_COUNT)
                    v.memset(tiny[:, :], TINY)
                    v.memset(key[:, NE:], -1.0)
                    v.memset(rem[:, NE:], 0.0)
                    v.memset(typ[:, NE:], 0.0)
                    k = 0
                    for dst in (key, rem, typ):
                        dv = dst[:, 0:NE].rearrange("e (p j) -> e j p", p=EP)
                        for j0, j1 in ((0, 6), (6, EJ)):
                            dve.wait_ge(cols_out, k + 1)
                            v.tensor_copy(dv[:, j0:j1, :], ps[0:ET, k, 0:(j1 - j0) * EP].rearrange("e (j p) -> e j p", p=EP)).then_inc(cols_in, 1)
                            k += 1
                    dve.wait_ge(cols_in, k)
                    dve.wait_ge(consts, 1)
                    v.tensor_copy(identb[:, :], ident[:, :])
                    v.tensor_copy(iota_t[:, 0:NE], iota_i[:, 0:NE])
                    v.tensor_copy(grp[:, 0:1], grp_i[:, :])
                    link(dve, "dve", v.tensor_copy(it9[:, :], it9i[:, :]))
                    link(dve, "dve", v.tensor_scalar(grp[:, 1:2], grp[:, 0:1], float(GD - 1), None, ALU.add))
                    link(dve, "dve", v.tensor_tensor(Y[:, 0:NE + PADE, 0:NTYPE], typ.unsqueeze(2).to_broadcast([ET, NE + PADE, NTYPE]),
                                                     it9[:, :].unsqueeze(1).to_broadcast([ET, NE + PADE, NTYPE]), ALU.is_equal))
                    it = iota_t[:, 0:NE]
                    cv = cov[:, 0:NE]
                    t0, t1 = tb[:, 0, 0:NE], tb[:, 1, 0:NE]
                    dve.wait_ge(bounds_in, 16)
                    link(dve, "dve", v.tensor_scalar(cv, t0, grp[:, 1:2], None, ALU.is_le))
                    link(dve, "dve", v.scalar_tensor_tensor(cv, t1, grp[:, 0:1], cv, ALU.is_ge, ALU.mult))
                    link(dve, "dve", v.scalar_tensor_tensor(t0, it, 1.0, cv, ALU.add, ALU.mult))
                    link(dve, "dve", v.tensor_scalar(it, it, -1.0, float(NE), ALU.mult, ALU.add))
                    link(dve, "dve", v.tensor_tensor(t1, it, cv, ALU.mult))
                    link(dve, "dve", v.tensor_reduce(win[:, 0:1], t1, AX.X, ALU.max))
                    link(dve, "dve", v.tensor_reduce(win[:, 1:2], t0, AX.X, ALU.max))
                    link(dve, "dve", v.tensor_scalar(win[:, 0:1], win[:, 0:1], -1.0, float(NE), ALU.mult, ALU.add))
                    link(dve, "dve", v.tensor_scalar(win[:, 0:1], win[:, 0:1], float(NE - 3 * U + 1), None, ALU.min))
                    link(dve, "dve", v.tensor_tensor(win[:, 1:2], win[:, 1:2], win[:, 0:1], ALU.subtract))
                    link(dve, "dve", v.tensor_scalar(win[:, 1:2], win[:, 1:2], float(3 * U), 1.0, ALU.max, ALU.add))
                    link(dve, "dve", v.tensor_scalar(win[:, 1:2], win[:, 1:2], 1.0 / U, None, ALU.mult))
                    link(dve, "dve", v.tensor_scalar(win[:, 1:2], win[:, 1:2], 2.0 ** 23, None, ALU.add))
                    link(dve, "dve", v.tensor_scalar(win[:, 1:2], win[:, 1:2], -2.0 ** 23, float(U), ALU.add, ALU.mult))
                    link(dve, "dve", v.tensor_tensor(win[:, 1:2], win[:, 1:2], win[:, 0:1], ALU.add))
                    v.tensor_copy(win_i[:, :], win[:, :]).then_inc(win_ready, 1)
                    dve.wait_ge(win_in, 16)
                    turn_reg = dve.alloc_register("dve_turn")
                    dve.reg_mov(turn_reg, 1)
                    with dve.Fori(0, NG) as g:
                        lo = dve.value_load(wins[0:1, bass.ds(g * 2, 1)], min_val=0, max_val=NE - 3 * U + 1)
                        hi = dve.value_load(wins[0:1, bass.ds(g * 2 + 1, 1)], min_val=3 * U, max_val=NE + U - 1)
                        v.tensor_scalar(iota_g, iota_g, float(P), None, ALU.add).then_inc(s_iota, 1)
                        dve.wait_ge(s_iota, g + 1)
                        v.memset(neg1[:, 1:2], 0.0)
                        with dve.Fori(lo, hi, U) as tt:
                            n = dve.snap(turn_reg)
                            for i in range(U):
                                dve.wait_ge(hot_used[i], n)
                                v.tensor_scalar(A[i], iota_g, key[:, bass.ds(tt + i, 1)], None, ALU.is_equal)
                                v.tensor_scalar(B[i], iotaR, rem[:, bass.ds(tt + i, 1)], None,
                                                ALU.is_equal).then_inc(hot[i], 1)
                            dve.reg_add(turn_reg, turn_reg, 1)

        def layer_stats(dve, y, root_in, root_out, n):
            for k in range(NT):
                v.bn_stats(bn6[:, k, :], y[:, k, :])
            link(dve, "dve", v.memset(neg1[:, 2:3], 0.0))
            for k in range(NT):
                last = v.bn_aggr(mv[:, k, :], bn6[:, k, :])
            link(dve, "dve", last)
            v.tensor_scalar(rstd[:, :], mv[:, :, 1], EPS, None, ALU.add).then_inc(root_in, 1)
            dve.wait_ge(root_out, n)

        def over_features(ap):
            return ap.unsqueeze(2).to_broadcast([P, NT, D])

        def norm_relu(dve):
            link(dve, "dve", v.tensor_tensor(hn, x, over_features(mv[:, :, 0]), ALU.subtract))
            link(dve, "dve", v.scalar_tensor_tensor(hn, hn, 0.0, over_features(rstd[:, :]), ALU.max, ALU.mult))

        def load_x(sp, zeroed, x_in):
            sp.dma_start(x[:, 0:NT - 1, :], t["x"][0:(NT - 1) * P, :].rearrange("(t p) d -> p t d", p=P)).then_inc(x_in, 16)
            sp.wait_ge(zeroed, 1)
            sp.dma_start(x[0:TAIL, NT - 1, :], t["x"][(NT - 1) * P:N, :]).then_inc(x_in, 16)

        def taken(eng, outs, i):
            if i >= 0:
                eng.wait_ge(outs[i % 2], i // 2 + 1)

        def take_all(eng, which, made, outs, jobs, first=0):
            for i, pieces in enumerate(jobs):
                if (first + i) % 2 == which:
                    eng.wait_ge(made, first + i + 1)
                    for dst, src in pieces:
                        last = a.activation(dst, src, ACT.Copy) if which == 0 else v.tensor_copy(dst, src)
                    last.then_inc(outs[which], 1)

        def phase_nodes():
            zeroed, x_in, w_in, made, var_ready, std_done, hn_ready = (sem(n) for n in ("n_zeroed", "n_x_in", "n_w_in", "n_made", "n_var", "n_std", "n_hn"))
            outs = [sem("n_out_act"), sem("n_out_dve")]
            ww_ready, wa_ready, tq_ready, t98_st = sem("n_ww"), sem("n_wa"), sem("n_tq"), sem("n_t98")
            wsrc = [("L1_gnn_W_msg", 1), ("L1_gnn_W_ih", 3), ("L1_gnn_W_hh", 3), ("L3_gnn_W1", 1), ("L3_gnn_W2", 1), ("L3_gnn_W3", 1)]
            cols = [("L1_gnn_b_ih", 0, 3), ("L1_gnn_b_hh", 3, 3), ("L2_gnn_b_mlp", 6, 1), ("L2_gnn_gamma1", 7, 1), ("L2_gnn_beta1", 8, 1),
                    ("L2_gnn_b_conv", 9, 1), ("L2_gnn_gamma2", 10, 1), ("L2_gnn_beta2", 11, 1)]
            n_w = 0

            jobs = []
            for b0, b1 in ((0, 4), (4, 8), (8, 10)):
                i = len(jobs)
                jobs.append([(WT[:, b0:b1, :], ps[:, i % 8, 0:(b1 - b0) * P].rearrange("p (w n) -> p w n", n=P))])
            for c in range(NC7):
                w = min(CW, SP_ - c * CW)
                jobs.append([(hT0[:, c * CW:c * CW + w], ps[:, len(jobs) % 8, 0:w])])
            trios = [(k, min(k + 3, NT)) for k in range(0, NT, 3)]
            for k0, k1 in trios:
                src = ps[:, len(jobs) % 8, 0:(k1 - k0) * (D + 2 * H)].rearrange("p (t n) -> p t n", n=D + 2 * H)
                jobs.append([(haug[:, k, :, 0:C], src[:, k - k0, 0:D].rearrange("p (h c) -> p h c", h=H)) for k in range(k0, k1)]
                            + [(asd[:, k0:k1, :], src[:, :, D:D + 2 * H])])
            for h in range(H):
                for c in range(NC7):
                    w = min(CW, SP_ - c * CW)
                    jobs.append([(as_bc[:, h, c * CW:c * CW + w], ps[:, len(jobs) % 8, 0:w])])
            for k in range(2):
                jobs.append([(T32[:, :, 49 * k:49 * k + 49].rearrange("p k g -> p g k"),
                              ps[0:GD, len(jobs) % 8, 0:49 * NTYPE].rearrange("p (g k) -> p g k", k=NTYPE))])
            jobs.append([(T98, ps[0:NG, len(jobs) % 8, 0:NTYPE * GD].rearrange("p (k d) -> p k d", k=NTYPE))])

            with nc.Block() as block:
                @block.sync
                def _(sp):
                    nonlocal n_w
                    k = 0
                    for name, n in wsrc:
                        sp.dma_start(Wraw[:, k:k + n, :], t[name].rearrange("(w p) d -> p w d", p=P)).then_inc(w_in, 16)
                        k += n
                    load_x(sp, zeroed, x_in)
                    sp.dma_start(WT[:, 10, :], t["L2_gnn_W_mlp"]).then_inc(w_in, 16)
                    sp.dma_start(WT[:, 11, :], t["L2_gnn_W_conv"]).then_inc(w_in, 16)
                    sp.dma_start(WW[:, 0:D], t["L0_gnn_W"]).then_inc(w_in, 16)
                    n_w = len(wsrc) + 3
                    for k, name in enumerate(("L0_gnn_a_src", "L0_gnn_a_dst")):
                        sp.dma_start(vec[:, 6 + k, :], t[name].rearrange("h c -> (h c)").partition_broadcast(P)).then_inc(w_in, 16)
                    for k, name in enumerate(("L0_gnn_bias", "L0_gnn_gamma", "L0_gnn_beta", "L3_gnn_b1", "L3_gnn_b2", "L3_gnn_b3")):
                        sp.dma_start(vec[:, k, :], t[name].partition_broadcast(P)).then_inc(w_in, 16)
                    for name, c0, n in cols:
                        sp.dma_start(col[:, c0:c0 + n], t[name].rearrange("(k p) -> p k", p=P), allow_slow_non_contiguous=True).then_inc(w_in, 16)
                    sp.dma_start(embx[:, :], t["L1_gnn_edge_embed"]).then_inc(w_in, 16)
                    sp.dma_start(bmsg9[:, :], t["L1_gnn_b_msg"].partition_broadcast(NTYPE)).then_inc(w_in, 16)
                    n_w += 8 + len(cols) + 2
                    taken(sp, outs, 49)
                    sp.dma_start(types_d.rearrange("k (g d) -> g k d", d=GD), T98).then_inc(t98_st, 16)
                    sp.wait_ge(t98_st, 16)

                @block.gpsimd
                def _(pool):
                    gp.memset(x[:, NT - 1, :], 0.0).then_inc(zeroed, 1)
                    link(pool, "pool", gp.memset(mhalf[:, :], -0.5))
                    pool.wait_ge(var_ready, 1)
                    gp.tensor_tensor(rstd[:, :], rstd[:, :], mhalf[:, :], ALU.pow).then_inc(std_done, 1)

                @block.vector
                def _(dve):
                    v.tensor_reduce(qsum[:, :], ident[:, :].rearrange("p (d q) -> p d q", q=Q), AX.X, ALU.add).then_inc(tq_ready, 1)
                    v.tensor_reduce(masks[:, 0:3], ident[:, :].rearrange("p (a k) -> p k a", k=32)[:, 0:3, :], AX.X, ALU.add)
                    dve.wait_ge(w_in, 16 * n_w)
                    v.tensor_tensor(embx[:, :], embx[:, :], bmsg9[:, :], ALU.add)
                    for k in range(2):
                        link(dve, "dve", v.tensor_tensor(wa_t[:, :], WW[:, 0:D], vec[:, 6 + k, :], ALU.mult))
                        last = v.tensor_reduce(WW[:, D + H * k:D + H * k + H], wa_t[:, :].rearrange("p (h c) -> p h c", h=H), AX.X, ALU.add)
                        link(dve, "dve", last)
                    v.tensor_copy(WAb, WW[:, D:D + H].unsqueeze(2).to_broadcast([P, H, P])).then_inc(ww_ready, 1)
                    dve.wait_ge(x_in, 32)
                    layer_stats(dve, x, var_ready, std_done, 1)
                    norm_relu(dve)
                    dve.sem_inc(hn_ready, 1)
                    take_all(dve, 1, made, outs, jobs[0:10])
                    v.memset(haug[:, :, :, C:C + 1], 1.0)
                    take_all(dve, 1, made, outs, jobs[10:], 10)
                    for k in range(len(jobs)):
                        taken(dve, outs, k)
                    v.tensor_scalar(ad8[:, :].rearrange("p (t h) -> p t h", h=H), asd[:, :, H:2 * H], 1.0 - SLOPE, None, ALU.mult)
                    for h in range(H):
                        last = v.tensor_scalar(Z3[32 * h:32 * h + 32, :], as_bc[32 * h:32 * h + 32, h, :], SLOPE, None, ALU.mult)
                    link(dve, "dve", last)
                    link(dve, "dve", v.tensor_copy(Z3b, Z3))
                    link(dve, "dve", v.tensor_tensor(Z3c, Z3, Z3b, ALU.subtract))
                    link(dve, "dve", v.tensor_scalar(A3, Z3b, masks[:, 0:1], None, ALU.mult))
                    link(dve, "dve", v.tensor_copy(Z3b, Z3c))
                    link(dve, "dve", v.scalar_tensor_tensor(A3, Z3b, masks[:, 1:2], A3, ALU.mult, ALU.add))
                    link(dve, "dve", v.tensor_tensor(Z3c, Z3c, Z3b, ALU.subtract))
                    link(dve, "dve", v.scalar_tensor_tensor(A3, Z3c, masks[:, 2:3], A3, ALU.mult, ALU.add))

                @block.scalar
                def _(act):
                    take_all(act, 0, made, outs, jobs[0:10])
                    act.wait_ge(x_in, 32)
                    act.wait_ge(hn_ready, 1)
                    take_all(act, 0, made, outs, jobs[10:], 10)

                @block.tensor
                def _(pe):
                    made_n = [0]

                    def bank():
                        i = made_n[0]
                        taken(pe, outs, i - 8)
                        return ps[:, i % 8, :]

                    def done(ins):
                        made_n[0] += 1
                        ins.then_inc(made, 1)

                    pe.wait_ge(w_in, 16 * n_w)
                    for b0, b1 in ((0, 4), (4, 8), (8, 10)):
                        o = bank()
                        for k in range(b0, b1):
                            last = pt.transpose(o[:, (k - b0) * P:(k - b0 + 1) * P], Wraw[:, k, :], ident[:, :])
                        done(last)
                    for i in range(3):
                        taken(pe, outs, i)
                    pe.wait_ge(hn_ready, 1)
                    for c in range(NC7):
                        o = bank()
                        for k in range(4 * c, min(4 * c + 4, NT)):
                            last = pt.transpose(o[:, (k - 4 * c) * P:(k - 4 * c + 1) * P], hn[:, k, :], ident[:, :])
                        done(last)
                    pe.wait_ge(ww_ready, 1)
                    for k in range(3, 10):
                        taken(pe, outs, k)
                    for k0, k1 in trios:
                        o = bank()
                        for k in range(k0, k1):
                            last = pt.matmul(o[:, (k - k0) * (D + 2 * H):(k - k0 + 1) * (D + 2 * H)], hT0[:, k * P:(k + 1) * P], WW[:, :],
                                             start=True, stop=True)
                        done(last)
                    for h in range(H):
                        for c in range(NC7):
                            w = min(CW, SP_ - c * CW)
                            done(pt.matmul(bank()[:, 0:w], WAb[:, h, :], hT0[:, c * CW:c * CW + w], start=True, stop=True))
                    pe.wait_ge(tq_ready, 1)
                    for k in range(2):
                        done(pt.matmul(bank()[0:GD, 0:49 * NTYPE], qsum[:, :], Traw[:, 49 * k:49 * k + 49, :].rearrange("p g k -> p (g k)"),
                                       start=True, stop=True))
                    taken(pe, outs, 47)
                    taken(pe, outs, 48)
                    o = bank()
                    for k in range(NTYPE):
                        last = pt.transpose(o[0:NG, k * GD:(k + 1) * GD], T32[:, k, :], ident[0:GD, 0:GD])
                    done(last)

        def phase_attention():
            names = ("block_in0", "block_in1", "mask_ready", "ln_ready", "logs_ready", "max_done", "relu_done", "sum_done", "turned", "scores_done",
                     "exp_done", "used", "sums_out", "back", "sums_in", "cleared", "ident_in")
            (in0, in1, mask_ready, ln_ready, logs_ready, max_done, relu_done, sum_done, turned, scores_done,
             exp_done, used, sums_out, back, sums_in, cleared, ident_in) = (sem("a_" + n) for n in names)
            block_in = [in0, in1]
            psT = [psf[:, 2 * CW * i:2 * CW * i + TG * P] for i in range(2)]

            def blocks(eng, body):
                body(0, 0, 0)
                with eng.Fori(0, NT // 2) as m:
                    body(m * 2 + 1, 1, m)
                    body(m * 2 + 2, 0, m + 1)

            with nc.Block() as block:
                @block.sync
                def _(sp):
                    sp.wait_ge(cleared, 1)
                    sp.dma_start(Cb[0][:, 0:S], rows32[0:P, :]).then_inc(block_in[0], 16)
                    sp.dma_start(Cb[1][:, 0:S], rows32[P:2 * P, :]).then_inc(block_in[1], 16)
                    with sp.Fori(0, NT // 2 - 1) as m:
                        for i in range(2):
                            b = m * 2 + 2 + i
                            sp.wait_ge(logs_ready, m * 2 + 1 + i)
                            sp.dma_start(Cb[i][:, 0:S], rows32[bass.ds(b * P, P), :]).then_inc(block_in[i], 16)
                    sp.wait_ge(cleared, 2)
                    sp.dma_start(Cb[0][0:STAIL, 0:S], rows32[(NT - 1) * P:S, :]).then_inc(block_in[0], 16)

                @block.gpsimd
                def _(pool):
                    pool.sem_inc(max_done, 2)
                    pool.sem_inc(sum_done, 1)
                    gp.memset(acc, 0.0)
                    gp.memset(nm[0][:, S:SP_], BIG)
                    gp.memset(nm[1][:, S:SP_], BIG)
                    gp.memset(L[:, S:SP_], -BIG).then_inc(cleared, 1)

                    def body(b, i, turn, last=False):
                        if last:
                            pool.wait_ge(logs_ready, NT - 1)
                            gp.memset(Cb[0][STAIL:P, 0:S], 0.0).then_inc(cleared, 1)
                        pool.wait_ge(block_in[i], turn * 16 + 16)
                        gp.tensor_tensor(acc[:, 0:S], acc[:, 0:S], Cb[i][:, 0:S], ALU.add).then_inc(acc_done, 1)
                        width = STAIL if last else P
                        diag = Cb[i][:, bass.ds(b * P, width)]
                        pool.wait_ge(acc_done, b + 1)
                        gp.tensor_tensor(diag, diag, ident[:, 0:width], ALU.add).then_inc(ident_in, 1)
                        pool.wait_ge(ln_ready, b + 1)
                        pool.wait_ge(sum_done, b * 4 + 1)
                        gp.tensor_tensor(L[:, 0:S], Cb[i][:, 0:S], nm[i][:, 0:S], ALU.subtract).then_inc(logs_ready, 1)

                    body(0, 0, 0)
                    with pool.Fori(0, NT // 2 - 1) as m:
                        body(m * 2 + 1, 1, m)
                        body(m * 2 + 2, 0, m + 1)
                    body(NT - 2, 1, NT // 2 - 1)
                    body(NT - 1, 0, NT // 2, last=True)

                @block.vector
                def _(dve):
                    dve.wait_ge(cleared, 1)

                    def mask(b, i, turn):
                        dve.wait_ge(ident_in, b + 1)
                        v.tensor_scalar(nm[i][:, 0:S], Cb[i][:, 0:S], 0.0, BIG, ALU.is_equal, ALU.mult).then_inc(mask_ready, 1)

                    def source_max(b, i, h):
                        if h == 0:
                            dve.wait_ge(mask_ready, b + 1)
                            v.memset(neg1[:, 2:3], 0.0)
                        dve.wait_ge(max_done, b * 4 + h + 2)
                        v.memset(neg1[:, 3:4], 0.0)
                        ins = v.tensor_tensor_reduce(out=junk[:, 0:SP_], in0=as_bc[:, h, :], in1=nm[i], scale=1.0, scalar=NEG_HUGE,
                                                     op0=ALU.subtract, op1=ALU.max, accum_out=mx[:, i, 0, h:h + 1])
                        ins.then_inc(max_done, 1)

                    def shifts(b, i):
                        dve.wait_ge(max_done, b * 4 + 6)
                        adv = asd[:, bass.ds(b, 1), H:2 * H].rearrange("p o h -> p (o h)")
                        v.tensor_tensor(mx[:, i, 1, :], mx[:, i, 0, :], adv, ALU.add).then_inc(shift_step, 1)
                        dve.wait_ge(shift_step, b * 2 + 1)
                        v.scalar_tensor_tensor(mx[:, i, 1, :], mx[:, i, 1, :], SLOPE, mx[:, i, 1, :], ALU.mult, ALU.max).then_inc(shift_step, 1)
                        dve.wait_ge(shift_step, b * 2 + 2)
                        v.scalar_tensor_tensor(mx[:, i, 2, :], adv, SLOPE, mx[:, i, 1, :], ALU.mult, ALU.subtract).then_inc(shifted, 1)

                    def body(b, i, turn, last=False):
                        shifts(b, i)
                        for h in range(H):
                            if h == 0 and not last:
                                mask(b + 1, 1 - i, turn)
                            dve.wait_ge(relu_done, b * 4 + h + 1)
                            if h == 0:
                                dve.wait_ge(logs_ready, b + 1)
                                dve.wait_ge(shifted, b + 1)
                            v.scalar_tensor_tensor(u[h % 2], u[h % 2], mx[:, i, 2, h:h + 1], L, ALU.add, ALU.add).then_inc(sum_done, 1)
                            if not last:
                                source_max(b + 1, 1 - i, h)

                    mask(0, 0, 0)
                    for h in range(H):
                        source_max(0, 0, h)
                    body(0, 0, 0)
                    with dve.Fori(0, NT // 2 - 1) as m:
                        body(m * 2 + 1, 1, m)
                        body(m * 2 + 2, 0, m + 1)
                    body(NT - 2, 1, NT // 2 - 1)
                    body(NT - 1, 0, NT // 2, last=True)

                @block.scalar
                def _(act):
                    act.sem_inc(turned, 2)
                    act.sem_inc(used, 2)

                    def logs(b, i, turn):
                        act.wait_ge(mask_ready, b + 1)
                        a.activation(Cb[i][:, 0:S], Cb[i][:, 0:S], ACT.Ln, bias=tiny[:, 0:1]).then_inc(ln_ready, 1)

                    def relu(b, h):
                        act.wait_ge(turned, b * 4 + h + 1)
                        a.activation(u[h % 2], as_bc[:, h, :], ACT.Relu, scale=1.0 - SLOPE,
                                     bias=ad8[:, bass.ds(b * 4 + h, 1)]).then_inc(relu_done, 1)

                    def body(b, i, turn, first=False, last=False):
                        for h in range(H):
                            if h < 3:
                                relu(b, h + 1)
                            elif not last:
                                relu(b + 1, 0)
                            if h == 0 and not last:
                                logs(b + 1, 1 - i, turn)
                            for g in range(5):
                                j = (5 * h + g) % 2
                                act.wait_ge(scores_done, b * 20 + 5 * h + g + 1)
                                act.wait_ge(used, b * 20 + 5 * h + g + 1)
                                a.activation(PT[j][:, :], psT[j], ACT.Exp).then_inc(exp_done, 1)
                            if h == 0 and not first:
                                take_sums(b - 1, 1 - i)
                        if not first:
                            put_back(b - 1, 1 - i)

                    def take_sums(b, i):
                        act.wait_ge(used, b * 20 + 22)
                        a.activation(aggS[i][:, :], ps[0:C + 1, 4 + i, :], ACT.Copy).then_inc(sums_out, 1)

                    def put_back(b, i):
                        act.wait_ge(back, b + 1)
                        a.activation(nb[:, bass.ds(b, 1), :].rearrange("p o n -> p (o n)"), ps[:, 6, 0:H * (C + 1)], ACT.Copy).then_inc(sums_in, 1)

                    logs(0, 0, 0)
                    relu(0, 0)
                    body(0, 0, 0, first=True)
                    with act.Fori(0, NT // 2 - 1) as m:
                        body(m * 2 + 1, 1, m)
                        body(m * 2 + 2, 0, m + 1)
                    body(NT - 2, 1, NT // 2 - 1)
                    body(NT - 1, 0, NT // 2, last=True)
                    take_sums(NT - 1, 0)
                    put_back(NT - 1, 0)

                @block.tensor
                def _(pe):
                    pe.sem_inc(exp_done, 2)
                    pe.sem_inc(sums_out, 2)
                    pe.sem_inc(sums_in, 2)

                    def scores(b, h, g):
                        j = (5 * h + g) % 2
                        pe.wait_ge(exp_done, b * 20 + 5 * h + g + 1)
                        if g == 0:
                            pe.wait_ge(sum_done, b * 4 + h + 2)
                        for k in range(TG):
                            o = psT[j][:, k * P:(k + 1) * P]
                            s0 = (g * TG + k) * P
                            pt.matmul(o, u[h % 2][:, s0:s0 + P], ident[:, :], is_transpose=True, start=True, stop=False)
                            last = pt.matmul(o, A3[32 * h:32 * h + 32, s0:s0 + P], onesb[32 * h:32 * h + 32, :], start=False, stop=True)
                        last.then_inc(scores_done, 1)

                    def weigh(b, i, h, g):
                        j = (5 * h + g) % 2
                        if h == 0 and g == 0:
                            pe.wait_ge(sums_out, b + 1)
                        pe.wait_ge(exp_done, b * 20 + 5 * h + g + 3)
                        for k in range(TG):
                            s = g * TG + k
                            last = pt.matmul(ps[0:C + 1, 4 + i, h * P:(h + 1) * P], haug[:, s, h, :], PT[j][:, k * P:(k + 1) * P],
                                             start=s == 0, stop=s == NT - 1)
                        last.then_inc(used, 1)

                    def turn_back(b, i):
                        pe.wait_ge(sums_out, b + 3)
                        pe.wait_ge(sums_in, b + 2)
                        pt.matmul(ps[0:1, 7, 0:1], onesb[:, 0:1], onesb[:, 0:1], start=True, stop=True)
                        for h in range(H):
                            last = pt.transpose(ps[:, 6, h * (C + 1):(h + 1) * (C + 1)], aggS[i][:, h * P:(h + 1) * P],
                                                ident[0:C + 1, 0:C + 1])
                        last.then_inc(back, 1)

                    def body(b, i, turn, first=False):
                        for h in range(H):
                            for g in range(5):
                                scores(b, h, g)
                                if h or g:
                                    weigh(b, i, (5 * h + g - 1) // 5, (g - 1) % 5)
                                elif not first:
                                    weigh(b - 1, 1 - i, 3, 4)
                            pt.matmul(ps[0:1, 7, 0:1], onesb[:, 0:1], onesb[:, 0:1], start=True, stop=True, skip_group_check=True).then_inc(turned, 1)
                            if h == 2 and not first:
                                turn_back(b - 1, 1 - i)

                    body(0, 0, 0, first=True)
                    with pe.Fori(0, NT // 2) as m:
                        body(m * 2 + 1, 1, m)
                        body(m * 2 + 2, 0, m + 1)
                    weigh(NT - 1, 0, 3, 4)
                    turn_back(NT - 1, 0)

        def each(n, w=CW):
            return [(c, c * w, min(w, n - c * w)) for c in range(-(-n // w))]

        def bc_vec(k, n=NT):
            return vec[:, k:k + 1, :].to_broadcast([P, n, D])

        def split(dve):
            link(dve, "dve", v.tensor_copy(G[:, :, 0, :], hn))
            link(dve, "dve", v.tensor_tensor(rest, hn, G[:, :, 0, :], ALU.subtract))
            link(dve, "dve", v.tensor_copy(G[:, :, 1, :], rest))
            v.tensor_tensor(G[:, :, 2, :], rest, G[:, :, 1, :], ALU.subtract).then_inc(split_done, 1)

        USES = [7, 6, 6, 6]

        def stream_counts(sp, k, rows):
            def load(t_, i, m, n_rows=P):
                use = m + k * USES[i]
                if not (k == 0 and isinstance(m, int) and m == 0):
                    sp.wait_ge(ring_used[i], use)
                sp.dma_start(ring[i][0:n_rows, :], rows[bass.ds(t_ * P, n_rows), :]).then_inc(ring_in[i], 16)

            for i in range(4):
                load(i, i, 0)
            with sp.Fori(1, 6) as m:
                for i in range(4):
                    load(m * 4 + i, i, m)
            load(NT - 1, 0, 6, STAIL)

        def sum_edges(pe, k, self_loops=False):
            def tile(t_, i, m, first=False, last=False):
                rows = STAIL if last else P
                use = m + k * USES[i]
                pe.wait_ge(ring_in[i], use * 16 + 16)

                def part_of(part):
                    return G[0:rows, NT - 1, part, :] if last else G[:, bass.ds(t_, 1), part, :].rearrange("p o d -> p (o d)")

                def own():
                    for part in range(3):
                        ins = pt.matmul(psf[:, bass.ds(t_ * P, rows)], part_of(part), identb[0:rows, 0:rows], start=False, stop=False)
                    return ins

                if self_loops and last:
                    own()
                for part in range(3):
                    for c, c0, cw in each(S):
                        ins = pt.matmul(ps[:, c, 0:cw], part_of(part), ring[i][0:rows, c0:c0 + cw], start=first and part == 0,
                                        stop=last and part == 2)
                if self_loops and not last:
                    ins = own()
                ins.then_inc(ring_used[i], 1)

            pe.wait_ge(split_done, k + 1)
            for i in range(4):
                tile(i, i, 0, first=i == 0)
            with pe.Fori(1, 6) as m:
                for i in range(4):
                    tile(m * 4 + i, i, m)
            tile(NT - 1, 0, 6, last=True)

        def summed(eng, k):
            eng.wait_ge(ring_used[0], 7 * (k + 1))

        def phase_turn():
            f_names = ("staged_in0", "staged_in1", "turned", "taken", "stored0", "stored1", "x_in", "zeroed", "root_in", "root_out", "tt_in", "deg", "tail")
            staged0, staged1, turned, took, stored0, stored1, x_in, zeroed, root_in, root_out, tt_in, deg_made, tail = (sem("t_" + n) for n in f_names)
            staged, stored = [staged0, staged1], [stored0, stored1]
            BANKS = [(0, 7), (7, 13), (13, 19), (19, 25)]

            def bank16(i, g, n, w):
                return ps[:, 4 * i + g, :].bitcast(BF16)[:, 0:n * P].rearrange("p (t d) -> p t d", d=P)[:, :, 0:w]

            with nc.Block() as block:
                @block.sync
                def _(sp):
                    load_x(sp, zeroed, x_in)
                    sp.dma_start(TT[:, 0:S], types_d).then_inc(tt_in, 16)

                    def store(pair, j, w=2 * P):
                        cols_ = bass.ds(pair * 2 * P, w)
                        sp.dma_start(turned16[0:(NT - 1) * P, cols_].rearrange("(t p) d -> p t d", p=P), stageT[j][:, 0:NT - 1, 0:w]).then_inc(stored[j], 16)
                        sp.dma_start(turned16[(NT - 1) * P:S, cols_], stageT[j][0:STAIL, NT - 1, 0:w]).then_inc(stored[j], 16)

                    with sp.Fori(0, 6) as q:
                        for j in range(2):
                            sp.wait_ge(took, q * 16 + 8 * j + 16)
                            store(q * 2 + j, j)
                    sp.wait_ge(took, 108)
                    store(12, 0, STAIL)
                    sp.wait_ge(stored[0], 32 * 8)
                    sp.wait_ge(stored[1], 32 * 7)

                @block.gpsimd
                def _(pool):
                    gp.memset(x[:, NT - 1, :], 0.0).then_inc(zeroed, 1)
                    for i in range(2):
                        gp.memset(stg16[i][:, S:SP_], 0.0)
                    gp.memset(TT[:, S:SP_], 0.0).then_inc(tail, 1)

                    def load(b, i, n=P):
                        pool.dma_start(stg16[i][0:n, 0:S], rows16[bass.ds(b * P, n), :]).then_inc(staged[i], 16)

                    load(0, 0)
                    load(1, 1)
                    with pool.Fori(1, 12) as m:
                        for i in range(2):
                            pool.wait_ge(turned, m * 8 - 4 + 4 * i)
                            load(m * 2 + i, i)
                    pool.wait_ge(turned, 92)
                    load(NT - 1, 0, STAIL)
                    for k in range(2):
                        pool.wait_ge(root_in, k + 1)
                        gp.tensor_tensor(rstd[:, :], rstd[:, :], mhalf[:, :], ALU.pow).then_inc(root_out, 1)
                    pool.wait_ge(root_in, 3)
                    gp.tensor_tensor(dinv[:, :], dinv[:, :], mhalf[:, :], ALU.pow).then_inc(root_out, 1)

                @block.tensor
                def _(pe):
                    pe.wait_ge(tail, 1)

                    def turn(b, i, turn_, n=P):
                        pe.wait_ge(staged[i], turn_ * 16 + 16)
                        for g, (t0, t1) in enumerate(BANKS):
                            pe.wait_ge(took, b * 4 + g + 1)
                            o = bank16(i, g, t1 - t0, n)
                            for k in range(t0, t1):
                                last = pt.transpose(o[:, k - t0, :], stg16[i][0:n, k * P:(k + 1) * P], identb[0:n, 0:n])
                            last.then_inc(turned, 1)

                    with pe.Fori(0, 12) as m:
                        turn(m * 2, 0, m)
                        turn(m * 2 + 1, 1, m)
                    turn(NT - 1, 0, 12, STAIL)
                    pe.wait_ge(took, 108)
                    for k in range(NT):
                        pt.matmul(ps[:, 0, k:k + 1], acc[:, k * P:(k + 1) * P], ones[:, 0:1], start=True, stop=True)
                    pe.wait_ge(tt_in, 16)
                    for k in range(NT):
                        last = pt.matmul(ps[:, 1, k:k + 1], TT[:, k * P:(k + 1) * P], ones[0:NTYPE, 0:1], start=True, stop=True)
                    last.then_inc(deg_made, 1)

                @block.scalar
                def _(act):
                    act.sem_inc(took, 8)
                    act.sem_inc(stored[0], 32)
                    act.sem_inc(stored[1], 32)

                    def take(b, i, j, q, w=P):
                        act.wait_ge(stored[j], q * 32 + 32)
                        for g, (t0, t1) in enumerate(BANKS):
                            act.wait_ge(turned, b * 4 + g + 1)
                            a.activation(stageT[j][:, t0:t1, i * P:i * P + w], bank16(i, g, t1 - t0, w), ACT.Copy).then_inc(took, 1)

                    with act.Fori(0, 6) as q:
                        for j in range(2):
                            for i in range(2):
                                take(q * 4 + 2 * j + i, i, j, q)
                    take(NT - 1, 0, 0, 6, STAIL)

                @block.vector
                def _(dve):
                    att = nb[:, :, :].rearrange("p t (h c) -> p t h c", h=H)
                    link(dve, "dve", v.tensor_scalar(rden[:, :, :], att[:, :, :, C], 1e-16, None, ALU.add))
                    link(dve, "dve", v.reciprocal(rden[:, :, :], rden[:, :, :]))
                    for h in range(H):
                        last = v.tensor_tensor(att_o[:, :, h * C:(h + 1) * C], att[:, :, h, 0:C],
                                               rden[:, :, h:h + 1].to_broadcast([P, NT, C]), ALU.mult)
                    link(dve, "dve", last)
                    link(dve, "dve", v.tensor_tensor(att_o, att_o, bc_vec(0), ALU.add))
                    layer_stats(dve, att_o, root_in, root_out, 1)
                    link(dve, "dve", v.tensor_tensor(att_o, att_o, over_features(mv[:, :, 0]), ALU.subtract))
                    link(dve, "dve", v.tensor_tensor(att_o, att_o, over_features(rstd[:, :]), ALU.mult))
                    link(dve, "dve", v.tensor_tensor(att_o, att_o, bc_vec(1), ALU.mult))
                    link(dve, "dve", v.tensor_tensor(att_o, att_o, bc_vec(2), ALU.add))
                    dve.wait_ge(x_in, 32)
                    link(dve, "dve", v.scalar_tensor_tensor(x, att_o, 0.0, x, ALU.max, ALU.add))
                    layer_stats(dve, x, root_in, root_out, 2)
                    norm_relu(dve)
                    dve.wait_ge(deg_made, 1)
                    link(dve, "dve", v.tensor_scalar(rdeg[:, :], ps[:, 0, 0:NT], 1.0, None, ALU.max))
                    link(dve, "dve", v.reciprocal(rdeg[:, :], rdeg[:, :]))
                    v.tensor_scalar(dinv[:, :], ps[:, 1, 0:NT], 1.0, None, ALU.add).then_inc(root_in, 1)
                    dve.wait_ge(root_out, 3)

        def phase_gated():
            names = ("h_by_f", "h_out", "sum_out_act", "sum_out_dve", "msg", "msg_out", "gates", "rz", "pre", "cand", "new", "back", "added", "root_in", "root_out", "zero", "deg", "deg_out", "diag")
            (h_by_f, h_out, sum_act, sum_dve, msg, msg_out, gates, rz, pre, cand, new, back, added, root_in, root_out, zero, deg, deg_out, diag_ready) = (sem("g_" + n) for n in names)
            with nc.Block() as block:
                @block.sync
                def _(sp):
                    stream_counts(sp, 0, turned16)

                @block.gpsimd
                def _(pool):
                    pool.wait_ge(deg, 7)
                    gp.memset(FB[:, S:SP_], 0.0).then_inc(zero, 1)
                    pool.wait_ge(root_in, 1)
                    gp.tensor_tensor(rstd[:, :], rstd[:, :], mhalf[:, :], ALU.pow).then_inc(root_out, 1)

                @block.tensor
                def _(pe):
                    for c, c0, cw in each(SP_):
                        for k in range(cw // P):
                            last = pt.transpose(ps[:, c, k * P:(k + 1) * P], hn[:, 4 * c + k, :], ident[:, :])
                        last.then_inc(h_by_f, 1)
                    pe.wait_ge(diag_ready, 1)
                    for c, c0, cw in each(SP_):
                        pe.wait_ge(h_out, c + 1)
                        pt.matmul(ps[:, c, 0:cw], ones[:, :], FB[:, c0:c0 + cw], start=True, stop=True).then_inc(deg, 1)
                    pe.wait_ge(deg_out, 7)
                    sum_edges(pe, 0)
                    pe.wait_ge(sum_act, 4)
                    pe.wait_ge(sum_dve, 3)
                    for c, c0, cw in each(S):
                        pt.matmul(ps[:, c, 0:cw], WT[:, 0, :], FB[:, c0:c0 + cw], start=True, stop=False)
                        pt.matmul(ps[:, c, 0:cw], embx[:, :], TT[:, c0:c0 + cw], start=False, stop=True).then_inc(msg, 1)
                    pe.wait_ge(msg_out, 7)
                    def gate(c, c0, cw):
                        if c >= 2:
                            pe.wait_ge(added, c - 1)
                        b0 = 4 * (c % 2)
                        m_, h_ = FC[:, c0:c0 + cw], FA[:, c0:c0 + cw]
                        for k in range(2):
                            pt.matmul(ps[:, b0 + k, 0:cw], WT[:, 1 + k, :], m_, start=True, stop=False)
                            pt.matmul(ps[:, b0 + k, 0:cw], WT[:, 4 + k, :], h_, start=False, stop=True)
                        pt.matmul(ps[:, b0 + 2, 0:cw], WT[:, 3, :], m_, start=True, stop=True)
                        pt.matmul(ps[:, b0 + 3, 0:cw], WT[:, 6, :], h_, start=True, stop=True).then_inc(gates, 1)

                    def by_node(c, c0, cw):
                        pe.wait_ge(new, c + 1)
                        for k in range(-(-cw // P)):
                            last = pt.transpose(ps[:, 4 * (c % 2), k * P:(k + 1) * P], FB[:, c0 + k * P:c0 + (k + 1) * P], ident[:, :])
                        last.then_inc(back, 1)

                    pe.wait_ge(zero, 1)
                    for c, c0, cw in each(S):
                        gate(c, c0, cw)
                        if c:
                            by_node(*each(S)[c - 1])
                    by_node(*each(S)[6])

                @block.scalar
                def _(act):
                    for c, c0, cw in each(SP_):
                        act.wait_ge(h_by_f, c + 1)
                        a.activation(FA[:, c0:c0 + cw], ps[:, c, 0:cw], ACT.Copy).then_inc(h_out, 1)
                    for c, c0, cw in each(SP_):
                        act.wait_ge(deg, c + 1)
                        a.activation(DB[:, c0:c0 + cw], ps[:, c, 0:cw], ACT.Copy).then_inc(deg_out, 1)
                    summed(act, 0)
                    for c, c0, cw in each(S)[0::2]:
                        a.activation(FB[:, c0:c0 + cw], ps[:, c, 0:cw], ACT.Copy).then_inc(sum_act, 1)
                    for c, c0, cw in each(S):
                        act.wait_ge(msg, c + 1)
                        a.activation(FC[:, c0:c0 + cw], ps[:, c, 0:cw], ACT.Copy).then_inc(msg_out, 1)
                    for c, c0, cw in each(S):
                        act.wait_ge(gates, c + 1)
                        if c:
                            act.wait_ge(new, c)
                        b0 = 4 * (c % 2)
                        a.activation(gr[:, 0:cw], ps[:, b0, 0:cw], ACT.Sigmoid, bias=col[:, 12:13])
                        a.activation(gz[:, 0:cw], ps[:, b0 + 1, 0:cw], ACT.Sigmoid, bias=col[:, 13:14]).then_inc(rz, 1)
                        act.wait_ge(pre, c + 1)
                        a.activation(gn[:, 0:cw], gn[:, 0:cw], ACT.Tanh, bias=col[:, 2:3]).then_inc(cand, 1)

                @block.vector
                def _(dve):
                    link(dve, "dve", v.tensor_tensor(col[:, 12:14], col[:, 0:2], col[:, 3:5], ALU.add))
                    v.tensor_tensor(FB.rearrange("p (t d) -> p t d", d=P), ident[:, :].unsqueeze(1).to_broadcast([P, NT, P]),
                                    dinv[:, :].unsqueeze(2).to_broadcast([P, NT, P]), ALU.mult).then_inc(diag_ready, 1)
                    split(dve)
                    summed(dve, 0)
                    for c, c0, cw in each(S)[1::2]:
                        v.tensor_copy(FB[:, c0:c0 + cw], ps[:, c, 0:cw]).then_inc(sum_dve, 1)
                    for c, c0, cw in each(S):
                        b0 = 4 * (c % 2)
                        dve.wait_ge(rz, c + 1)
                        link(dve, "dve", v.scalar_tensor_tensor(gn[:, 0:cw], ps[:, b0 + 3, 0:cw], col[:, 5:6], gr[:, 0:cw], ALU.add, ALU.mult))
                        v.tensor_tensor(gn[:, 0:cw], gn[:, 0:cw], ps[:, b0 + 2, 0:cw], ALU.add).then_inc(pre, 1)
                        dve.wait_ge(cand, c + 1)
                        link(dve, "dve", v.tensor_tensor(gr[:, 0:cw], FA[:, c0:c0 + cw], gn[:, 0:cw], ALU.subtract))
                        link(dve, "dve", v.tensor_tensor(gr[:, 0:cw], gr[:, 0:cw], gz[:, 0:cw], ALU.mult))
                        v.tensor_tensor(FB[:, c0:c0 + cw], gr[:, 0:cw], gn[:, 0:cw], ALU.add).then_inc(new, 1)
                        dve.wait_ge(back, c + 1)
                        xs = x[:, 4 * c:4 * c + -(-cw // P), :].rearrange("p t d -> p (t d)")
                        n_ = -(-cw // P) * P
                        v.tensor_tensor(xs, xs, ps[:, b0, 0:n_], ALU.add).then_inc(added, 1)
                    dve.wait_ge(added, 7)
                    layer_stats(dve, x, root_in, root_out, 1)
                    norm_relu(dve)

        def phase_conv():
            names = ("h_by_f", "h_out", "mlp", "mlp_out", "bn_in", "bn_out", "normed", "conv", "scaled", "sum_out", "biased", "back", "added", "root_in", "root_out", "shifted")
            (h_by_f, h_out, mlp, mlp_out, bn_in, bn_out, normed, conv, scaled, sum_out, biased, back, added, root_in, root_out, shifted) = (sem("c_" + n) for n in names)

            def batch_norm(dve, n, g, b):
                for c, c0, cw in each(N):
                    v.bn_stats(bn6[:, c, :], FB[:, c0:c0 + cw])
                link(dve, "dve", v.memset(neg1[:, 3:4], 0.0))
                link(dve, "dve", v.bn_aggr(mv[:, 0, :], bn6[:, 0:7, :].rearrange("p c k -> p (c k)")))
                v.tensor_scalar(col[:, 18:19], mv[:, 0, 1:2], EPS, None, ALU.add).then_inc(bn_in, 1)
                dve.wait_ge(bn_out, n)
                link(dve, "dve", v.tensor_tensor(col[:, 20:21], col[:, 18:19], col[:, g:g + 1], ALU.mult))
                link(dve, "dve", v.tensor_tensor(col[:, 19:20], col[:, 20:21], mv[:, 0, 0:1], ALU.mult))
                v.tensor_tensor(col[:, 21:22], col[:, b:b + 1], col[:, 19:20], ALU.subtract).then_inc(shifted, 1)

            with nc.Block() as block:
                @block.sync
                def _(sp):
                    stream_counts(sp, 1, turned16)

                @block.gpsimd
                def _(pool):
                    for k in range(2):
                        pool.wait_ge(bn_in, k + 1)
                        gp.tensor_tensor(col[:, 18:19], col[:, 18:19], mhalf[:, 0:1], ALU.pow).then_inc(bn_out, 1)
                    pool.wait_ge(root_in, 1)
                    gp.tensor_tensor(rstd[:, :], rstd[:, :], mhalf[:, :], ALU.pow).then_inc(root_out, 1)

                @block.tensor
                def _(pe):
                    for c, c0, cw in each(SP_):
                        for k in range(cw // P):
                            last = pt.transpose(ps[:, c, k * P:(k + 1) * P], hn[:, 4 * c + k, :], ident[:, :])
                        last.then_inc(h_by_f, 1)
                    for c, c0, cw in each(SP_):
                        pe.wait_ge(h_out, c + 1)
                        pt.matmul(ps[:, c, 0:cw], WT[:, 10, :], FA[:, c0:c0 + cw], start=True, stop=True).then_inc(mlp, 1)
                    pe.wait_ge(normed, 1)
                    for c, c0, cw in each(SP_):
                        for k in range(cw // P):
                            last = pt.matmul(ps[:, c, k * P:(k + 1) * P], FA[:, c0 + k * P:c0 + (k + 1) * P], WT[:, 11, :], start=True, stop=True)
                        last.then_inc(conv, 1)
                    pe.wait_ge(scaled, 7)
                    sum_edges(pe, 1, self_loops=True)
                    pe.wait_ge(normed, 2)
                    for c, c0, cw in each(SP_):
                        for k in range(cw // P):
                            last = pt.transpose(ps[:, c, k * P:(k + 1) * P], FA[:, c0 + k * P:c0 + (k + 1) * P], ident[:, :])
                        last.then_inc(back, 1)

                @block.scalar
                def _(act):
                    for c, c0, cw in each(SP_):
                        act.wait_ge(h_by_f, c + 1)
                        a.activation(FA[:, c0:c0 + cw], ps[:, c, 0:cw], ACT.Copy).then_inc(h_out, 1)
                    for c, c0, cw in each(SP_):
                        act.wait_ge(mlp, c + 1)
                        a.activation(FB[:, c0:c0 + cw], ps[:, c, 0:cw], ACT.Identity, bias=col[:, 6:7]).then_inc(mlp_out, 1)
                    act.wait_ge(mlp_out, 7)
                    act.wait_ge(shifted, 1)
                    a.activation(FA, FB, ACT.Relu, scale=col[:, 20:21], bias=col[:, 21:22]).then_inc(normed, 1)
                    act.wait_ge(sum_out, 7)
                    a.activation(FB, FB, ACT.Identity, bias=col[:, 9:10]).then_inc(biased, 1)
                    act.wait_ge(biased, 1)
                    act.wait_ge(shifted, 2)
                    a.activation(FA, FB, ACT.Relu, scale=col[:, 20:21], bias=col[:, 21:22]).then_inc(normed, 1)

                @block.vector
                def _(dve):
                    dve.wait_ge(mlp_out, 7)
                    batch_norm(dve, 1, 7, 8)
                    for c, c0, cw in each(SP_):
                        k0, n_ = 4 * c, cw // P
                        dve.wait_ge(conv, c + 1)
                        v.tensor_tensor(hn[:, k0:k0 + n_, :], ps[:, c, 0:cw].rearrange("p (t d) -> p t d", d=D),
                                        dinv[:, k0:k0 + n_].unsqueeze(2).to_broadcast([P, n_, D]), ALU.mult).then_inc(scaled, 1)
                    dve.wait_ge(scaled, 7)
                    split(dve)
                    summed(dve, 1)
                    for c, c0, cw in each(S):
                        v.tensor_tensor(FB[:, c0:c0 + cw], ps[:, c, 0:cw], DB[:, c0:c0 + cw], ALU.mult).then_inc(sum_out, 1)
                    dve.wait_ge(biased, 1)
                    batch_norm(dve, 2, 10, 11)
                    for c, c0, cw in each(SP_):
                        dve.wait_ge(back, c + 1)
                        xs = x[:, 4 * c:4 * c + cw // P, :].rearrange("p t d -> p (t d)")
                        v.tensor_tensor(xs, xs, ps[:, c, 0:cw], ALU.add).then_inc(added, 1)
                    dve.wait_ge(added, 7)
                    layer_stats(dve, x, root_in, root_out, 1)
                    norm_relu(dve)

        def phase_mean():
            names = ("h_by_f", "h_out", "lin", "lin_out", "sum_out_act", "sum_out_dve", "out_ready", "out_st")
            h_by_f, h_out, lin, lin_out, sum_act, sum_dve, out_ready, out_st = (sem("m_" + n) for n in names)
            with nc.Block() as block:
                @block.sync
                def _(sp):
                    stream_counts(sp, 2, rows16)
                    stream_counts(sp, 3, rows16)
                    sp.wait_ge(out_ready, 1)
                    sp.dma_start(out[0:(NT - 1) * P, :].rearrange("(t p) d -> p t d", p=P), hn[:, 0:NT - 1, :]).then_inc(out_st, 16)
                    sp.dma_start(out[(NT - 1) * P:N, :], hn[0:TAIL, NT - 1, :]).then_inc(out_st, 16)
                    sp.wait_ge(out_st, 32)

                @block.tensor
                def _(pe):
                    for c, c0, cw in each(SP_):
                        for k in range(cw // P):
                            last = pt.transpose(ps[:, c, k * P:(k + 1) * P], hn[:, 4 * c + k, :], ident[:, :])
                        last.then_inc(h_by_f, 1)

                    def linear(src, w):
                        for c, c0, cw in each(SP_):
                            for k in range(cw // P):
                                last = pt.matmul(ps[:, c, k * P:(k + 1) * P], src[:, c0 + k * P:c0 + (k + 1) * P], WT[:, w, :], start=True, stop=True)
                            last.then_inc(lin, 1)

                    pe.wait_ge(h_out, 7)
                    linear(FA, 7)
                    for k in range(2):
                        pe.wait_ge(lin_out, 7 * (k + 1))
                        sum_edges(pe, 2 + k)
                        pe.wait_ge(sum_act, 4 * (k + 1))
                        pe.wait_ge(sum_dve, 3 * (k + 1))
                        linear(FB, 8 + k)

                @block.scalar
                def _(act):
                    for c, c0, cw in each(SP_):
                        act.wait_ge(h_by_f, c + 1)
                        a.activation(FA[:, c0:c0 + cw], ps[:, c, 0:cw], ACT.Copy).then_inc(h_out, 1)
                    for k in range(2):
                        summed(act, 2 + k)
                        for c, c0, cw in each(S)[0::2]:
                            a.activation(FB[:, c0:c0 + cw], ps[:, c, 0:cw], ACT.Relu).then_inc(sum_act, 1)

                @block.vector
                def _(dve):
                    for k in range(3):
                        for c, c0, cw in each(SP_):
                            k0, n_ = 4 * c, cw // P
                            o, src = hn[:, k0:k0 + n_, :], ps[:, c, 0:cw].rearrange("p (t d) -> p t d", d=D)
                            dve.wait_ge(lin, 7 * k + c + 1)
                            if k == 0:
                                v.tensor_tensor(o, src, bc_vec(3, n_), ALU.add).then_inc(lin_out, 1)
                            else:
                                v.tensor_tensor(o, src, rdeg[:, k0:k0 + n_].unsqueeze(2).to_broadcast([P, n_, D]), ALU.mult).then_inc(lin_out, 1)
                        dve.wait_ge(lin_out, 7 * (k + 1))
                        if k:
                            link(dve, "dve", v.tensor_tensor(hn, hn, bc_vec(3 + k), ALU.add))
                        if k == 2:
                            v.tensor_tensor(hn, hn, x, ALU.add).then_inc(out_ready, 1)
                            break
                        split(dve)
                        summed(dve, 2 + k)
                        for c, c0, cw in each(S)[1::2]:
                            v.tensor_scalar(FB[:, c0:c0 + cw], ps[:, c, 0:cw], 0.0, None, ALU.max).then_inc(sum_dve, 1)

        acc_done, shift_step, shifted = sem("a_acc_done"), sem("a_shift_step"), sem("a_shifted")
        split_done = sem("split_done")
        ring_in = [sem(f"ring_in{i}") for i in range(4)]
        ring_used = [sem(f"ring_used{i}") for i in range(4)]
        s_iota = sem("iota_step")
        phase_counts()
        phase_nodes()
        phase_attention()
        phase_turn()
        phase_gated()
        phase_conv()
        phase_mean()


_IN = ["x", "src", "dst", "edge_type_9", "L0_gnn_W", "L0_gnn_a_src", "L0_gnn_a_dst", "L0_gnn_bias", "L0_gnn_gamma", "L0_gnn_beta",
       "L1_gnn_W_msg", "L1_gnn_b_msg", "L1_gnn_edge_embed", "L1_gnn_W_ih", "L1_gnn_W_hh", "L1_gnn_b_ih", "L1_gnn_b_hh",
       "L2_gnn_W_mlp", "L2_gnn_b_mlp", "L2_gnn_gamma1", "L2_gnn_beta1", "L2_gnn_W_conv", "L2_gnn_b_conv", "L2_gnn_gamma2", "L2_gnn_beta2",
       "L3_gnn_W1", "L3_gnn_b1", "L3_gnn_W2", "L3_gnn_b2", "L3_gnn_W3", "L3_gnn_b3"]
DBG = False


def kernel(**inputs):
    import concourse.bacc as _bacc
    from concourse.bass_utils import run_bass_kernel_spmd as _run
    nc = _bacc.Bacc("TRN2", target_bir_lowering=False, num_devices=1)
    arrays, aps = {}, {}
    for name in _IN:
        a = np.ascontiguousarray(inputs[name])
        arrays[f"in_{name}"] = a
        aps[name] = nc.dram_tensor(f"in_{name}", a.shape, mybir.dt.from_np(a.dtype), kind="ExternalInput").ap()
    out = nc.dram_tensor("out_x", (N, D), F32, kind="ExternalOutput").ap()
    gnn_program(nc, aps, out, DBG)
    r = _run(nc, [arrays], core_ids=[0])
    return r.results[0]["out_x"]
```

```python
import numpy as np
import concourse.bass as bass
from concourse import mybir
from contextlib import ExitStack

F32 = mybir.dt.float32
BF16 = mybir.dt.bfloat16
I32 = mybir.dt.int32
I16 = mybir.dt.int16
ALU = mybir.AluOpType
ACT = mybir.ActivationFunctionType
AX = mybir.AxisListType

P = 128
N, D, E = 3125, 128, 103125
H, C = 4, 32
NTYPE = 9
ET = 125
NE = E // ET
EP, EJ = 75, 11
Q = 4
R = 784
S = Q * R
GD = P // Q
NG = S // GD
U = 3
PADE = 4
TB, TK = 112, 7
HALF = 7
NT = 25
SP_ = NT * P
TAIL = N - (NT - 1) * P
STAIL = S - (NT - 1) * P
CW = 512
NC7 = 7
CHUNKS = [(c * CW, min(CW, S - c * CW)) for c in range(NC7)]
TG = 5
EPS = 1e-5
BIG = 1e30
TINY = 2.0 ** -60
SLOPE = 0.2
BF16_MAX_COUNT = 256.0
NEG_HUGE = -3.0e38


def gnn_program(nc, t, out, dbg):
    ctx = ExitStack()
    with ctx:
        def sb(name, shape, dt):
            return ctx.enter_context(nc.sbuf_tensor(name, shape, dt))

        def sem(name):
            return ctx.enter_context(nc.semaphore(name))

        scratch = "ExternalOutput" if dbg else "Internal"

        def dram(name, shape, dt):
            return nc.dram_tensor(name, shape, dt, kind=scratch).ap()

        count32 = dram("count32", (NG * P, R), F32)
        count16 = dram("count16", (NG * P, R), BF16)
        turned16 = dram("turned16", (S, S), BF16)
        residue = dram("residue", (S, S), BF16)
        residue_turned = dram("residue_turned", (S, S), BF16)
        bounds_d = dram("bounds_d", (2, NE), F32)
        win_d = dram("win_d", (NG, 2), I32)
        types_d = dram("types_d", (NTYPE, S), F32)
        hn_d = dram("hn_d", (SP_, D), F32)
        rows32 = count32.rearrange("(d q) r -> d (q r)", q=Q)
        rows16 = count16.rearrange("(d q) r -> d (q r)", q=Q)

        AW = 38400
        arena = sb("arena", [P, AW], F32)

        def ar(a, shape, dt=F32, parts=P, pb=0):
            n = int(np.prod(shape)) * mybir.dt.size(dt)
            assert n % 4 == 0 and a + n // 4 <= AW, (a, shape)
            v = arena[pb:pb + parts, a:a + n // 4]
            if dt != F32:
                v = v.bitcast(dt)
            if len(shape) == 2:
                v = v.rearrange("p (a b) -> p a b", b=shape[1])
            if len(shape) == 3:
                v = v.rearrange("p (a b c) -> p a b c", b=shape[1], c=shape[2])
            return v

        e_int = ar(12800, [3, EJ * ET], I32, EP)
        e_f = ar(16928, [3, EJ * ET], F32, EP)
        e_t = ar(21056, [EJ * ET], F32, EP)
        e_key = ar(22432, [EJ * ET], F32, EP)
        key = ar(23808, [NE + PADE], F32, ET)
        rem = ar(24640, [NE + PADE], F32, ET)
        typ = ar(25472, [NE + PADE], F32, ET)
        Y = ar(26304, [NE + PADE + 1, NTYPE + 1], BF16, ET)
        A = [ar(30460 + 64 * i, [P], BF16, ET) for i in range(U)]
        B = [ar(30972 + 392 * i, [R], BF16, ET) for i in range(U)]
        stage32 = [ar(34108 + 784 * i, [R]) for i in range(2)]
        stage16 = [ar(35676 + 392 * i, [R], BF16) for i in range(2)]
        ovf_junk = [ar(36460 + 392 * i, [R], BF16) for i in range(2)]
        turned_st = ar(12800, [Q * TK, 2 * HALF * GD], BF16, TB)
        tb = ar(0, [2, NE + 1], F32, NG)
        cov = ar(1700, [NE + 1], F32, NG)
        iota_t = ar(2600, [NE + 1], F32, NG)
        iota_i = ar(3500, [NE + 1], I32, NG)
        iota_keys = ar(5500, [NG * P], I16, ET)
        iotaR = ar(4600, [R], I16, ET)
        T32 = ar(32000, [NTYPE, NG], F32, GD)
        T98 = ar(33000, [NTYPE, GD], F32, NG)
        WAb = ar(19200, [H, P])
        as_bc = ar(0, [H, SP_])
        Cb = [ar(12800 + 3200 * i, [SP_]) for i in range(2)]
        nm = [ar(22400 + 1600 * i, [SP_], BF16) for i in range(2)]
        u = [ar(25600 + 3200 * i, [SP_]) for i in range(2)]
        acc = ar(32000, [SP_])
        junk = ar(35200, [SP_], BF16)
        A3 = ar(36800, [SP_], BF16)
        Z, Zb = ar(19200, [SP_]), junk
        hT0 = ar(12800, [SP_])
        ring = [ar(9600 + 1568 * i, [S], BF16) for i in range(4)]
        G = ar(15872, [NT, 3, D], BF16)
        FA, FB, FC = ar(20672, [SP_]), ar(23872, [SP_]), ar(27072, [SP_])
        rest = FC.rearrange("p (t d) -> p t d", d=D)
        att_o = rest
        gr, gz, gn = (ar(30272 + CW * i, [CW]) for i in range(3))
        DB = ar(0, [SP_])
        TT = ar(35200, [SP_], F32, NTYPE)

        nb = sb("nb", [P, NT, H * (C + 1)], F32)
        hn = nb[:, :, 0:D]
        haug = sb("haug", [P, NT, H, C + 1], F32)
        x = haug[:, :, :, :].rearrange("p t h c -> p (t h c)")[:, 0:NT * D].rearrange("p (t d) -> p t d", d=D)
        PT = [sb(f"PT{i}", [P, TG * P], F32) for i in range(2)]
        aggS = [sb(f"aggS{i}", [C + 1, H * P], F32) for i in range(2)]
        ident = sb("ident", [P, P], F32)
        identb = sb("identb", [P, P], BF16)
        ones = sb("ones", [P, P], F32)
        onesb = sb("onesb", [P, P], BF16)
        head_rows = sb("head_rows", [P, H, P], BF16)
        qsum = sb("qsum", [P, GD], F32)
        Wraw = ar(0, [10, D])
        WT = sb("WT", [P, 12, D], F32)
        WW = sb("WW", [P, D + 2 * H], F32)
        wa_t = sb("wa_t", [P, D], F32)
        vec = sb("vec", [P, 8, D], F32)
        col = sb("col", [P, 24], F32)
        embx = sb("embx", [NTYPE, D], F32)
        bmsg9 = sb("bmsg9", [NTYPE, D], F32)
        Traw = sb("Traw", [P, NG, NTYPE], F32)
        asd = sb("asd", [P, NT, 2 * H], F32)
        ad8 = sb("ad8", [P, NT * H], F32)
        mx = sb("mx", [P, 2, 3, H], F32)
        wins = sb("wins", [1, NG * 2], I32)
        win = sb("win", [NG, 2], F32)
        win_i = sb("win_i", [NG, 2], I32)
        tlo = sb("tlo", [EP, 2, EJ], F32)
        grp_i = sb("grp_i", [NG, 1], I32)
        tiny = sb("tiny", [P, 1], F32)
        neg1 = sb("neg1", [P, 4], F32)
        grp = sb("grp", [NG, 2], F32)
        it9 = sb("it9", [ET, NTYPE], F32)
        it9i = sb("it9i", [ET, NTYPE], I32)
        ovf = sb("ovf", [P, NG], F32)
        flag_f = sb("flag_f", [P, 1], F32)
        flag_i = sb("flag_i", [1, 1], I32)
        bn6 = sb("bn6", [P, NT, 6], F32)
        mv = sb("mv", [P, NT, 2], F32)
        rstd = sb("rstd", [P, NT], F32)
        rden = sb("rden", [P, NT, H], F32)
        dinv = sb("dinv", [P, NT], F32)
        rdeg = sb("rdeg", [P, NT], F32)
        mhalf = sb("mhalf", [P, NT], F32)
        masks = sb("masks", [P, H], F32)

        ps = ctx.enter_context(nc.psum_tensor("ps", [P, 8, CW], F32))
        psf = ps[:, :, :].rearrange("p a b -> p (a b)")


        v, a, gp, pt, sy = nc.vector, nc.scalar, nc.gpsimd, nc.tensor, nc.sync
        s_chain = {e: sem("chain_" + e) for e in ("dve", "act", "pool")}
        chain = {e: 0 for e in s_chain}

        def link(eng, which, ins):
            chain[which] += 1
            ins.then_inc(s_chain[which], 1)
            eng.wait_ge(s_chain[which], chain[which])

        NPASS = NG // 2

        def halves(x):
            return x.rearrange("p (h n) -> p h n", h=2)

        weights_in, zeroed, x_in = sem("weights_in"), sem("x_zeroed"), sem("x_in")
        WSRC = [("L1_gnn_W_msg", 1), ("L1_gnn_W_ih", 3), ("L1_gnn_W_hh", 3), ("L3_gnn_W1", 1), ("L3_gnn_W2", 1), ("L3_gnn_W3", 1)]
        COLS = [("L1_gnn_b_ih", 0, 3), ("L1_gnn_b_hh", 3, 3), ("L2_gnn_b_mlp", 6, 1), ("L2_gnn_gamma1", 7, 1), ("L2_gnn_beta1", 8, 1),
                ("L2_gnn_b_conv", 9, 1), ("L2_gnn_gamma2", 10, 1), ("L2_gnn_beta2", 11, 1)]
        N_WEIGHTS = len(WSRC) + 3 + 8 + len(COLS) + 2

        def load_weights(sp):
            k = 0
            for name, n in WSRC:
                sp.dma_start(Wraw[:, k:k + n, :], t[name].rearrange("(w p) d -> p w d", p=P)).then_inc(weights_in, 16)
                k += n
            sp.dma_start(WT[:, 10, :], t["L2_gnn_W_mlp"]).then_inc(weights_in, 16)
            sp.dma_start(WT[:, 11, :], t["L2_gnn_W_conv"]).then_inc(weights_in, 16)
            sp.dma_start(WW[:, 0:D], t["L0_gnn_W"]).then_inc(weights_in, 16)
            for k, name in enumerate(("L0_gnn_a_src", "L0_gnn_a_dst")):
                sp.dma_start(vec[:, 6 + k, :], t[name].rearrange("h c -> (h c)").partition_broadcast(P)).then_inc(weights_in, 16)
            for k, name in enumerate(("L0_gnn_bias", "L0_gnn_gamma", "L0_gnn_beta", "L3_gnn_b1", "L3_gnn_b2", "L3_gnn_b3")):
                sp.dma_start(vec[:, k, :], t[name].partition_broadcast(P)).then_inc(weights_in, 16)
            for name, c0, n in COLS:
                sp.dma_start(col[:, c0:c0 + n], t[name].rearrange("(k p) -> p k", p=P), allow_slow_non_contiguous=True).then_inc(weights_in, 16)
            sp.dma_start(embx[:, :], t["L1_gnn_edge_embed"]).then_inc(weights_in, 16)
            sp.dma_start(bmsg9[:, :], t["L1_gnn_b_msg"].partition_broadcast(NTYPE)).then_inc(weights_in, 16)

        def load_x(sp, zeroed, x_in):
            sp.dma_start(x[:, 0:NT - 1, :], t["x"][0:(NT - 1) * P, :].rearrange("(t p) d -> p t d", p=P)).then_inc(x_in, 16)
            sp.wait_ge(zeroed, 1)
            sp.dma_start(x[0:TAIL, NT - 1, :], t["x"][(NT - 1) * P:N, :]).then_inc(x_in, 16)

        def phase_counts():
            edges_in, consts, split_ready, cols_out, cols_in = sem("edges_in"), sem("consts"), sem("split_ready"), sem("cols_out"), sem("cols_in")
            bounds_ready, bounds_st, bounds_in = sem("bounds_ready"), sem("bounds_st"), sem("bounds_in")
            win_ready, win_st, win_in = sem("win_ready"), sem("win_st"), sem("win_in")
            hot = [sem(f"hot{i}") for i in range(U)]
            hot_used = [sem(f"hot_used{i}") for i in range(U)]
            group_done = [sem(f"group_done{i}") for i in range(2)]
            staged = [sem(f"staged{i}") for i in range(2)]
            stored = [sem(f"stored{i}") for i in range(2)]
            turned_out, turned_stored, sp_step = sem("turned_out"), sem("turned_stored"), sem("sp_step")
            def window(eng, regs, g):
                eng.reg_load(regs, wins[0:1, bass.ds(g * 2, 2)])
                return (eng.snap(regs.lo, min_val=0, max_val=NE - 3 * U + 1), eng.snap(regs.hi, min_val=3 * U, max_val=NE + U - 1))

            with nc.Block() as block:
                @block.sync
                def _(sp):
                    for k, n in enumerate(("src", "dst", "edge_type_9")):
                        sp.dma_start(e_int[:, k, :], t[n].rearrange("(p e) -> p e", p=EP)).then_inc(edges_in, 16)
                    sp.wait_ge(bounds_ready, 1)
                    sp.dma_start(bounds_d.rearrange("k (p j) -> p k j", p=EP), tlo[:, :, :]).then_inc(bounds_st, 16)
                    sp.wait_ge(bounds_st, 16)
                    sp.dma_start(tb[:, :, 0:NE], bounds_d.partition_broadcast(NG)).then_inc(bounds_in, 16)
                    sp.wait_ge(win_ready, 1)
                    sp.dma_start(win_d, win_i[:, :]).then_inc(win_st, 16)
                    sp.wait_ge(win_st, 16)
                    sp.dma_start(wins[0:1, :], win_d.rearrange("(o g) k -> o (g k)", o=1)).then_inc(win_in, 16)
                    load_weights(sp)
                    load_x(sp, zeroed, x_in)
                    with sp.Fori(0, HALF) as r:
                        for i in range(2 * HALF):
                            rows = bass.ds((r * (2 * HALF) + i) * P, P)
                            sp.wait_ge(staged[i % 2], r * HALF + i // 2 + 2)
                            sp.sem_inc(sp_step, 1)
                            for dst, st in ((count32, stage32), (count16, stage16)):
                                sp.dma_start(dst[rows, :], st[i % 2]).then_inc(stored[i % 2], 16)
                            if i in (HALF, 2 * HALF - 1):
                                half = i // HALF if i > HALF else 0
                                sp.wait_ge(turned_out, r * (2 * HALF) + HALF * half + HALF + 1)
                                sp.sem_inc(sp_step, 1)
                                sp.wait_ge(turned_stored, r * 32 + 16 * half + 33)
                                sp.sem_inc(sp_step, 1)
                                sp.dma_start(turned16[:, bass.ds((r * 2 + half) * HALF * GD, HALF * GD)].rearrange("(j p) d -> p j d", p=TB),
                                             turned_st[:, :, half * HALF * GD:(half + 1) * HALF * GD]).then_inc(turned_stored, 16)
                    for b in range(2):
                        sp.wait_ge(stored[b], 32 * (NPASS + 1))
                    sp.wait_ge(turned_stored, 16 * 2 * HALF + 33)

                @block.gpsimd
                def _(pool):
                    gp.memset(x[:, NT - 1, :], 0.0).then_inc(zeroed, 1)
                    link(pool, "pool", gp.memset(ones[:, :], 1.0))
                    gp.affine_select(out=ident[:, :], in_=ones[:, :], compare_op=ALU.is_equal, fill=0.0, base=0,
                                     pattern=[[-1, P]], channel_multiplier=1)
                    gp.memset(onesb[:, :], 1.0)
                    gp.memset(stage16[1], 0.0)
                    link(pool, "pool", gp.memset(head_rows[:, :, :], 0.0))
                    for h in range(H):
                        link(pool, "pool", gp.memset(head_rows[32 * h:32 * h + 32, h, :], 1.0))
                    gp.iota(iota_i[:, 0:NE], [[1, NE]], base=0, channel_multiplier=0)
                    gp.iota(grp_i[:, :], [[1, 1]], base=0, channel_multiplier=GD)
                    gp.iota(it9i[:, :], [[1, NTYPE]], base=0, channel_multiplier=0)
                    gp.iota(iota_keys, [[1, NG * P]], base=0, channel_multiplier=0)
                    gp.iota(iotaR, [[1, R]], base=0, channel_multiplier=0).then_inc(consts, 1)

                @block.tensor
                def _(pe):
                    for i in range(U):
                        pe.sem_inc(hot_used[i], 1)
                    pe.wait_ge(consts, 1)
                    pe.wait_ge(split_ready, 1)
                    k = 0
                    for src in (e_key, e_f[:, 0, :], e_f[:, 2, :]):
                        for j0, j1 in ((0, 6), (6, EJ)):
                            for j in range(j0, j1):
                                last = pt.transpose(ps[0:ET, k, (j - j0) * EP:(j - j0 + 1) * EP],
                                                    src[:, j * ET:(j + 1) * ET], ident[0:EP, 0:EP])
                            last.then_inc(cols_out, 1)
                            k += 1
                    pe.wait_ge(cols_in, k)
                    pe.wait_ge(win_in, 16)
                    window_regs = pe.alloc_register64("pe_window")
                    turn_reg = pe.alloc_register("pe_turn")
                    pe.reg_mov(turn_reg, 1)

                    def turn(t0, b, first, last, m=None):
                        n = pe.snap(turn_reg)
                        if first:
                            pe.wait_ge(staged[b], m + 1)
                        for i in range(U):
                            pe.wait_ge(hot[i], n)
                            start, stop = first and i == 0, last and i == U - 1
                            for h in range(2):
                                pt.matmul(ps[:, 3 * b + h, 0:R // 2], A[i], B[i][:, h * (R // 2):(h + 1) * (R // 2)],
                                          start=start, stop=stop)
                            pt.matmul(ps[:, 3 * b + 2, 0:NTYPE], A[i], Y[:, bass.ds(t0 + i, 1), 0:NTYPE],
                                      start=start, stop=stop).then_inc(hot_used[i], 1)
                        pe.reg_add(turn_reg, turn_reg, 1)

                    def transpose_group(b):
                        for k in range(TK):
                            pt.transpose(ps[0:TB, 6, :].bitcast(BF16)[:, k * P:(k + 1) * P], stage16[b][:, k * TB:(k + 1) * TB], identb[:, :])

                    with pe.Fori(0, NPASS) as m:
                        for b in range(2):
                            lo, hi = window(pe, window_regs, m * 2 + b)
                            turn(lo, b, True, False, m)
                            with pe.Fori(lo + U, hi - U, U) as tt:
                                turn(tt, b, False, False)
                            turn(hi - U, b, False, True)
                            pe.wait_ge(staged[1 - b], m + 1 + b)
                            transpose_group(1 - b)
                            pt.matmul(ps[0:1, 7, 0:1], onesb[:, 0:1], onesb[:, 0:1], start=True, stop=True).then_inc(group_done[b], 1)
                    pe.wait_ge(staged[1], NPASS + 1)
                    transpose_group(1)
                    pt.matmul(ps[0:1, 7, 0:1], onesb[:, 0:1], onesb[:, 0:1], start=True, stop=True).then_inc(group_done[0], 1)

                @block.scalar
                def _(act):
                    for b in range(2):
                        act.sem_inc(staged[b], 1)
                        act.sem_inc(stored[b], 32)
                    act.sem_inc(turned_stored, 33)
                    a.preload_act_table(ACT.Copy)
                    col_reg = act.alloc_register("turned_col")
                    act.reg_mov(col_reg, (2 * HALF - 1) * GD)

                    def take_turned(col_):
                        a.activation(turned_st.rearrange("p (q k) w -> p k q w", q=Q)[:, :, :, col_],
                                     ps[0:TB, 6, :].bitcast(BF16)[:, 0:TK * P].rearrange("p (k d q) -> p k q d", k=TK, q=Q),
                                     ACT.Copy).then_inc(turned_out, 1)

                    with act.Fori(0, NPASS) as m:
                        for b in range(2):
                            col_ = act.snap(col_reg, min_val=0, max_val=(2 * HALF - 1) * GD)
                            act.reg_add(col_reg, col_reg, GD)
                            act.reg_mod(col_reg, col_reg, 2 * HALF * GD)
                            halves_stored = act.snap((m * 2 + b + HALF - 1) // HALF)
                            act.wait_ge(group_done[b], m + 1)
                            act.wait_ge(turned_stored, halves_stored * 16 + 1)
                            take_turned(bass.ds(col_, GD))
                            act.wait_ge(stored[b], m * 32 + 32)
                            counts = ps[:, 3 * b:3 * b + 2, 0:R // 2]
                            a.activation(halves(stage32[b]), counts, ACT.Copy)
                            a.activation(halves(stage16[b]), counts, ACT.Copy)
                            a.activation(halves(ovf_junk[b]), counts, ACT.Relu, bias=neg1[:, 0:1],
                                         accum_out=ovf[:, bass.ds(m * 2 + b, 1)])
                            a.activation(Traw[:, bass.ds(m * 2 + b, 1), :].rearrange("p o k -> p (o k)"), ps[:, 3 * b + 2, 0:NTYPE],
                                         ACT.Copy).then_inc(staged[b], 1)
                    act.wait_ge(group_done[0], NPASS + 1)
                    act.wait_ge(turned_stored, 16 * 2 * HALF + 1)
                    take_turned(slice((2 * HALF - 1) * GD, 2 * HALF * GD))

                @block.vector
                def _(dve):
                    dve.wait_ge(edges_in, 48)
                    link(dve, "dve", v.tensor_copy(e_f, e_int))
                    v.tensor_reduce(tlo[:, 0, :], e_f[:, 1, :].rearrange("p (j e) -> p j e", j=EJ), AX.X, ALU.min)
                    v.tensor_reduce(tlo[:, 1, :], e_f[:, 1, :].rearrange("p (j e) -> p j e", j=EJ), AX.X, ALU.max).then_inc(bounds_ready, 1)
                    link(dve, "dve", v.tensor_scalar(e_t, e_f[:, 0, :], float(R), None, ALU.is_ge))
                    for k in (2, 3):
                        link(dve, "dve", v.tensor_scalar(e_key, e_f[:, 0, :], float(k * R), None, ALU.is_ge))
                        link(dve, "dve", v.tensor_tensor(e_t, e_t, e_key, ALU.add))
                    link(dve, "dve", v.scalar_tensor_tensor(e_f[:, 0, :], e_t, -float(R), e_f[:, 0, :], ALU.mult, ALU.add))
                    link(dve, "dve", v.scalar_tensor_tensor(e_key, e_f[:, 1, :], float(Q), e_t, ALU.mult, ALU.add))
                    v.tensor_scalar(e_f[:, 2, :], e_f[:, 2, :], 0.0, float(NTYPE - 1), ALU.max, ALU.min).then_inc(split_ready, 1)
                    v.memset(neg1[:, 0:1], -BF16_MAX_COUNT)
                    v.memset(tiny[:, :], TINY)
                    v.memset(key[:, NE:], -1.0)
                    v.memset(rem[:, NE:], 0.0)
                    v.memset(typ[:, NE:], 0.0)
                    k = 0
                    for dst in (key, rem, typ):
                        dv = dst[:, 0:NE].rearrange("e (p j) -> e j p", p=EP)
                        for j0, j1 in ((0, 6), (6, EJ)):
                            dve.wait_ge(cols_out, k + 1)
                            v.tensor_copy(dv[:, j0:j1, :], ps[0:ET, k, 0:(j1 - j0) * EP].rearrange("e (j p) -> e j p", p=EP)).then_inc(cols_in, 1)
                            k += 1
                    dve.wait_ge(cols_in, k)
                    dve.wait_ge(consts, 1)
                    v.tensor_copy(identb[:, :], ident[:, :])
                    v.tensor_copy(iota_t[:, 0:NE], iota_i[:, 0:NE])
                    v.tensor_copy(grp[:, 0:1], grp_i[:, :])
                    link(dve, "dve", v.tensor_copy(it9[:, :], it9i[:, :]))
                    link(dve, "dve", v.tensor_scalar(grp[:, 1:2], grp[:, 0:1], float(GD - 1), None, ALU.add))
                    link(dve, "dve", v.tensor_tensor(Y[:, 0:NE + PADE, 0:NTYPE], typ.unsqueeze(2).to_broadcast([ET, NE + PADE, NTYPE]),
                                                     it9[:, :].unsqueeze(1).to_broadcast([ET, NE + PADE, NTYPE]), ALU.is_equal))
                    it = iota_t[:, 0:NE]
                    cv = cov[:, 0:NE]
                    t0, t1 = tb[:, 0, 0:NE], tb[:, 1, 0:NE]
                    dve.wait_ge(bounds_in, 16)
                    link(dve, "dve", v.tensor_scalar(cv, t0, grp[:, 1:2], None, ALU.is_le))
                    link(dve, "dve", v.scalar_tensor_tensor(cv, t1, grp[:, 0:1], cv, ALU.is_ge, ALU.mult))
                    link(dve, "dve", v.scalar_tensor_tensor(t0, it, 1.0, cv, ALU.add, ALU.mult))
                    link(dve, "dve", v.tensor_scalar(it, it, -1.0, float(NE), ALU.mult, ALU.add))
                    link(dve, "dve", v.tensor_tensor(t1, it, cv, ALU.mult))
                    link(dve, "dve", v.tensor_reduce(win[:, 0:1], t1, AX.X, ALU.max))
                    link(dve, "dve", v.tensor_reduce(win[:, 1:2], t0, AX.X, ALU.max))
                    link(dve, "dve", v.tensor_scalar(win[:, 0:1], win[:, 0:1], -1.0, float(NE), ALU.mult, ALU.add))
                    link(dve, "dve", v.tensor_scalar(win[:, 0:1], win[:, 0:1], float(NE - 3 * U + 1), None, ALU.min))
                    link(dve, "dve", v.tensor_tensor(win[:, 1:2], win[:, 1:2], win[:, 0:1], ALU.subtract))
                    link(dve, "dve", v.tensor_scalar(win[:, 1:2], win[:, 1:2], float(3 * U), (U - 1) / 2, ALU.max, ALU.add))
                    link(dve, "dve", v.tensor_scalar(win[:, 1:2], win[:, 1:2], 1.0 / U, None, ALU.mult))
                    link(dve, "dve", v.tensor_scalar(win[:, 1:2], win[:, 1:2], 2.0 ** 23, None, ALU.add))
                    link(dve, "dve", v.tensor_scalar(win[:, 1:2], win[:, 1:2], -2.0 ** 23, float(U), ALU.add, ALU.mult))
                    link(dve, "dve", v.tensor_tensor(win[:, 1:2], win[:, 1:2], win[:, 0:1], ALU.add))
                    v.tensor_copy(win_i[:, :], win[:, :]).then_inc(win_ready, 1)
                    dve.wait_ge(win_in, 16)
                    window_regs = dve.alloc_register64("dve_window")
                    turn_reg = dve.alloc_register("dve_turn")
                    dve.reg_mov(turn_reg, 1)
                    with dve.Fori(0, NG) as g:
                        lo, hi = window(dve, window_regs, g)
                        group_keys = iota_keys[:, bass.ds(dve.snap(g * P), P)]
                        with dve.Fori(lo, hi, U) as tt:
                            n = dve.snap(turn_reg)
                            for i in range(U):
                                dve.wait_ge(hot_used[i], n)
                                v.tensor_scalar(A[i], group_keys, key[:, bass.ds(tt + i, 1)], None, ALU.is_equal)
                                v.tensor_scalar(B[i], iotaR, rem[:, bass.ds(tt + i, 1)], None,
                                                ALU.is_equal).then_inc(hot[i], 1)
                            dve.reg_add(turn_reg, turn_reg, 1)

        def layer_stats(dve, y, root_in, root_out, n, counted=False):
            if not counted:
                for k in range(NT):
                    v.bn_stats(bn6[:, k, :], y[:, k, :])
            link(dve, "dve", v.memset(neg1[:, 2:3], 0.0))
            for k in range(NT):
                last = v.bn_aggr(mv[:, k, :], bn6[:, k, :])
            link(dve, "dve", last)
            v.tensor_scalar(rstd[:, :], mv[:, :, 1], EPS, None, ALU.add).then_inc(root_in, 1)
            dve.wait_ge(root_out, n)

        def tile_stats(dve, added, c):
            dve.wait_ge(added, c + 1)
            for k in range(4 * c, min(4 * c + 4, NT)):
                v.bn_stats(bn6[:, k, :], x[:, k, :])

        def over_features(ap, n=NT):
            return ap.unsqueeze(2).to_broadcast([P, n, D])

        def norm_relu(dve, normed_x):
            for k0 in range(0, NT, 4):
                k = slice(k0, min(k0 + 4, NT))
                n = k.stop - k0
                link(dve, "dve", v.tensor_tensor(hn[:, k, :], x[:, k, :], over_features(mv[:, k, 0], n), ALU.subtract))
                v.scalar_tensor_tensor(hn[:, k, :], hn[:, k, :], 0.0, over_features(rstd[:, k], n), ALU.max, ALU.mult).then_inc(normed_x, 1)
            dve.wait_ge(normed_x, 7)

        def taken(eng, outs, i):
            if i >= 0:
                eng.wait_ge(outs[i % 2], i // 2 + 1)

        def take_all(eng, which, made, outs, jobs, first=0):
            for i, pieces in enumerate(jobs):
                if (first + i) % 2 == which:
                    eng.wait_ge(made, first + i + 1)
                    for dst, src in pieces:
                        last = a.activation(dst, src, ACT.Copy) if which == 0 else v.tensor_copy(dst, src)
                    last.then_inc(outs[which], 1)

        def phase_nodes():
            made, var_ready, std_done, hn_ready = (sem(n) for n in ("n_made", "n_var", "n_std", "n_hn"))
            outs = [sem("n_out_act"), sem("n_out_dve")]
            ww_ready, wa_ready, tq_ready, t98_st = sem("n_ww"), sem("n_wa"), sem("n_tq"), sem("n_t98")
            jobs = []
            for b0, b1 in ((0, 4), (4, 8), (8, 10)):
                i = len(jobs)
                jobs.append([(WT[:, b0:b1, :], ps[:, i % 8, 0:(b1 - b0) * P].rearrange("p (w n) -> p w n", n=P))])
            for c in range(NC7):
                w = min(CW, SP_ - c * CW)
                jobs.append([(hT0[:, c * CW:c * CW + w], ps[:, len(jobs) % 8, 0:w])])
            trios = [(k, min(k + 3, NT)) for k in range(0, NT, 3)]
            for k0, k1 in trios:
                src = ps[:, len(jobs) % 8, 0:(k1 - k0) * (D + 2 * H)].rearrange("p (t n) -> p t n", n=D + 2 * H)
                jobs.append([(haug[:, k, :, 0:C], src[:, k - k0, 0:D].rearrange("p (h c) -> p h c", h=H)) for k in range(k0, k1)]
                            + [(asd[:, k0:k1, :], src[:, :, D:D + 2 * H])])
            for h in range(H):
                for c in range(NC7):
                    w = min(CW, SP_ - c * CW)
                    jobs.append([(as_bc[:, h, c * CW:c * CW + w], ps[:, len(jobs) % 8, 0:w])])
            for k in range(2):
                jobs.append([(T32[:, :, 49 * k:49 * k + 49].rearrange("p k g -> p g k"),
                              ps[0:GD, len(jobs) % 8, 0:49 * NTYPE].rearrange("p (g k) -> p g k", k=NTYPE))])
            jobs.append([(T98, ps[0:NG, len(jobs) % 8, 0:NTYPE * GD].rearrange("p (k d) -> p k d", k=NTYPE))])

            with nc.Block() as block:
                @block.sync
                def _(sp):
                    taken(sp, outs, 49)
                    sp.dma_start(types_d.rearrange("k (g d) -> g k d", d=GD), T98).then_inc(t98_st, 16)
                    sp.wait_ge(t98_st, 16)

                @block.gpsimd
                def _(pool):
                    link(pool, "pool", gp.memset(mhalf[:, :], -0.5))
                    pool.wait_ge(var_ready, 1)
                    gp.tensor_tensor(rstd[:, :], rstd[:, :], mhalf[:, :], ALU.pow).then_inc(std_done, 1)

                @block.vector
                def _(dve):
                    v.tensor_reduce(qsum[:, :], ident[:, :].rearrange("p (d q) -> p d q", q=Q), AX.X, ALU.add).then_inc(tq_ready, 1)
                    v.tensor_reduce(masks[:, 0:3], ident[:, :].rearrange("p (a k) -> p k a", k=32)[:, 0:3, :], AX.X, ALU.add)
                    dve.wait_ge(weights_in, 16 * N_WEIGHTS)
                    v.tensor_tensor(embx[:, :], embx[:, :], bmsg9[:, :], ALU.add)
                    for k in range(2):
                        link(dve, "dve", v.tensor_tensor(wa_t[:, :], WW[:, 0:D], vec[:, 6 + k, :], ALU.mult))
                        last = v.tensor_reduce(WW[:, D + H * k:D + H * k + H], wa_t[:, :].rearrange("p (h c) -> p h c", h=H), AX.X, ALU.add)
                        link(dve, "dve", last)
                    v.tensor_copy(WAb, WW[:, D:D + H].unsqueeze(2).to_broadcast([P, H, P])).then_inc(ww_ready, 1)
                    dve.wait_ge(x_in, 32)
                    layer_stats(dve, x, var_ready, std_done, 1)
                    norm_relu(dve, hn_ready)
                    take_all(dve, 1, made, outs, jobs[0:10])
                    v.memset(haug[:, :, :, C:C + 1], 1.0)
                    take_all(dve, 1, made, outs, jobs[10:], 10)
                    for k in range(len(jobs)):
                        taken(dve, outs, k)
                    v.tensor_scalar(ad8[:, :].rearrange("p (t h) -> p t h", h=H), asd[:, :, H:2 * H], 1.0 - SLOPE, None, ALU.mult)

                @block.scalar
                def _(act):
                    take_all(act, 0, made, outs, jobs[0:10])
                    act.wait_ge(x_in, 32)
                    act.wait_ge(hn_ready, 7)
                    take_all(act, 0, made, outs, jobs[10:], 10)

                @block.tensor
                def _(pe):
                    made_n = [0]

                    def bank():
                        i = made_n[0]
                        taken(pe, outs, i - 8)
                        return ps[:, i % 8, :]

                    def done(ins):
                        made_n[0] += 1
                        ins.then_inc(made, 1)

                    pe.wait_ge(weights_in, 16 * N_WEIGHTS)
                    for b0, b1 in ((0, 4), (4, 8), (8, 10)):
                        o = bank()
                        for k in range(b0, b1):
                            last = pt.transpose(o[:, (k - b0) * P:(k - b0 + 1) * P], Wraw[:, k, :], ident[:, :])
                        done(last)
                    for i in range(3):
                        taken(pe, outs, i)
                    for c in range(NC7):
                        pe.wait_ge(hn_ready, c + 1)
                        o = bank()
                        for k in range(4 * c, min(4 * c + 4, NT)):
                            last = pt.transpose(o[:, (k - 4 * c) * P:(k - 4 * c + 1) * P], hn[:, k, :], ident[:, :])
                        done(last)
                    pe.wait_ge(ww_ready, 1)
                    for k in range(3, 10):
                        taken(pe, outs, k)
                    for k0, k1 in trios:
                        o = bank()
                        for k in range(k0, k1):
                            last = pt.matmul(o[:, (k - k0) * (D + 2 * H):(k - k0 + 1) * (D + 2 * H)], hT0[:, k * P:(k + 1) * P], WW[:, :],
                                             start=True, stop=True)
                        done(last)
                    for h in range(H):
                        for c in range(NC7):
                            w = min(CW, SP_ - c * CW)
                            done(pt.matmul(bank()[:, 0:w], WAb[:, h, :], hT0[:, c * CW:c * CW + w], start=True, stop=True))
                    pe.wait_ge(tq_ready, 1)
                    for k in range(2):
                        done(pt.matmul(bank()[0:GD, 0:49 * NTYPE], qsum[:, :], Traw[:, 49 * k:49 * k + 49, :].rearrange("p g k -> p (g k)"),
                                       start=True, stop=True))
                    taken(pe, outs, 47)
                    taken(pe, outs, 48)
                    o = bank()
                    for k in range(NTYPE):
                        last = pt.transpose(o[0:NG, k * GD:(k + 1) * GD], T32[:, k, :], ident[0:GD, 0:GD])
                    done(last)

        def phase_attention():
            names = ("block_in0", "block_in1", "mask_ready", "ln_ready", "logs_ready", "max_done", "relu_done", "sum_done", "turned", "scores_done",
                     "exp_done", "used", "sums_out", "back", "sums_in", "cleared", "ident_in", "own_terms")
            (in0, in1, mask_ready, ln_ready, logs_ready, max_done, relu_done, sum_done, turned, scores_done,
             exp_done, used, sums_out, back, sums_in, cleared, ident_in, own_terms) = (sem("a_" + n) for n in names)
            block_in = [in0, in1]
            psT = [psf[:, 2 * CW * i:2 * CW * i + TG * P] for i in range(2)]

            def blocks(eng, body):
                body(0, 0, 0)
                with eng.Fori(0, NT // 2) as m:
                    body(m * 2 + 1, 1, m)
                    body(m * 2 + 2, 0, m + 1)

            with nc.Block() as block:
                @block.sync
                def _(sp):
                    sp.wait_ge(cleared, 1)
                    sp.dma_start(Cb[0][:, 0:S], rows32[0:P, :]).then_inc(block_in[0], 16)
                    sp.dma_start(Cb[1][:, 0:S], rows32[P:2 * P, :]).then_inc(block_in[1], 16)
                    with sp.Fori(0, NT // 2 - 1) as m:
                        for i in range(2):
                            b = m * 2 + 2 + i
                            sp.wait_ge(sum_done, m * 8 + 4 * i + 5)
                            sp.dma_start(Cb[i][:, 0:S], rows32[bass.ds(b * P, P), :]).then_inc(block_in[i], 16)
                    sp.wait_ge(cleared, 2)
                    sp.dma_start(Cb[0][0:STAIL, 0:S], rows32[(NT - 1) * P:S, :]).then_inc(block_in[0], 16)

                @block.gpsimd
                def _(pool):
                    pool.sem_inc(max_done, 2)
                    pool.sem_inc(sum_done, 1)
                    gp.memset(acc, 0.0)
                    for i in range(2):
                        gp.memset(nm[i][:, S:SP_], BIG)
                        last = gp.memset(Cb[i][:, S:SP_], -BIG)
                    last.then_inc(cleared, 1)

                    def body(b, i, turn, last=False):
                        if last:
                            pool.wait_ge(sum_done, 4 * (NT - 2) + 1)
                            pool.wait_ge(logs_ready, NT - 1)
                            gp.memset(Cb[0][STAIL:P, 0:S], 0.0).then_inc(cleared, 1)
                        pool.wait_ge(block_in[i], turn * 16 + 16)
                        width = STAIL if last else P
                        diag = Cb[i][:, bass.ds(b * P, width)]
                        gp.tensor_tensor(diag, diag, ident[:, 0:width], ALU.add).then_inc(ident_in, 1)
                        pool.wait_ge(ident_in, b + 1)
                        gp.tensor_tensor(acc[:, 0:S], acc[:, 0:S], Cb[i][:, 0:S], ALU.add).then_inc(acc_done, 1)
                        pool.wait_ge(ln_ready, b + 1)
                        gp.tensor_tensor(Cb[i][:, 0:S], Cb[i][:, 0:S], nm[i][:, 0:S], ALU.subtract).then_inc(logs_ready, 1)

                    body(0, 0, 0)
                    with pool.Fori(0, NT // 2 - 1) as m:
                        body(m * 2 + 1, 1, m)
                        body(m * 2 + 2, 0, m + 1)
                    body(NT - 2, 1, NT // 2 - 1)
                    body(NT - 1, 0, NT // 2, last=True)

                @block.vector
                def _(dve):
                    for h in range(H):
                        last = v.tensor_scalar(Z[32 * h:32 * h + 32, :], as_bc[32 * h:32 * h + 32, h, :], SLOPE, None, ALU.mult)
                    link(dve, "dve", last)
                    for part in range(3):
                        link(dve, "dve", v.tensor_copy(Zb, Z))
                        if part == 0:
                            link(dve, "dve", v.tensor_scalar(A3, Zb, masks[:, 0:1], None, ALU.mult))
                        else:
                            link(dve, "dve", v.scalar_tensor_tensor(A3, Zb, masks[:, part:part + 1], A3, ALU.mult, ALU.add))
                        if part < 2:
                            link(dve, "dve", v.tensor_tensor(Z, Z, Zb, ALU.subtract))
                    dve.sem_inc(own_terms, 1)
                    dve.wait_ge(cleared, 1)

                    def mask(b, i, turn):
                        dve.wait_ge(ident_in, b + 1)
                        v.tensor_scalar(nm[i][:, 0:S], Cb[i][:, 0:S], 0.0, BIG, ALU.is_equal, ALU.mult).then_inc(mask_ready, 1)

                    def source_max(b, i, h):
                        if h == 0:
                            dve.wait_ge(mask_ready, b + 1)
                            v.memset(neg1[:, 2:3], 0.0)
                        dve.wait_ge(max_done, b * 4 + h + 2)
                        v.memset(neg1[:, 3:4], 0.0)
                        ins = v.tensor_tensor_reduce(out=junk[:, 0:SP_], in0=as_bc[:, h, :], in1=nm[i], scale=1.0, scalar=NEG_HUGE,
                                                     op0=ALU.subtract, op1=ALU.max, accum_out=mx[:, i, 0, h:h + 1])
                        ins.then_inc(max_done, 1)

                    def shifts(b, i):
                        dve.wait_ge(max_done, b * 4 + 6)
                        adv = asd[:, bass.ds(b, 1), H:2 * H].rearrange("p o h -> p (o h)")
                        v.tensor_tensor(mx[:, i, 1, :], mx[:, i, 0, :], adv, ALU.add).then_inc(shift_step, 1)
                        dve.wait_ge(shift_step, b * 2 + 1)
                        v.scalar_tensor_tensor(mx[:, i, 1, :], mx[:, i, 1, :], SLOPE, mx[:, i, 1, :], ALU.mult, ALU.max).then_inc(shift_step, 1)
                        dve.wait_ge(shift_step, b * 2 + 2)
                        v.scalar_tensor_tensor(mx[:, i, 2, :], adv, SLOPE, mx[:, i, 1, :], ALU.mult, ALU.subtract).then_inc(shifted, 1)

                    def body(b, i, turn, last=False):
                        shifts(b, i)
                        for h in range(H):
                            dve.wait_ge(relu_done, b * 4 + h + 1)
                            if h == 0:
                                dve.wait_ge(logs_ready, b + 1)
                                dve.wait_ge(shifted, b + 1)
                            v.scalar_tensor_tensor(u[h % 2], u[h % 2], mx[:, i, 2, h:h + 1], Cb[i], ALU.add, ALU.add).then_inc(sum_done, 1)
                            if h == 1 and not last:
                                mask(b + 1, 1 - i, turn)
                            if h and not last:
                                source_max(b + 1, 1 - i, h - 1)
                        if not last:
                            source_max(b + 1, 1 - i, 3)

                    mask(0, 0, 0)
                    for h in range(H):
                        source_max(0, 0, h)
                    body(0, 0, 0)
                    with dve.Fori(0, NT // 2 - 1) as m:
                        body(m * 2 + 1, 1, m)
                        body(m * 2 + 2, 0, m + 1)
                    body(NT - 2, 1, NT // 2 - 1)
                    body(NT - 1, 0, NT // 2, last=True)

                @block.scalar
                def _(act):
                    act.sem_inc(turned, 2)
                    act.sem_inc(used, 2)
                    a.preload_act_table_set("natural_log_exp_and_others")

                    def logs(b, i, turn):
                        act.wait_ge(mask_ready, b + 1)
                        act.wait_ge(acc_done, b + 1)
                        a.activation(Cb[i][:, 0:S], Cb[i][:, 0:S], ACT.Ln, bias=tiny[:, 0:1]).then_inc(ln_ready, 1)

                    def relu(b, h, half):
                        if half == 0:
                            act.wait_ge(turned, b * 4 + h + 1)
                        sources = slice(half * SP_ // 2, (half + 1) * SP_ // 2)
                        ins = a.activation(u[h % 2][:, sources], as_bc[:, h, sources], ACT.Relu, scale=1.0 - SLOPE,
                                           bias=ad8[:, bass.ds(b * 4 + h, 1)])
                        if half:
                            ins.then_inc(relu_done, 1)

                    def body(b, i, turn, first=False, last=False):
                        for h in range(H):
                            for g in range(5):
                                if g < 2 and h < 3:
                                    relu(b, h + 1, g)
                                elif g < 2 and not last:
                                    relu(b + 1, 0, g)
                                if h == 2 and g == 3 and not last:
                                    logs(b + 1, 1 - i, turn)
                                j = (5 * h + g) % 2
                                act.wait_ge(scores_done, b * 20 + 5 * h + g + 1)
                                act.wait_ge(used, b * 20 + 5 * h + g + 1)
                                a.activation(PT[j][:, :], psT[j], ACT.Exp).then_inc(exp_done, 1)
                            if h == 0 and not first:
                                take_sums(b - 1, 1 - i)
                        if not first:
                            put_back(b - 1, 1 - i)

                    def take_sums(b, i):
                        act.wait_ge(used, b * 20 + 22)
                        a.activation(aggS[i][:, :], ps[0:C + 1, 4 + i, :], ACT.Copy).then_inc(sums_out, 1)

                    def put_back(b, i):
                        act.wait_ge(back, b + 1)
                        a.activation(nb[:, bass.ds(b, 1), :].rearrange("p o n -> p (o n)"), ps[:, 6, 0:H * (C + 1)], ACT.Copy).then_inc(sums_in, 1)

                    logs(0, 0, 0)
                    relu(0, 0, 0)
                    relu(0, 0, 1)
                    body(0, 0, 0, first=True)
                    with act.Fori(0, NT // 2 - 1) as m:
                        body(m * 2 + 1, 1, m)
                        body(m * 2 + 2, 0, m + 1)
                    body(NT - 2, 1, NT // 2 - 1)
                    body(NT - 1, 0, NT // 2, last=True)
                    take_sums(NT - 1, 0)
                    put_back(NT - 1, 0)

                @block.tensor
                def _(pe):
                    pe.sem_inc(exp_done, 2)
                    pe.sem_inc(sums_out, 2)
                    pe.sem_inc(sums_in, 2)
                    pe.wait_ge(own_terms, 1)

                    def scores(b, h, g):
                        j = (5 * h + g) % 2
                        pe.wait_ge(exp_done, b * 20 + 5 * h + g + 1)
                        if g == 0:
                            pe.wait_ge(sum_done, b * 4 + h + 2)
                        for k in range(TG):
                            o = psT[j][:, k * P:(k + 1) * P]
                            s0 = (g * TG + k) * P
                            pt.matmul(o, u[h % 2][:, s0:s0 + P], ident[:, :], is_transpose=True, start=True, stop=False)
                            last = pt.matmul(o, A3[:, s0:s0 + P], head_rows[:, h, :], start=False, stop=True)
                        last.then_inc(scores_done, 1)

                    def weigh(b, i, h, g):
                        j = (5 * h + g) % 2
                        if h == 0 and g == 0:
                            pe.wait_ge(sums_out, b + 1)
                        pe.wait_ge(exp_done, b * 20 + 5 * h + g + 3)
                        for k in range(TG):
                            s = g * TG + k
                            last = pt.matmul(ps[0:C + 1, 4 + i, h * P:(h + 1) * P], haug[:, s, h, :], PT[j][:, k * P:(k + 1) * P],
                                             start=s == 0, stop=s == NT - 1)
                        last.then_inc(used, 1)

                    def turn_back(b, i):
                        pe.wait_ge(sums_out, b + 3)
                        pe.wait_ge(sums_in, b + 2)
                        pt.matmul(ps[0:1, 7, 0:1], onesb[:, 0:1], onesb[:, 0:1], start=True, stop=True)
                        for h in range(H):
                            last = pt.transpose(ps[:, 6, h * (C + 1):(h + 1) * (C + 1)], aggS[i][:, h * P:(h + 1) * P],
                                                ident[0:C + 1, 0:C + 1])
                        last.then_inc(back, 1)

                    def body(b, i, turn, first=False):
                        for h in range(H):
                            for g in range(5):
                                scores(b, h, g)
                                if h or g:
                                    weigh(b, i, (5 * h + g - 1) // 5, (g - 1) % 5)
                                elif not first:
                                    weigh(b - 1, 1 - i, 3, 4)
                            pt.matmul(ps[0:1, 7, 0:1], onesb[:, 0:1], onesb[:, 0:1], start=True, stop=True, skip_group_check=True).then_inc(turned, 1)
                            if h == 2 and not first:
                                turn_back(b - 1, 1 - i)

                    body(0, 0, 0, first=True)
                    with pe.Fori(0, NT // 2) as m:
                        body(m * 2 + 1, 1, m)
                        body(m * 2 + 2, 0, m + 1)
                    weigh(NT - 1, 0, 3, 4)
                    turn_back(NT - 1, 0)

        def each(n, w=CW):
            return [(c, c * w, min(w, n - c * w)) for c in range(-(-n // w))]

        def bc_vec(k, n=NT):
            return vec[:, k:k + 1, :].to_broadcast([P, n, D])

        HEAD = 4

        def split(dve):
            for k0, k1 in ((0, HEAD), (HEAD, NT)):
                link(dve, "dve", v.tensor_copy(G[:, k0:k1, 0, :], hn[:, k0:k1, :]))
                link(dve, "dve", v.tensor_tensor(rest[:, k0:k1, :], hn[:, k0:k1, :], G[:, k0:k1, 0, :], ALU.subtract))
                link(dve, "dve", v.tensor_copy(G[:, k0:k1, 1, :], rest[:, k0:k1, :]))
                v.tensor_tensor(G[:, k0:k1, 2, :], rest[:, k0:k1, :], G[:, k0:k1, 1, :], ALU.subtract).then_inc(split_done, 1)

        USES = [7, 6, 6, 6]

        def stream_counts(sp, k, rows, residues):
            def load(t_, i, m, n_rows=P):
                use = m + k * USES[i]
                if not (k == 0 and isinstance(m, int) and m == 0):
                    sp.wait_ge(ring_used[i], use)
                sp.dma_start(ring[i][0:n_rows, :], rows[bass.ds(t_ * P, n_rows), :]).then_inc(ring_in[i], 16)

            for i in range(4):
                load(i, i, 0)
            with sp.Fori(1, 6) as m:
                for i in range(4):
                    load(m * 4 + i, i, m)
            load(NT - 1, 0, 6, STAIL)
            with sp.If(large_counts(sp) > 0):
                summed(sp, k)
                for t_ in range(NT):
                    n_rows = STAIL if t_ == NT - 1 else P
                    if t_:
                        sp.wait_ge(res_used, k * NT + t_)
                    sp.dma_start(ring[1][0:n_rows, :], residues[t_ * P:t_ * P + n_rows, :]).then_inc(res_in, 16)
                sp.wait_ge(res_used, (k + 1) * NT)

        def sum_edges(pe, k, self_loops=False):
            def tile(t_, i, m, first=False, last=False):
                rows = STAIL if last else P
                use = m + k * USES[i]
                pe.wait_ge(ring_in[i], use * 16 + 16)

                def part_of(part):
                    return G[0:rows, NT - 1, part, :] if last else G[:, bass.ds(t_, 1), part, :].rearrange("p o d -> p (o d)")

                def own():
                    for part in range(3):
                        ins = pt.matmul(psf[:, bass.ds(t_ * P, rows)], part_of(part), identb[0:rows, 0:rows], start=False, stop=False)
                    return ins

                if self_loops and last:
                    own()
                for part in range(3):
                    for c, c0, cw in each(S):
                        ins = pt.matmul(ps[:, c, 0:cw], part_of(part), ring[i][0:rows, c0:c0 + cw], start=first and part == 0,
                                        stop=last and part == 2)
                if self_loops and not last:
                    ins = own()
                ins.then_inc(ring_used[i], 1)

            pe.wait_ge(split_done, 2 * k + 1)
            for i in range(HEAD):
                tile(i, i, 0, first=i == 0)
            pe.wait_ge(split_done, 2 * k + 2)
            with pe.Fori(1, 6) as m:
                for i in range(4):
                    tile(m * 4 + i, i, m)
            tile(NT - 1, 0, 6, last=True)
            with pe.If(large_counts(pe) > 0):
                for t_ in range(NT):
                    rows = STAIL if t_ == NT - 1 else P
                    pe.wait_ge(res_in, (k * NT + t_ + 1) * 16)
                    for part in range(3):
                        for c, c0, cw in each(S):
                            ins = pt.matmul(ps[:, c, 0:cw], G[0:rows, t_, part, :], ring[1][0:rows, c0:c0 + cw], start=False, stop=True,
                                            skip_group_check=True)
                    ins.then_inc(res_used, 1)
            pt.matmul(ps[0:1, 7, 0:1], onesb[:, 0:1], onesb[:, 0:1], start=True, stop=True).then_inc(sums_done, 1)

        def summed(eng, k):
            eng.wait_ge(ring_used[0], 7 * (k + 1))

        def all_summed(eng, k):
            eng.wait_ge(sums_done, k + 1)

        def large_counts(eng):
            return eng.value_load(flag_i[0:1, 0:1], min_val=0, max_val=1)

        def phase_attention_end():
            x_in, zeroed, root_in, root_out, flag_made, ovf_summed = (sem("t_" + n) for n in ("x_in", "zeroed", "root_in", "root_out", "flag", "ovf_summed"))
            with nc.Block() as block:
                @block.sync
                def _(sp):
                    load_x(sp, zeroed, x_in)
                    sp.dma_start(TT[:, 0:S], types_d).then_inc(tt_in, 16)

                @block.gpsimd
                def _(pool):
                    gp.memset(x[:, NT - 1, :], 0.0).then_inc(zeroed, 1)
                    gp.memset(TT[:, S:SP_], 0.0)
                    for k in range(2):
                        pool.wait_ge(root_in, k + 1)
                        gp.tensor_tensor(rstd[:, :], rstd[:, :], mhalf[:, :], ALU.pow).then_inc(root_out, 1)

                @block.tensor
                def _(pe):
                    pe.wait_ge(ovf_summed, 1)
                    pt.matmul(ps[0:1, 2, 0:1], flag_f[:, 0:1], ones[:, 0:1], start=True, stop=True).then_inc(flag_made, 1)

                @block.vector
                def _(dve):
                    v.tensor_reduce(flag_f[:, 0:1], ovf[:, :], AX.X, ALU.add).then_inc(ovf_summed, 1)
                    att = nb[:, :, :].rearrange("p t (h c) -> p t h c", h=H)
                    link(dve, "dve", v.tensor_scalar(rden[:, :, :], att[:, :, :, C], 1e-16, None, ALU.add))
                    link(dve, "dve", v.reciprocal(rden[:, :, :], rden[:, :, :]))
                    for h in range(H):
                        last = v.tensor_tensor(att_o[:, :, h * C:(h + 1) * C], att[:, :, h, 0:C],
                                               rden[:, :, h:h + 1].to_broadcast([P, NT, C]), ALU.mult)
                    link(dve, "dve", last)
                    link(dve, "dve", v.tensor_tensor(att_o, att_o, bc_vec(0), ALU.add))
                    layer_stats(dve, att_o, root_in, root_out, 1)
                    link(dve, "dve", v.tensor_tensor(att_o, att_o, over_features(mv[:, :, 0]), ALU.subtract))
                    link(dve, "dve", v.tensor_tensor(att_o, att_o, over_features(rstd[:, :]), ALU.mult))
                    link(dve, "dve", v.tensor_tensor(att_o, att_o, bc_vec(1), ALU.mult))
                    link(dve, "dve", v.tensor_tensor(att_o, att_o, bc_vec(2), ALU.add))
                    dve.wait_ge(x_in, 32)
                    link(dve, "dve", v.scalar_tensor_tensor(x, att_o, 0.0, x, ALU.max, ALU.add))
                    layer_stats(dve, x, root_in, root_out, 2)
                    dve.wait_ge(flag_made, 1)
                    v.tensor_scalar(flag_i[:, :], ps[0:1, 2, 0:1], 0.0, None, ALU.is_gt)

        def phase_residue():
            names = ("rows_in", "left", "stored", "turned", "taken")
            rows_in, left, stored, turned, took = (sem("r_" + n) for n in names)
            W = 64
            NB = S // W
            BANKS = [(0, 16), (16, 32), (32, 48), (48, 49)]
            exact = FA[0:W, 0:S]
            rounded = FB[0:W, :].bitcast(BF16)[:, 0:S]
            left_t = FC[0:W, :].bitcast(BF16)[:, 0:S].rearrange("p (t d) -> p t d", d=W)
            with nc.Block() as block:
                @block.scalar
                def _(act):
                    with act.If(large_counts(act) > 0):
                        act.sem_inc(stored, 32)
                        with act.Fori(0, NB) as b:
                            rows = bass.ds(act.snap(b * W), W)
                            act.wait_ge(stored, b * 32 + 32)
                            act.dma_start(exact, rows32[rows, :]).then_inc(rows_in, 16)
                            act.dma_start(rounded, rows16[rows, :]).then_inc(rows_in, 16)
                            act.wait_ge(left, b + 1)
                            act.dma_start(residue[rows, :], rounded).then_inc(stored, 16)
                            act.wait_ge(took, b * 4 + 4)
                            act.dma_start(residue_turned[:, rows].rearrange("(t p) d -> p t d", p=W), left_t).then_inc(stored, 16)
                        act.wait_ge(stored, 32 * (NB + 1))

                @block.vector
                def _(dve):
                    with dve.If(large_counts(dve) > 0):
                        with dve.Fori(0, NB) as b:
                            dve.wait_ge(rows_in, b * 32 + 32)
                            v.tensor_tensor(rounded, exact, rounded, ALU.subtract).then_inc(left, 1)
                            for g, (t0, t1) in enumerate(BANKS):
                                dve.wait_ge(turned, b * 4 + g + 1)
                                v.tensor_copy(left_t[:, t0:t1, :], ps[0:W, g, :].bitcast(BF16)[:, 0:(t1 - t0) * W].rearrange("p (t d) -> p t d", d=W)).then_inc(took, 1)

                @block.tensor
                def _(pe):
                    with pe.If(large_counts(pe) > 0):
                        with pe.Fori(0, NB) as b:
                            pe.wait_ge(left, b + 1)
                            pt.matmul(ps[0:1, 7, 0:1], onesb[:, 0:1], onesb[:, 0:1], start=True, stop=True)
                            for g, (t0, t1) in enumerate(BANKS):
                                for k in range(t0, t1):
                                    last = pt.transpose(ps[0:W, g, :].bitcast(BF16)[:, (k - t0) * W:(k - t0 + 1) * W], rounded[:, k * W:(k + 1) * W],
                                                        identb[0:W, 0:W])
                                last.then_inc(turned, 1)

        def phase_gated():
            names = ("h_by_f", "h_out", "sum_out_act", "sum_out_dve", "msg", "msg_out", "gates", "rz", "pre", "cand", "new", "back", "added", "root_in", "root_out", "zero", "deg", "deg_out", "diag")
            (h_by_f, h_out, sum_act, sum_dve, msg, msg_out, gates, rz, pre, cand, new, back, added, root_in, root_out, zero, deg, deg_out, diag_ready) = (sem("g_" + n) for n in names)
            normed_x, dst_deg, src_deg, dinv_in, dinv_out = (sem("g_" + n) for n in ("normed_x", "dst_deg", "src_deg", "dinv_in", "dinv_out"))
            with nc.Block() as block:
                @block.sync
                def _(sp):
                    stream_counts(sp, 0, turned16, residue_turned)

                @block.gpsimd
                def _(pool):
                    pool.wait_ge(dinv_in, 1)
                    gp.tensor_tensor(dinv[:, :], dinv[:, :], mhalf[:, :], ALU.pow).then_inc(dinv_out, 1)
                    pool.wait_ge(deg, 7)
                    gp.memset(FB[:, S:SP_], 0.0).then_inc(zero, 1)
                    pool.wait_ge(root_in, 1)
                    gp.tensor_tensor(rstd[:, :], rstd[:, :], mhalf[:, :], ALU.pow).then_inc(root_out, 1)

                @block.tensor
                def _(pe):
                    pe.wait_ge(tt_in, 16)
                    for k in range(NT):
                        last = pt.matmul(ps[:, 7, k:k + 1], TT[:, k * P:(k + 1) * P], ones[0:NTYPE, 0:1], start=True, stop=True)
                    last.then_inc(dst_deg, 1)
                    for c, c0, cw in each(SP_):
                        pe.wait_ge(normed_x, c + 1)
                        for k in range(cw // P):
                            last = pt.transpose(ps[:, c, k * P:(k + 1) * P], hn[:, 4 * c + k, :], ident[:, :])
                        last.then_inc(h_by_f, 1)
                    pe.wait_ge(diag_ready, 1)
                    for c, c0, cw in each(SP_):
                        pe.wait_ge(h_out, c + 1)
                        pt.matmul(ps[:, c, 0:cw], ones[:, :], FB[:, c0:c0 + cw], start=True, stop=True).then_inc(deg, 1)
                    pe.wait_ge(deg_out, 7)
                    sum_edges(pe, 0)
                    pe.wait_ge(sum_act, 4)
                    pe.wait_ge(sum_dve, 3)
                    for c, c0, cw in each(S):
                        pt.matmul(ps[:, c, 0:cw], WT[:, 0, :], FB[:, c0:c0 + cw], start=True, stop=False)
                        pt.matmul(ps[:, c, 0:cw], embx[:, :], TT[:, c0:c0 + cw], start=False, stop=True).then_inc(msg, 1)
                    pe.wait_ge(msg_out, 7)
                    def gate(c, c0, cw):
                        if c >= 2:
                            pe.wait_ge(added, c - 1)
                        b0 = 4 * (c % 2)
                        m_, h_ = FC[:, c0:c0 + cw], FA[:, c0:c0 + cw]
                        for k in range(2):
                            pt.matmul(ps[:, b0 + k, 0:cw], WT[:, 1 + k, :], m_, start=True, stop=False)
                            pt.matmul(ps[:, b0 + k, 0:cw], WT[:, 4 + k, :], h_, start=False, stop=True)
                        pt.matmul(ps[:, b0 + 2, 0:cw], WT[:, 3, :], m_, start=True, stop=True)
                        pt.matmul(ps[:, b0 + 3, 0:cw], WT[:, 6, :], h_, start=True, stop=True).then_inc(gates, 1)

                    def by_node(c, c0, cw):
                        pe.wait_ge(new, c + 1)
                        for k in range(-(-cw // P)):
                            last = pt.transpose(ps[:, 4 * (c % 2), k * P:(k + 1) * P], FB[:, c0 + k * P:c0 + (k + 1) * P], ident[:, :])
                        last.then_inc(back, 1)

                    pe.wait_ge(zero, 1)
                    for c, c0, cw in each(S):
                        gate(c, c0, cw)
                        if c:
                            by_node(*each(S)[c - 1])
                    by_node(*each(S)[6])
                    pe.wait_ge(added, 6)
                    for k in range(NT):
                        last = pt.matmul(ps[:, 7, k:k + 1], acc[:, k * P:(k + 1) * P], ones[:, 0:1], start=True, stop=True)
                    last.then_inc(src_deg, 1)

                @block.scalar
                def _(act):
                    for c, c0, cw in each(SP_):
                        act.wait_ge(h_by_f, c + 1)
                        a.activation(FA[:, c0:c0 + cw], ps[:, c, 0:cw], ACT.Copy).then_inc(h_out, 1)
                    for c, c0, cw in each(SP_):
                        act.wait_ge(deg, c + 1)
                        a.activation(DB[:, c0:c0 + cw], ps[:, c, 0:cw], ACT.Copy).then_inc(deg_out, 1)
                    all_summed(act, 0)
                    for c, c0, cw in each(S)[0::2]:
                        a.activation(FB[:, c0:c0 + cw], ps[:, c, 0:cw], ACT.Copy).then_inc(sum_act, 1)
                    for c, c0, cw in each(S):
                        act.wait_ge(msg, c + 1)
                        a.activation(FC[:, c0:c0 + cw], ps[:, c, 0:cw], ACT.Copy).then_inc(msg_out, 1)
                    for c, c0, cw in each(S):
                        act.wait_ge(gates, c + 1)
                        if c:
                            act.wait_ge(new, c)
                        b0 = 4 * (c % 2)
                        a.activation(gr[:, 0:cw], ps[:, b0, 0:cw], ACT.Sigmoid, bias=col[:, 12:13])
                        a.activation(gz[:, 0:cw], ps[:, b0 + 1, 0:cw], ACT.Sigmoid, bias=col[:, 13:14]).then_inc(rz, 1)
                        act.wait_ge(pre, c + 1)
                        a.activation(gn[:, 0:cw], gn[:, 0:cw], ACT.Tanh, bias=col[:, 2:3]).then_inc(cand, 1)

                @block.vector
                def _(dve):
                    dve.wait_ge(dst_deg, 1)
                    v.tensor_scalar(dinv[:, :], ps[:, 7, 0:NT], 1.0, None, ALU.add).then_inc(dinv_in, 1)
                    norm_relu(dve, normed_x)
                    dve.wait_ge(dinv_out, 1)
                    link(dve, "dve", v.tensor_tensor(col[:, 12:14], col[:, 0:2], col[:, 3:5], ALU.add))
                    v.tensor_tensor(FB.rearrange("p (t d) -> p t d", d=P), ident[:, :].unsqueeze(1).to_broadcast([P, NT, P]),
                                    dinv[:, :].unsqueeze(2).to_broadcast([P, NT, P]), ALU.mult).then_inc(diag_ready, 1)
                    split(dve)
                    all_summed(dve, 0)
                    for c, c0, cw in each(S)[1::2]:
                        v.tensor_copy(FB[:, c0:c0 + cw], ps[:, c, 0:cw]).then_inc(sum_dve, 1)
                    for c, c0, cw in each(S):
                        b0 = 4 * (c % 2)
                        dve.wait_ge(rz, c + 1)
                        link(dve, "dve", v.scalar_tensor_tensor(gn[:, 0:cw], ps[:, b0 + 3, 0:cw], col[:, 5:6], gr[:, 0:cw], ALU.add, ALU.mult))
                        v.tensor_tensor(gn[:, 0:cw], gn[:, 0:cw], ps[:, b0 + 2, 0:cw], ALU.add).then_inc(pre, 1)
                        dve.wait_ge(cand, c + 1)
                        link(dve, "dve", v.tensor_tensor(gr[:, 0:cw], FA[:, c0:c0 + cw], gn[:, 0:cw], ALU.subtract))
                        link(dve, "dve", v.tensor_tensor(gr[:, 0:cw], gr[:, 0:cw], gz[:, 0:cw], ALU.mult))
                        v.tensor_tensor(FB[:, c0:c0 + cw], gr[:, 0:cw], gn[:, 0:cw], ALU.add).then_inc(new, 1)
                        dve.wait_ge(back, c + 1)
                        xs = x[:, 4 * c:4 * c + -(-cw // P), :].rearrange("p t d -> p (t d)")
                        n_ = -(-cw // P) * P
                        v.tensor_tensor(xs, xs, ps[:, b0, 0:n_], ALU.add).then_inc(added, 1)
                        if c:
                            tile_stats(dve, added, c - 1)
                    tile_stats(dve, added, 6)
                    layer_stats(dve, x, root_in, root_out, 1, counted=True)
                    dve.wait_ge(src_deg, 1)
                    link(dve, "dve", v.tensor_scalar(rdeg[:, :], ps[:, 7, 0:NT], -1.0, 1.0, ALU.add, ALU.max))
                    v.reciprocal(rdeg[:, :], rdeg[:, :])

        def phase_conv():
            names = ("h_by_f", "h_out", "mlp", "mlp_out", "bn_in", "bn_out", "normed", "conv", "scaled", "sum_out", "biased", "back", "added", "root_in", "root_out", "shifted")
            (h_by_f, h_out, mlp, mlp_out, bn_in, bn_out, normed, conv, scaled, sum_out, biased, back, added, root_in, root_out, shifted) = (sem("c_" + n) for n in names)

            def batch_norm(dve, n, g, b, made=None):
                for c, c0, cw in each(N):
                    if made is not None:
                        dve.wait_ge(made, c + 1)
                    v.bn_stats(bn6[:, c, :], FB[:, c0:c0 + cw])
                link(dve, "dve", v.memset(neg1[:, 3:4], 0.0))
                link(dve, "dve", v.bn_aggr(mv[:, 0, :], bn6[:, 0:7, :].rearrange("p c k -> p (c k)")))
                v.tensor_scalar(col[:, 18:19], mv[:, 0, 1:2], EPS, None, ALU.add).then_inc(bn_in, 1)
                dve.wait_ge(bn_out, n)
                link(dve, "dve", v.tensor_tensor(col[:, 20:21], col[:, 18:19], col[:, g:g + 1], ALU.mult))
                link(dve, "dve", v.tensor_tensor(col[:, 19:20], col[:, 20:21], mv[:, 0, 0:1], ALU.mult))
                v.tensor_tensor(col[:, 21:22], col[:, b:b + 1], col[:, 19:20], ALU.subtract).then_inc(shifted, 1)

            normed_x = sem("c_normed_x")
            with nc.Block() as block:
                @block.sync
                def _(sp):
                    stream_counts(sp, 1, turned16, residue_turned)

                @block.gpsimd
                def _(pool):
                    for k in range(2):
                        pool.wait_ge(bn_in, k + 1)
                        gp.tensor_tensor(col[:, 18:19], col[:, 18:19], mhalf[:, 0:1], ALU.pow).then_inc(bn_out, 1)
                    pool.wait_ge(root_in, 1)
                    gp.tensor_tensor(rstd[:, :], rstd[:, :], mhalf[:, :], ALU.pow).then_inc(root_out, 1)

                @block.tensor
                def _(pe):
                    for c, c0, cw in each(SP_):
                        pe.wait_ge(normed_x, c + 1)
                        for k in range(cw // P):
                            last = pt.transpose(ps[:, c, k * P:(k + 1) * P], hn[:, 4 * c + k, :], ident[:, :])
                        last.then_inc(h_by_f, 1)
                    for c, c0, cw in each(SP_):
                        pe.wait_ge(h_out, c + 1)
                        pt.matmul(ps[:, c, 0:cw], WT[:, 10, :], FA[:, c0:c0 + cw], start=True, stop=True).then_inc(mlp, 1)
                    for c, c0, cw in each(SP_):
                        pe.wait_ge(normed, c + 1)
                        for k in range(cw // P):
                            last = pt.matmul(ps[:, c, k * P:(k + 1) * P], FA[:, c0 + k * P:c0 + (k + 1) * P], WT[:, 11, :], start=True, stop=True)
                        last.then_inc(conv, 1)
                    pe.wait_ge(scaled, 7)
                    sum_edges(pe, 1, self_loops=True)
                    for c, c0, cw in each(SP_):
                        pe.wait_ge(normed, 7 + c + 1)
                        for k in range(cw // P):
                            last = pt.transpose(ps[:, c, k * P:(k + 1) * P], FA[:, c0 + k * P:c0 + (k + 1) * P], ident[:, :])
                        last.then_inc(back, 1)

                @block.scalar
                def _(act):
                    for c, c0, cw in each(SP_):
                        act.wait_ge(h_by_f, c + 1)
                        a.activation(FA[:, c0:c0 + cw], ps[:, c, 0:cw], ACT.Copy).then_inc(h_out, 1)
                    for c, c0, cw in each(SP_):
                        act.wait_ge(mlp, c + 1)
                        a.activation(FB[:, c0:c0 + cw], ps[:, c, 0:cw], ACT.Identity, bias=col[:, 6:7]).then_inc(mlp_out, 1)
                    act.wait_ge(mlp_out, 7)
                    act.wait_ge(shifted, 1)
                    for c, c0, cw in each(SP_):
                        a.activation(FA[:, c0:c0 + cw], FB[:, c0:c0 + cw], ACT.Relu, scale=col[:, 20:21], bias=col[:, 21:22]).then_inc(normed, 1)
                    for c, c0, cw in each(S):
                        act.wait_ge(sum_out, c + 1)
                        a.activation(FB[:, c0:c0 + cw], FB[:, c0:c0 + cw], ACT.Identity, bias=col[:, 9:10]).then_inc(biased, 1)
                    act.wait_ge(biased, 7)
                    act.wait_ge(shifted, 2)
                    for c, c0, cw in each(SP_):
                        a.activation(FA[:, c0:c0 + cw], FB[:, c0:c0 + cw], ACT.Relu, scale=col[:, 20:21], bias=col[:, 21:22]).then_inc(normed, 1)

                @block.vector
                def _(dve):
                    norm_relu(dve, normed_x)
                    dve.wait_ge(mlp_out, 7)
                    batch_norm(dve, 1, 7, 8)
                    for c, c0, cw in each(SP_):
                        k0, n_ = 4 * c, cw // P
                        dve.wait_ge(conv, c + 1)
                        v.tensor_tensor(hn[:, k0:k0 + n_, :], ps[:, c, 0:cw].rearrange("p (t d) -> p t d", d=D),
                                        dinv[:, k0:k0 + n_].unsqueeze(2).to_broadcast([P, n_, D]), ALU.mult).then_inc(scaled, 1)
                    dve.wait_ge(scaled, 7)
                    split(dve)
                    all_summed(dve, 1)
                    for c, c0, cw in each(S):
                        v.tensor_tensor(FB[:, c0:c0 + cw], ps[:, c, 0:cw], DB[:, c0:c0 + cw], ALU.mult).then_inc(sum_out, 1)
                    batch_norm(dve, 2, 10, 11, biased)
                    for c, c0, cw in each(SP_):
                        dve.wait_ge(back, c + 1)
                        xs = x[:, 4 * c:4 * c + cw // P, :].rearrange("p t d -> p (t d)")
                        v.tensor_tensor(xs, xs, ps[:, c, 0:cw], ALU.add).then_inc(added, 1)
                        if c:
                            tile_stats(dve, added, c - 1)
                    tile_stats(dve, added, 6)
                    layer_stats(dve, x, root_in, root_out, 1, counted=True)

        def phase_mean():
            names = ("h_by_f", "h_out", "lin", "lin_out", "sum_out_act", "sum_out_dve", "out_ready", "out_st")
            h_by_f, h_out, lin, lin_out, sum_act, sum_dve, out_ready, out_st = (sem("m_" + n) for n in names)
            normed_x = sem("m_normed_x")
            with nc.Block() as block:
                @block.sync
                def _(sp):
                    stream_counts(sp, 2, rows16, residue)
                    stream_counts(sp, 3, rows16, residue)
                    sp.wait_ge(out_ready, 1)
                    sp.dma_start(out[0:(NT - 1) * P, :].rearrange("(t p) d -> p t d", p=P), hn[:, 0:NT - 1, :]).then_inc(out_st, 16)
                    sp.dma_start(out[(NT - 1) * P:N, :], hn[0:TAIL, NT - 1, :]).then_inc(out_st, 16)
                    sp.wait_ge(out_st, 32)

                @block.tensor
                def _(pe):
                    for c, c0, cw in each(SP_):
                        pe.wait_ge(normed_x, c + 1)
                        for k in range(cw // P):
                            last = pt.transpose(ps[:, c, k * P:(k + 1) * P], hn[:, 4 * c + k, :], ident[:, :])
                        last.then_inc(h_by_f, 1)

                    def linear(src, w):
                        for c, c0, cw in each(SP_):
                            for k in range(cw // P):
                                last = pt.matmul(ps[:, c, k * P:(k + 1) * P], src[:, c0 + k * P:c0 + (k + 1) * P], WT[:, w, :], start=True, stop=True)
                            last.then_inc(lin, 1)

                    pe.wait_ge(h_out, 7)
                    linear(FA, 7)
                    for k in range(2):
                        pe.wait_ge(lin_out, 7 * (k + 1))
                        sum_edges(pe, 2 + k)
                        pe.wait_ge(sum_act, 4 * (k + 1))
                        pe.wait_ge(sum_dve, 3 * (k + 1))
                        linear(FB, 8 + k)

                @block.scalar
                def _(act):
                    for c, c0, cw in each(SP_):
                        act.wait_ge(h_by_f, c + 1)
                        a.activation(FA[:, c0:c0 + cw], ps[:, c, 0:cw], ACT.Copy).then_inc(h_out, 1)
                    for k in range(2):
                        all_summed(act, 2 + k)
                        for c, c0, cw in each(S)[0::2]:
                            a.activation(FB[:, c0:c0 + cw], ps[:, c, 0:cw], ACT.Relu).then_inc(sum_act, 1)

                @block.vector
                def _(dve):
                    norm_relu(dve, normed_x)
                    for k in range(3):
                        for c, c0, cw in each(SP_):
                            k0, n_ = 4 * c, cw // P
                            o, src = hn[:, k0:k0 + n_, :], ps[:, c, 0:cw].rearrange("p (t d) -> p t d", d=D)
                            dve.wait_ge(lin, 7 * k + c + 1)
                            if k == 0:
                                v.tensor_tensor(o, src, bc_vec(3, n_), ALU.add).then_inc(lin_out, 1)
                            else:
                                v.tensor_tensor(o, src, rdeg[:, k0:k0 + n_].unsqueeze(2).to_broadcast([P, n_, D]), ALU.mult).then_inc(lin_out, 1)
                        dve.wait_ge(lin_out, 7 * (k + 1))
                        if k:
                            link(dve, "dve", v.tensor_tensor(hn, hn, bc_vec(3 + k), ALU.add))
                        if k == 2:
                            v.tensor_tensor(hn, hn, x, ALU.add).then_inc(out_ready, 1)
                            break
                        split(dve)
                        all_summed(dve, 2 + k)
                        for c, c0, cw in each(S)[1::2]:
                            v.tensor_scalar(FB[:, c0:c0 + cw], ps[:, c, 0:cw], 0.0, None, ALU.max).then_inc(sum_dve, 1)

        acc_done, shift_step, shifted = sem("a_acc_done"), sem("a_shift_step"), sem("a_shifted")
        tt_in = sem("types_in")
        split_done, sums_done, res_in, res_used = sem("split_done"), sem("sums_done"), sem("residue_in"), sem("residue_used")
        ring_in = [sem(f"ring_in{i}") for i in range(4)]
        ring_used = [sem(f"ring_used{i}") for i in range(4)]
        phase_counts()
        phase_nodes()
        phase_attention()
        phase_attention_end()
        phase_residue()
        phase_gated()
        phase_conv()
        phase_mean()


_IN = ["x", "src", "dst", "edge_type_9", "L0_gnn_W", "L0_gnn_a_src", "L0_gnn_a_dst", "L0_gnn_bias", "L0_gnn_gamma", "L0_gnn_beta",
       "L1_gnn_W_msg", "L1_gnn_b_msg", "L1_gnn_edge_embed", "L1_gnn_W_ih", "L1_gnn_W_hh", "L1_gnn_b_ih", "L1_gnn_b_hh",
       "L2_gnn_W_mlp", "L2_gnn_b_mlp", "L2_gnn_gamma1", "L2_gnn_beta1", "L2_gnn_W_conv", "L2_gnn_b_conv", "L2_gnn_gamma2", "L2_gnn_beta2",
       "L3_gnn_W1", "L3_gnn_b1", "L3_gnn_W2", "L3_gnn_b2", "L3_gnn_W3", "L3_gnn_b3"]
DBG = False


def kernel(**inputs):
    import concourse.bacc as _bacc
    from concourse.bass_utils import run_bass_kernel_spmd as _run
    nc = _bacc.Bacc("TRN2", target_bir_lowering=False, num_devices=1)
    arrays, aps = {}, {}
    for name in _IN:
        a = np.ascontiguousarray(inputs[name])
        arrays[f"in_{name}"] = a
        aps[name] = nc.dram_tensor(f"in_{name}", a.shape, mybir.dt.from_np(a.dtype), kind="ExternalInput").ap()
    out = nc.dram_tensor("out_x", (N, D), F32, kind="ExternalOutput").ap()
    gnn_program(nc, aps, out, DBG)
    r = _run(nc, [arrays], core_ids=[0])
    return r.results[0]["out_x"]
```

```python
import numpy as np
import concourse.bass as bass
from concourse import mybir
from contextlib import ExitStack

F32 = mybir.dt.float32
BF16 = mybir.dt.bfloat16
I32 = mybir.dt.int32
I16 = mybir.dt.int16
ALU = mybir.AluOpType
ACT = mybir.ActivationFunctionType
AX = mybir.AxisListType

P = 128
N, D, E = 3125, 128, 103125
H, C = 4, 32
NTYPE = 9
ET = 125
NE = E // ET
EP, EJ = 75, 11
Q = 4
R = 784
S = Q * R
GD = P // Q
NG = S // GD
U = 3
PADE = 4
TB, TK = 112, 7
HALF = 7
NT = -(-N // P)
SPAD = NT * P
TAIL = N - (NT - 1) * P
STAIL = S - (NT - 1) * P
CW = 512
NCHUNK = -(-S // CW)
TG = 5
EPS = 1e-5
BIG = 1e30
TINY = 2.0 ** -60
SLOPE = 0.2
BF16_MAX_COUNT = 256.0
NEG_HUGE = -3.0e38


def gnn_program(nc, t, out):
    ctx = ExitStack()
    with ctx:
        def sb(name, shape, dt):
            return ctx.enter_context(nc.sbuf_tensor(name, shape, dt))

        def sem(name):
            return ctx.enter_context(nc.semaphore(name))

        def dram(name, shape, dt):
            return nc.dram_tensor(name, shape, dt, kind="Internal").ap()

        count32 = dram("count32", (NG * P, R), F32)
        count16 = dram("count16", (NG * P, R), BF16)
        turned16 = dram("turned16", (S, S), BF16)
        residue = dram("residue", (S, S), BF16)
        residue_turned = dram("residue_turned", (S, S), BF16)
        bounds_d = dram("bounds_d", (2, NE), F32)
        win_d = dram("win_d", (NG, 2), I32)
        types_d = dram("types_d", (NTYPE, S), F32)
        rows32 = count32.rearrange("(d q) r -> d (q r)", q=Q)
        rows16 = count16.rearrange("(d q) r -> d (q r)", q=Q)

        AW = 38400
        arena = sb("arena", [P, AW], F32)

        def ar(a, shape, dt=F32, parts=P, pb=0):
            n = int(np.prod(shape)) * mybir.dt.size(dt)
            assert n % 4 == 0 and a + n // 4 <= AW, (a, shape)
            v = arena[pb:pb + parts, a:a + n // 4]
            if dt != F32:
                v = v.bitcast(dt)
            if len(shape) == 2:
                v = v.rearrange("p (a b) -> p a b", b=shape[1])
            if len(shape) == 3:
                v = v.rearrange("p (a b c) -> p a b c", b=shape[1], c=shape[2])
            return v

        e_int = ar(12800, [3, EJ * ET], I32, EP)
        e_f = ar(16928, [3, EJ * ET], F32, EP)
        e_t = ar(21056, [EJ * ET], F32, EP)
        e_key = ar(22432, [EJ * ET], F32, EP)
        key = ar(23808, [NE + PADE], F32, ET)
        rem = ar(24640, [NE + PADE], F32, ET)
        typ = ar(25472, [NE + PADE], F32, ET)
        Y = ar(26304, [NE + PADE + 1, NTYPE + 1], BF16, ET)
        A = [ar(30460 + 64 * i, [P], BF16, ET) for i in range(U)]
        B = [ar(30972 + 392 * i, [R], BF16, ET) for i in range(U)]
        stage32 = [ar(34108 + 784 * i, [R]) for i in range(2)]
        stage16 = [ar(35676 + 392 * i, [R], BF16) for i in range(2)]
        ovf_junk = [ar(36460 + 392 * i, [R], BF16) for i in range(2)]
        turned_st = ar(12800, [Q * TK, 2 * HALF * GD], BF16, TB)
        tb = ar(0, [2, NE + 1], F32, NG)
        covers = ar(1700, [NE + 1], F32, NG)
        iota_t = ar(2600, [NE + 1], F32, NG)
        iota_i = ar(3500, [NE + 1], I32, NG)
        iota_keys = ar(5500, [NG * P], I16, ET)
        iotaR = ar(4600, [R], I16, ET)
        T32 = ar(32000, [NTYPE, NG], F32, GD)
        T98 = ar(33000, [NTYPE, GD], F32, NG)
        WAb = ar(19200, [H, P])
        as_bc = ar(0, [H, SPAD])
        Cb = [ar(12800 + 3200 * i, [SPAD]) for i in range(2)]
        nm = [ar(22400 + 1600 * i, [SPAD], BF16) for i in range(2)]
        u = [ar(25600 + 3200 * i, [SPAD]) for i in range(2)]
        acc = ar(32000, [SPAD])
        junk = ar(35200, [SPAD], BF16)
        A3 = ar(36800, [SPAD], BF16)
        Z, Zb = ar(19200, [SPAD]), junk
        hT0 = ar(12800, [SPAD])
        ring = [ar(9600 + 1568 * i, [S], BF16) for i in range(4)]
        G = ar(15872, [NT, 3, D], BF16)
        FA, FB, FC = ar(20672, [SPAD]), ar(23872, [SPAD]), ar(27072, [SPAD])
        rest = FC.rearrange("p (t d) -> p t d", d=D)
        att_o = rest
        gr, gz, gn = (ar(30272 + CW * i, [CW]) for i in range(3))
        DB = ar(0, [SPAD])
        TT = ar(35200, [SPAD], F32, NTYPE)

        nb = sb("nb", [P, NT, H * (C + 1)], F32)
        hn = nb[:, :, 0:D]
        haug = sb("haug", [P, NT, H, C + 1], F32)
        x = haug[:, :, :, :].rearrange("p t h c -> p (t h c)")[:, 0:NT * D].rearrange("p (t d) -> p t d", d=D)
        PT = [sb(f"PT{i}", [P, TG * P], F32) for i in range(2)]
        aggS = [sb(f"aggS{i}", [C + 1, H * P], F32) for i in range(2)]
        ident = sb("ident", [P, P], F32)
        identb = sb("identb", [P, P], BF16)
        ones = sb("ones", [P, P], F32)
        onesb = sb("onesb", [P, P], BF16)
        head_rows = sb("head_rows", [P, H, P], BF16)
        quarters_sum = sb("quarters_sum", [P, GD], F32)
        Wraw = ar(0, [10, D])
        WT = sb("WT", [P, 12, D], F32)
        WW = sb("WW", [P, D + 2 * H], F32)
        wa_t = sb("wa_t", [P, D], F32)
        vec = sb("vec", [P, 8, D], F32)
        col = sb("col", [P, 24], F32)
        embx = sb("embx", [NTYPE, D], F32)
        bmsg9 = sb("bmsg9", [NTYPE, D], F32)
        Traw = sb("Traw", [P, NG, NTYPE], F32)
        asd = sb("asd", [P, NT, 2 * H], F32)
        ad8 = sb("ad8", [P, NT * H], F32)
        mx = sb("mx", [P, 2, 3, H], F32)
        wins = sb("wins", [1, NG * 2], I32)
        win = sb("win", [NG, 2], F32)
        win_i = sb("win_i", [NG, 2], I32)
        tlo = sb("tlo", [EP, 2, EJ], F32)
        grp_i = sb("grp_i", [NG, 1], I32)
        tiny = sb("tiny", [P, 1], F32)
        marks = sb("marks", [P, 4], F32)
        grp = sb("grp", [NG, 2], F32)
        it9 = sb("it9", [ET, NTYPE], F32)
        it9i = sb("it9i", [ET, NTYPE], I32)
        ovf = sb("ovf", [P, NG], F32)
        flag_f = sb("flag_f", [P, 1], F32)
        flag_i = sb("flag_i", [1, 1], I32)
        bn6 = sb("bn6", [P, NT, 6], F32)
        mv = sb("mv", [P, NT, 2], F32)
        rstd = sb("rstd", [P, NT], F32)
        shift = sb("shift", [P, NT], F32)
        rden = sb("rden", [P, NT, H], F32)
        dinv = sb("dinv", [P, NT], F32)
        rdeg = sb("rdeg", [P, NT], F32)
        mhalf = sb("mhalf", [P, NT], F32)
        masks = sb("masks", [P, 6], F32)

        psum = ctx.enter_context(nc.psum_tensor("psum", [P, 8, CW], F32))
        psum_flat = psum[:, :, :].rearrange("p a b -> p (a b)")


        v, a, gp, pt = nc.vector, nc.scalar, nc.gpsimd, nc.tensor
        s_chain = {e: sem("chain_" + e) for e in ("dve", "act", "pool")}
        chain = {e: 0 for e in s_chain}

        def link(eng, which, ins):
            chain[which] += 1
            ins.then_inc(s_chain[which], 1)
            eng.wait_ge(s_chain[which], chain[which])

        NPASS = NG // 2

        def halves(x):
            return x.rearrange("p (h n) -> p h n", h=2)

        weights_in, zeroed, x_in = sem("weights_in"), sem("x_zeroed"), sem("x_in")
        WSRC = [("L1_gnn_W_msg", 1), ("L1_gnn_W_ih", 3), ("L1_gnn_W_hh", 3), ("L3_gnn_W1", 1), ("L3_gnn_W2", 1), ("L3_gnn_W3", 1)]
        COLS = [("L1_gnn_b_ih", 0, 3), ("L1_gnn_b_hh", 3, 3), ("L2_gnn_b_mlp", 6, 1), ("L2_gnn_gamma1", 7, 1), ("L2_gnn_beta1", 8, 1),
                ("L2_gnn_b_conv", 9, 1), ("L2_gnn_gamma2", 10, 1), ("L2_gnn_beta2", 11, 1)]
        N_WEIGHTS = len(WSRC) + 3 + 8 + len(COLS) + 2

        def load_weights(sp):
            k = 0
            for name, n in WSRC:
                sp.dma_start(Wraw[:, k:k + n, :], t[name].rearrange("(w p) d -> p w d", p=P)).then_inc(weights_in, 16)
                k += n
            sp.dma_start(WT[:, 10, :], t["L2_gnn_W_mlp"]).then_inc(weights_in, 16)
            sp.dma_start(WT[:, 11, :], t["L2_gnn_W_conv"]).then_inc(weights_in, 16)
            sp.dma_start(WW[:, 0:D], t["L0_gnn_W"]).then_inc(weights_in, 16)
            for k, name in enumerate(("L0_gnn_a_src", "L0_gnn_a_dst")):
                sp.dma_start(vec[:, 6 + k, :], t[name].rearrange("h c -> (h c)").partition_broadcast(P)).then_inc(weights_in, 16)
            for k, name in enumerate(("L0_gnn_bias", "L0_gnn_gamma", "L0_gnn_beta", "L3_gnn_b1", "L3_gnn_b2", "L3_gnn_b3")):
                sp.dma_start(vec[:, k, :], t[name].partition_broadcast(P)).then_inc(weights_in, 16)
            for name, c0, n in COLS:
                sp.dma_start(col[:, c0:c0 + n], t[name].rearrange("(k p) -> p k", p=P), allow_slow_non_contiguous=True).then_inc(weights_in, 16)
            sp.dma_start(embx[:, :], t["L1_gnn_edge_embed"]).then_inc(weights_in, 16)
            sp.dma_start(bmsg9[:, :], t["L1_gnn_b_msg"].partition_broadcast(NTYPE)).then_inc(weights_in, 16)

        def load_x(sp, zeroed, x_in):
            sp.dma_start(x[:, 0:NT - 1, :], t["x"][0:(NT - 1) * P, :].rearrange("(t p) d -> p t d", p=P)).then_inc(x_in, 16)
            sp.wait_ge(zeroed, 1)
            sp.dma_start(x[0:TAIL, NT - 1, :], t["x"][(NT - 1) * P:N, :]).then_inc(x_in, 16)

        def phase_counts():
            edges_in, consts, split_ready, cols_out, cols_in = sem("edges_in"), sem("consts"), sem("split_ready"), sem("cols_out"), sem("cols_in")
            bounds_ready, bounds_st, bounds_in = sem("bounds_ready"), sem("bounds_st"), sem("bounds_in")
            win_ready, win_st, win_in = sem("win_ready"), sem("win_st"), sem("win_in")
            hot = [sem(f"hot{i}") for i in range(U)]
            hot_used = [sem(f"hot_used{i}") for i in range(U)]
            group_done = [sem(f"group_done{i}") for i in range(2)]
            staged = [sem(f"staged{i}") for i in range(2)]
            stored = [sem(f"stored{i}") for i in range(2)]
            turned_out, turned_stored, sp_step = sem("turned_out"), sem("turned_stored"), sem("sp_step")
            def window(eng, regs, g):
                eng.reg_load(regs, wins[0:1, bass.ds(g * 2, 2)])
                return (eng.snap(regs.lo, min_val=0, max_val=NE - 3 * U + 1), eng.snap(regs.hi, min_val=3 * U, max_val=NE + U - 1))

            with nc.Block() as block:
                @block.sync
                def _(sp):
                    for k, n in enumerate(("src", "dst", "edge_type_9")):
                        sp.dma_start(e_int[:, k, :], t[n].rearrange("(p e) -> p e", p=EP)).then_inc(edges_in, 16)
                    sp.wait_ge(bounds_ready, 1)
                    sp.dma_start(bounds_d.rearrange("k (p j) -> p k j", p=EP), tlo[:, :, :]).then_inc(bounds_st, 16)
                    sp.wait_ge(bounds_st, 16)
                    sp.dma_start(tb[:, :, 0:NE], bounds_d.partition_broadcast(NG)).then_inc(bounds_in, 16)
                    sp.wait_ge(win_ready, 1)
                    sp.dma_start(win_d, win_i[:, :]).then_inc(win_st, 16)
                    sp.wait_ge(win_st, 16)
                    sp.dma_start(wins[0:1, :], win_d.rearrange("(o g) k -> o (g k)", o=1)).then_inc(win_in, 16)
                    load_weights(sp)
                    load_x(sp, zeroed, x_in)
                    with sp.Fori(0, HALF) as r:
                        for i in range(2 * HALF):
                            rows = bass.ds((r * (2 * HALF) + i) * P, P)
                            sp.wait_ge(staged[i % 2], r * HALF + i // 2 + 2)
                            sp.sem_inc(sp_step, 1)
                            for dst, st in ((count32, stage32), (count16, stage16)):
                                sp.dma_start(dst[rows, :], st[i % 2]).then_inc(stored[i % 2], 16)
                            if i in (HALF, 2 * HALF - 1):
                                half = i // HALF if i > HALF else 0
                                sp.wait_ge(turned_out, r * (2 * HALF) + HALF * half + HALF + 1)
                                sp.sem_inc(sp_step, 1)
                                sp.wait_ge(turned_stored, r * 32 + 16 * half + 33)
                                sp.sem_inc(sp_step, 1)
                                sp.dma_start(turned16[:, bass.ds((r * 2 + half) * HALF * GD, HALF * GD)].rearrange("(j p) d -> p j d", p=TB),
                                             turned_st[:, :, half * HALF * GD:(half + 1) * HALF * GD]).then_inc(turned_stored, 16)
                    for b in range(2):
                        sp.wait_ge(stored[b], 32 * (NPASS + 1))
                    sp.wait_ge(turned_stored, 16 * 2 * HALF + 33)

                @block.gpsimd
                def _(pool):
                    link(pool, "pool", gp.memset(ones[:, :], 1.0))
                    gp.affine_select(out=ident[:, :], in_=ones[:, :], compare_op=ALU.is_equal, fill=0.0, base=0,
                                     pattern=[[-1, P]], channel_multiplier=1).then_inc(consts, 1)
                    gp.iota(iota_i[:, 0:NE], [[1, NE]], base=0, channel_multiplier=0)
                    gp.iota(grp_i[:, :], [[1, 1]], base=0, channel_multiplier=GD)
                    gp.iota(it9i[:, :], [[1, NTYPE]], base=0, channel_multiplier=0).then_inc(consts, 1)
                    gp.memset(onesb[:, :], 1.0)
                    gp.memset(stage16[1], 0.0)
                    gp.iota(iotaR, [[1, R]], base=0, channel_multiplier=0)
                    gp.iota(iota_keys, [[1, NG * P]], base=0, channel_multiplier=0).then_inc(consts, 1)
                    gp.memset(x[:, NT - 1, :], 0.0).then_inc(zeroed, 1)
                    link(pool, "pool", gp.memset(head_rows[:, :, :], 0.0))
                    for h in range(H):
                        link(pool, "pool", gp.memset(head_rows[32 * h:32 * h + 32, h, :], 1.0))

                @block.tensor
                def _(pe):
                    for i in range(U):
                        pe.sem_inc(hot_used[i], 1)
                    pe.wait_ge(consts, 1)
                    pe.wait_ge(split_ready, 1)
                    k = 0
                    for src in (e_key, e_f[:, 0, :], e_f[:, 2, :]):
                        for j0, j1 in ((0, 6), (6, EJ)):
                            for j in range(j0, j1):
                                last = pt.transpose(psum[0:ET, k, (j - j0) * EP:(j - j0 + 1) * EP],
                                                    src[:, j * ET:(j + 1) * ET], ident[0:EP, 0:EP])
                            last.then_inc(cols_out, 1)
                            k += 1
                    pe.wait_ge(cols_in, k)
                    pe.wait_ge(win_in, 16)
                    window_regs = pe.alloc_register64("pe_window")
                    turn_reg = pe.alloc_register("pe_turn")
                    pe.reg_mov(turn_reg, 1)

                    def turn(t0, b, first, last, m=None):
                        n = pe.snap(turn_reg)
                        if first:
                            pe.wait_ge(staged[b], m + 1)
                        for i in range(U):
                            pe.wait_ge(hot[i], n)
                            start, stop = first and i == 0, last and i == U - 1
                            for h in range(2):
                                pt.matmul(psum[:, 3 * b + h, 0:R // 2], A[i], B[i][:, h * (R // 2):(h + 1) * (R // 2)],
                                          start=start, stop=stop)
                            pt.matmul(psum[:, 3 * b + 2, 0:NTYPE], A[i], Y[:, bass.ds(t0 + i, 1), 0:NTYPE],
                                      start=start, stop=stop).then_inc(hot_used[i], 1)
                        pe.reg_add(turn_reg, turn_reg, 1)

                    def transpose_group(b):
                        for k in range(TK):
                            pt.transpose(psum[0:TB, 6, :].bitcast(BF16)[:, k * P:(k + 1) * P], stage16[b][:, k * TB:(k + 1) * TB], identb[:, :])

                    with pe.Fori(0, NPASS) as m:
                        for b in range(2):
                            lo, hi = window(pe, window_regs, m * 2 + b)
                            turn(lo, b, True, False, m)
                            with pe.Fori(lo + U, hi - U, U) as tt:
                                turn(tt, b, False, False)
                            turn(hi - U, b, False, True)
                            pe.wait_ge(staged[1 - b], m + 1 + b)
                            transpose_group(1 - b)
                            pt.matmul(psum[0:1, 7, 0:1], onesb[:, 0:1], onesb[:, 0:1], start=True, stop=True).then_inc(group_done[b], 1)
                    pe.wait_ge(staged[1], NPASS + 1)
                    transpose_group(1)
                    pt.matmul(psum[0:1, 7, 0:1], onesb[:, 0:1], onesb[:, 0:1], start=True, stop=True).then_inc(group_done[0], 1)

                @block.scalar
                def _(act):
                    for b in range(2):
                        act.sem_inc(staged[b], 1)
                        act.sem_inc(stored[b], 32)
                    act.sem_inc(turned_stored, 33)
                    a.preload_act_table(ACT.Copy)
                    col_reg = act.alloc_register("turned_col")
                    act.reg_mov(col_reg, (2 * HALF - 1) * GD)

                    def take_turned(col_):
                        a.activation(turned_st.rearrange("p (q k) w -> p k q w", q=Q)[:, :, :, col_],
                                     psum[0:TB, 6, :].bitcast(BF16)[:, 0:TK * P].rearrange("p (k d q) -> p k q d", k=TK, q=Q),
                                     ACT.Copy).then_inc(turned_out, 1)

                    with act.Fori(0, NPASS) as m:
                        for b in range(2):
                            col_ = act.snap(col_reg, min_val=0, max_val=(2 * HALF - 1) * GD)
                            act.reg_add(col_reg, col_reg, GD)
                            act.reg_mod(col_reg, col_reg, 2 * HALF * GD)
                            halves_stored = act.snap((m * 2 + b + HALF - 1) // HALF)
                            act.wait_ge(group_done[b], m + 1)
                            act.wait_ge(turned_stored, halves_stored * 16 + 1)
                            take_turned(bass.ds(col_, GD))
                            act.wait_ge(stored[b], m * 32 + 32)
                            counts = psum[:, 3 * b:3 * b + 2, 0:R // 2]
                            a.activation(halves(stage32[b]), counts, ACT.Copy)
                            a.activation(halves(stage16[b]), counts, ACT.Copy)
                            a.activation(halves(ovf_junk[b]), counts, ACT.Relu, bias=marks[:, 0:1],
                                         accum_out=ovf[:, bass.ds(m * 2 + b, 1)])
                            a.activation(Traw[:, bass.ds(m * 2 + b, 1), :].rearrange("p o k -> p (o k)"), psum[:, 3 * b + 2, 0:NTYPE],
                                         ACT.Copy).then_inc(staged[b], 1)
                    act.wait_ge(group_done[0], NPASS + 1)
                    act.wait_ge(turned_stored, 16 * 2 * HALF + 1)
                    take_turned(slice((2 * HALF - 1) * GD, 2 * HALF * GD))

                @block.vector
                def _(dve):
                    dve.wait_ge(edges_in, 48)
                    link(dve, "dve", v.tensor_copy(e_f, e_int))
                    v.tensor_reduce(tlo[:, 0, :], e_f[:, 1, :].rearrange("p (j e) -> p j e", j=EJ), AX.X, ALU.min)
                    v.tensor_reduce(tlo[:, 1, :], e_f[:, 1, :].rearrange("p (j e) -> p j e", j=EJ), AX.X, ALU.max).then_inc(bounds_ready, 1)
                    link(dve, "dve", v.tensor_scalar(e_t, e_f[:, 0, :], float(R), None, ALU.is_ge))
                    for k in (2, 3):
                        link(dve, "dve", v.tensor_scalar(e_key, e_f[:, 0, :], float(k * R), None, ALU.is_ge))
                        link(dve, "dve", v.tensor_tensor(e_t, e_t, e_key, ALU.add))
                    link(dve, "dve", v.scalar_tensor_tensor(e_f[:, 0, :], e_t, -float(R), e_f[:, 0, :], ALU.mult, ALU.add))
                    link(dve, "dve", v.scalar_tensor_tensor(e_key, e_f[:, 1, :], float(Q), e_t, ALU.mult, ALU.add))
                    v.tensor_scalar(e_f[:, 2, :], e_f[:, 2, :], 0.0, float(NTYPE - 1), ALU.max, ALU.min).then_inc(split_ready, 1)
                    v.memset(marks[:, 0:1], -BF16_MAX_COUNT)
                    v.memset(tiny[:, :], TINY)
                    v.memset(key[:, NE:], -1.0)
                    v.memset(rem[:, NE:], 0.0)
                    v.memset(typ[:, NE:], 0.0)
                    k = 0
                    for dst in (key, rem, typ):
                        dv = dst[:, 0:NE].rearrange("e (p j) -> e j p", p=EP)
                        for j0, j1 in ((0, 6), (6, EJ)):
                            dve.wait_ge(cols_out, k + 1)
                            v.tensor_copy(dv[:, j0:j1, :], psum[0:ET, k, 0:(j1 - j0) * EP].rearrange("e (j p) -> e j p", p=EP)).then_inc(cols_in, 1)
                            k += 1
                    dve.wait_ge(cols_in, k)
                    dve.wait_ge(consts, 2)
                    v.tensor_copy(identb[:, :], ident[:, :])
                    v.tensor_copy(iota_t[:, 0:NE], iota_i[:, 0:NE])
                    v.tensor_copy(grp[:, 0:1], grp_i[:, :])
                    link(dve, "dve", v.tensor_copy(it9[:, :], it9i[:, :]))
                    link(dve, "dve", v.tensor_scalar(grp[:, 1:2], grp[:, 0:1], float(GD - 1), None, ALU.add))
                    it = iota_t[:, 0:NE]
                    cv = covers[:, 0:NE]
                    t0, t1 = tb[:, 0, 0:NE], tb[:, 1, 0:NE]
                    dve.wait_ge(bounds_in, 16)
                    link(dve, "dve", v.tensor_scalar(cv, t0, grp[:, 1:2], None, ALU.is_le))
                    link(dve, "dve", v.scalar_tensor_tensor(cv, t1, grp[:, 0:1], cv, ALU.is_ge, ALU.mult))
                    link(dve, "dve", v.scalar_tensor_tensor(t0, it, 1.0, cv, ALU.add, ALU.mult))
                    link(dve, "dve", v.tensor_scalar(it, it, -1.0, float(NE), ALU.mult, ALU.add))
                    link(dve, "dve", v.tensor_tensor(t1, it, cv, ALU.mult))
                    link(dve, "dve", v.tensor_reduce(win[:, 0:1], t1, AX.X, ALU.max))
                    link(dve, "dve", v.tensor_reduce(win[:, 1:2], t0, AX.X, ALU.max))
                    link(dve, "dve", v.tensor_scalar(win[:, 0:1], win[:, 0:1], -1.0, float(NE), ALU.mult, ALU.add))
                    link(dve, "dve", v.tensor_scalar(win[:, 0:1], win[:, 0:1], float(NE - 3 * U + 1), None, ALU.min))
                    link(dve, "dve", v.tensor_tensor(win[:, 1:2], win[:, 1:2], win[:, 0:1], ALU.subtract))
                    link(dve, "dve", v.tensor_scalar(win[:, 1:2], win[:, 1:2], float(3 * U), (U - 1) / 2, ALU.max, ALU.add))
                    link(dve, "dve", v.tensor_scalar(win[:, 1:2], win[:, 1:2], 1.0 / U, None, ALU.mult))
                    link(dve, "dve", v.tensor_scalar(win[:, 1:2], win[:, 1:2], 2.0 ** 23, None, ALU.add))
                    link(dve, "dve", v.tensor_scalar(win[:, 1:2], win[:, 1:2], -2.0 ** 23, float(U), ALU.add, ALU.mult))
                    link(dve, "dve", v.tensor_tensor(win[:, 1:2], win[:, 1:2], win[:, 0:1], ALU.add))
                    v.tensor_copy(win_i[:, :], win[:, :]).then_inc(win_ready, 1)
                    v.tensor_tensor(Y[:, 0:NE + PADE, 0:NTYPE], typ.unsqueeze(2).to_broadcast([ET, NE + PADE, NTYPE]),
                                    it9[:, :].unsqueeze(1).to_broadcast([ET, NE + PADE, NTYPE]), ALU.is_equal)
                    dve.wait_ge(win_in, 16)
                    dve.wait_ge(consts, 3)
                    window_regs = dve.alloc_register64("dve_window")
                    turn_reg = dve.alloc_register("dve_turn")
                    dve.reg_mov(turn_reg, 1)
                    with dve.Fori(0, NG) as g:
                        lo, hi = window(dve, window_regs, g)
                        group_keys = iota_keys[:, bass.ds(dve.snap(g * P), P)]
                        with dve.Fori(lo, hi, U) as tt:
                            n = dve.snap(turn_reg)
                            for i in range(U):
                                dve.wait_ge(hot_used[i], n)
                                v.tensor_scalar(A[i], group_keys, key[:, bass.ds(tt + i, 1)], None, ALU.is_equal)
                                v.tensor_scalar(B[i], iotaR, rem[:, bass.ds(tt + i, 1)], None,
                                                ALU.is_equal).then_inc(hot[i], 1)
                            dve.reg_add(turn_reg, turn_reg, 1)

        def layer_stats(dve, y, root_in, root_out, n, counted=False):
            if not counted:
                for k in range(NT):
                    v.bn_stats(bn6[:, k, :], y[:, k, :])
            link(dve, "dve", v.memset(marks[:, 2:3], 0.0))
            for k in range(NT):
                last = v.bn_aggr(mv[:, k, :], bn6[:, k, :])
            link(dve, "dve", last)
            v.tensor_scalar(rstd[:, :], mv[:, :, 1], EPS, None, ALU.add).then_inc(root_in, 1)
            dve.wait_ge(root_out, n)

        def tile_stats(dve, added, c):
            dve.wait_ge(added, c + 1)
            for k in range(4 * c, min(4 * c + 4, NT)):
                v.bn_stats(bn6[:, k, :], x[:, k, :])

        def over_features(ap, n=NT):
            return ap.unsqueeze(2).to_broadcast([P, n, D])

        def norm_relu(dve, shift_ready, normed):
            link(dve, "dve", v.tensor_tensor(shift[:, :], mv[:, :, 0], rstd[:, :], ALU.mult))
            v.tensor_scalar(shift[:, :], shift[:, :], -1.0, None, ALU.mult).then_inc(shift_ready, 1)
            for k0 in range(0, NT, 8):
                k = slice(k0, min(k0 + 4, NT))
                n = k.stop - k0
                link(dve, "dve", v.tensor_tensor(hn[:, k, :], x[:, k, :], over_features(mv[:, k, 0], n), ALU.subtract))
                v.scalar_tensor_tensor(hn[:, k, :], hn[:, k, :], 0.0, over_features(rstd[:, k], n), ALU.max, ALU.mult).then_inc(normed[0], 1)
            normed_all(dve, normed)

        def norm_relu_act(act, shift_ready, normed):
            act.wait_ge(shift_ready, 1)
            for k0 in range(4, NT, 8):
                for k in range(k0, min(k0 + 4, NT)):
                    last = a.activation(hn[:, k, :], x[:, k, :], ACT.Relu, scale=rstd[:, k:k + 1], bias=shift[:, k:k + 1])
                last.then_inc(normed[1], 1)

        def normed_chunk(eng, normed, c):
            eng.wait_ge(normed[c % 2], c // 2 + 1)

        def normed_all(eng, normed):
            eng.wait_ge(normed[0], 4)
            eng.wait_ge(normed[1], 3)

        def taken(eng, outs, i):
            if i >= 0:
                eng.wait_ge(outs[i % 2], i // 2 + 1)

        def take_all(eng, which, made, outs, jobs, first=0):
            for i, pieces in enumerate(jobs):
                if (first + i) % 2 == which:
                    eng.wait_ge(made, first + i + 1)
                    for dst, src in pieces:
                        last = a.activation(dst, src, ACT.Copy) if which == 0 else v.tensor_copy(dst, src)
                    last.then_inc(outs[which], 1)

        def phase_nodes():
            made, var_ready, std_done, norm_shift = (sem(n) for n in ("n_made", "n_var", "n_std", "n_norm_shift"))
            hn_normed = [sem("n_normed_dve"), sem("n_normed_act")]
            outs = [sem("n_out_act"), sem("n_out_dve")]
            w_and_a_ready, quarters_ready, types_stored = sem("n_ww"), sem("n_tq"), sem("n_t98")
            jobs = []
            for b0, b1 in ((0, 4), (4, 8), (8, 10)):
                i = len(jobs)
                jobs.append([(WT[:, b0:b1, :], psum[:, i % 8, 0:(b1 - b0) * P].rearrange("p (w n) -> p w n", n=P))])
            for c in range(NCHUNK):
                w = min(CW, SPAD - c * CW)
                jobs.append([(hT0[:, c * CW:c * CW + w], psum[:, len(jobs) % 8, 0:w])])
            trios = [(k, min(k + 3, NT)) for k in range(0, NT, 3)]
            for k0, k1 in trios:
                src = psum[:, len(jobs) % 8, 0:(k1 - k0) * (D + 2 * H)].rearrange("p (t n) -> p t n", n=D + 2 * H)
                jobs.append([(haug[:, k, :, 0:C], src[:, k - k0, 0:D].rearrange("p (h c) -> p h c", h=H)) for k in range(k0, k1)]
                            + [(asd[:, k0:k1, :], src[:, :, D:D + 2 * H])])
            for h in range(H):
                for c in range(NCHUNK):
                    w = min(CW, SPAD - c * CW)
                    jobs.append([(as_bc[:, h, c * CW:c * CW + w], psum[:, len(jobs) % 8, 0:w])])
            for k in range(2):
                jobs.append([(T32[:, :, 49 * k:49 * k + 49].rearrange("p k g -> p g k"),
                              psum[0:GD, len(jobs) % 8, 0:49 * NTYPE].rearrange("p (g k) -> p g k", k=NTYPE))])
            jobs.append([(T98, psum[0:NG, len(jobs) % 8, 0:NTYPE * GD].rearrange("p (k d) -> p k d", k=NTYPE))])

            with nc.Block() as block:
                @block.sync
                def _(sp):
                    taken(sp, outs, 49)
                    sp.dma_start(types_d.rearrange("k (g d) -> g k d", d=GD), T98).then_inc(types_stored, 16)
                    sp.wait_ge(types_stored, 16)

                @block.gpsimd
                def _(pool):
                    link(pool, "pool", gp.memset(mhalf[:, :], -0.5))
                    pool.wait_ge(var_ready, 1)
                    gp.tensor_tensor(rstd[:, :], rstd[:, :], mhalf[:, :], ALU.pow).then_inc(std_done, 1)

                @block.vector
                def _(dve):
                    v.tensor_reduce(quarters_sum[:, :], ident[:, :].rearrange("p (d q) -> p d q", q=Q), AX.X, ALU.add).then_inc(quarters_ready, 1)
                    link(dve, "dve", v.tensor_reduce(masks[:, 0:3], ident[:, :].rearrange("p (a k) -> p k a", k=32)[:, 0:3, :], AX.X, ALU.add))
                    v.tensor_scalar(masks[:, 3:4], masks[:, 0:1], -1.0, None, ALU.add)
                    v.tensor_scalar(masks[:, 4:5], masks[:, 2:3], -1.0, None, ALU.mult)
                    link(dve, "dve", v.tensor_reduce(masks[:, 5:6], masks[:, 0:3], AX.X, ALU.add))
                    v.tensor_scalar(head_rows[:, :, :], head_rows[:, :, :], masks[:, 5:6], None, ALU.mult)
                    dve.wait_ge(weights_in, 16 * N_WEIGHTS)
                    v.tensor_tensor(embx[:, :], embx[:, :], bmsg9[:, :], ALU.add)
                    for k in range(2):
                        link(dve, "dve", v.tensor_tensor(wa_t[:, :], WW[:, 0:D], vec[:, 6 + k, :], ALU.mult))
                        last = v.tensor_reduce(WW[:, D + H * k:D + H * k + H], wa_t[:, :].rearrange("p (h c) -> p h c", h=H), AX.X, ALU.add)
                        link(dve, "dve", last)
                    v.tensor_copy(WAb, WW[:, D:D + H].unsqueeze(2).to_broadcast([P, H, P])).then_inc(w_and_a_ready, 1)
                    dve.wait_ge(x_in, 32)
                    layer_stats(dve, x, var_ready, std_done, 1)
                    norm_relu(dve, norm_shift, hn_normed)
                    take_all(dve, 1, made, outs, jobs[0:10])
                    v.memset(haug[:, :, :, C:C + 1], 1.0)
                    take_all(dve, 1, made, outs, jobs[10:], 10)
                    for k in range(len(jobs)):
                        taken(dve, outs, k)
                    v.tensor_scalar(ad8[:, :].rearrange("p (t h) -> p t h", h=H), asd[:, :, H:2 * H], 1.0 - SLOPE, None, ALU.mult)

                @block.scalar
                def _(act):
                    take_all(act, 0, made, outs, jobs[0:3])
                    act.wait_ge(x_in, 32)
                    norm_relu_act(act, norm_shift, hn_normed)
                    take_all(act, 0, made, outs, jobs[3:10], 3)
                    take_all(act, 0, made, outs, jobs[10:], 10)

                @block.tensor
                def _(pe):
                    made_n = [0]

                    def bank():
                        i = made_n[0]
                        taken(pe, outs, i - 8)
                        return psum[:, i % 8, :]

                    def done(ins):
                        made_n[0] += 1
                        ins.then_inc(made, 1)

                    pe.wait_ge(weights_in, 16 * N_WEIGHTS)
                    for b0, b1 in ((0, 4), (4, 8), (8, 10)):
                        o = bank()
                        for k in range(b0, b1):
                            last = pt.transpose(o[:, (k - b0) * P:(k - b0 + 1) * P], Wraw[:, k, :], ident[:, :])
                        done(last)
                    for i in range(3):
                        taken(pe, outs, i)
                    for c in range(NCHUNK):
                        normed_chunk(pe, hn_normed, c)
                        o = bank()
                        for k in range(4 * c, min(4 * c + 4, NT)):
                            last = pt.transpose(o[:, (k - 4 * c) * P:(k - 4 * c + 1) * P], hn[:, k, :], ident[:, :])
                        done(last)
                    pe.wait_ge(w_and_a_ready, 1)
                    for k in range(3, 10):
                        taken(pe, outs, k)
                    for k0, k1 in trios:
                        o = bank()
                        for k in range(k0, k1):
                            last = pt.matmul(o[:, (k - k0) * (D + 2 * H):(k - k0 + 1) * (D + 2 * H)], hT0[:, k * P:(k + 1) * P], WW[:, :],
                                             start=True, stop=True)
                        done(last)
                    for h in range(H):
                        for c in range(NCHUNK):
                            w = min(CW, SPAD - c * CW)
                            done(pt.matmul(bank()[:, 0:w], WAb[:, h, :], hT0[:, c * CW:c * CW + w], start=True, stop=True))
                    pe.wait_ge(quarters_ready, 1)
                    for k in range(2):
                        done(pt.matmul(bank()[0:GD, 0:49 * NTYPE], quarters_sum[:, :], Traw[:, 49 * k:49 * k + 49, :].rearrange("p g k -> p (g k)"),
                                       start=True, stop=True))
                    taken(pe, outs, 47)
                    taken(pe, outs, 48)
                    o = bank()
                    for k in range(NTYPE):
                        last = pt.transpose(o[0:NG, k * GD:(k + 1) * GD], T32[:, k, :], ident[0:GD, 0:GD])
                    done(last)

        def phase_attention():
            names = ("block_in0", "block_in1", "mask_ready", "ln_ready", "logs_ready", "max_done", "relu_done", "sum_done", "turned", "scores_done",
                     "exp_done", "used", "sums_out", "back", "sums_in", "cleared", "ident_in", "own_terms", "half_scaled")
            (in0, in1, mask_ready, ln_ready, logs_ready, max_done, relu_done, sum_done, turned, scores_done,
             exp_done, used, sums_out, back, sums_in, cleared, ident_in, own_terms, half_scaled) = (sem("a_" + n) for n in names)
            block_in = [in0, in1]
            psT = [psum_flat[:, 2 * CW * i:2 * CW * i + TG * P] for i in range(2)]

            def blocks(eng, body):
                body(0, 0, 0)
                with eng.Fori(0, NT // 2) as m:
                    body(m * 2 + 1, 1, m)
                    body(m * 2 + 2, 0, m + 1)

            with nc.Block() as block:
                @block.sync
                def _(sp):
                    sp.wait_ge(cleared, 1)
                    sp.dma_start(Cb[0][:, 0:S], rows32[0:P, :]).then_inc(block_in[0], 16)
                    sp.dma_start(Cb[1][:, 0:S], rows32[P:2 * P, :]).then_inc(block_in[1], 16)
                    with sp.Fori(0, NT // 2 - 1) as m:
                        for i in range(2):
                            b = m * 2 + 2 + i
                            sp.wait_ge(sum_done, m * 8 + 4 * i + 5)
                            sp.dma_start(Cb[i][:, 0:S], rows32[bass.ds(b * P, P), :]).then_inc(block_in[i], 16)
                    sp.wait_ge(cleared, 2)
                    sp.dma_start(Cb[0][0:STAIL, 0:S], rows32[(NT - 1) * P:S, :]).then_inc(block_in[0], 16)

                @block.gpsimd
                def _(pool):
                    pool.sem_inc(max_done, 2)
                    pool.sem_inc(sum_done, 1)
                    gp.memset(acc, 0.0)
                    for i in range(2):
                        gp.memset(nm[i][:, S:SPAD], BIG)
                        last = gp.memset(Cb[i][:, S:SPAD], -BIG)
                    last.then_inc(cleared, 1)

                    def body(b, i, turn, last=False):
                        if last:
                            pool.wait_ge(sum_done, 4 * (NT - 2) + 1)
                            pool.wait_ge(logs_ready, NT - 1)
                            gp.memset(Cb[0][STAIL:P, 0:S], 0.0).then_inc(cleared, 1)
                        pool.wait_ge(block_in[i], turn * 16 + 16)
                        width = STAIL if last else P
                        diag = Cb[i][:, bass.ds(b * P, width)]
                        gp.tensor_tensor(diag, diag, ident[:, 0:width], ALU.add).then_inc(ident_in, 1)
                        pool.wait_ge(ident_in, b + 1)
                        gp.tensor_tensor(acc[:, 0:S], acc[:, 0:S], Cb[i][:, 0:S], ALU.add).then_inc(acc_done, 1)
                        pool.wait_ge(ln_ready, b + 1)
                        gp.tensor_tensor(Cb[i][:, 0:S], Cb[i][:, 0:S], nm[i][:, 0:S], ALU.subtract).then_inc(logs_ready, 1)

                    body(0, 0, 0)
                    with pool.Fori(0, NT // 2 - 1) as m:
                        body(m * 2 + 1, 1, m)
                        body(m * 2 + 2, 0, m + 1)
                    body(NT - 2, 1, NT // 2 - 1)
                    body(NT - 1, 0, NT // 2, last=True)

                @block.vector
                def _(dve):
                    for h in range(2):
                        last = v.tensor_scalar(Z[32 * h:32 * h + 32, :], as_bc[32 * h:32 * h + 32, h, :], SLOPE, None, ALU.mult)
                    link(dve, "dve", last)
                    dve.wait_ge(half_scaled, 1)
                    link(dve, "dve", v.tensor_copy(Zb, Z))
                    link(dve, "dve", v.scalar_tensor_tensor(Z, Zb, masks[:, 3:4], Z, ALU.mult, ALU.add))
                    link(dve, "dve", v.tensor_copy(Zb, Z))
                    link(dve, "dve", v.scalar_tensor_tensor(Z, Zb, masks[:, 4:5], Z, ALU.mult, ALU.add))
                    v.tensor_copy(A3, Z).then_inc(own_terms, 1)
                    dve.wait_ge(cleared, 1)

                    def mask(b, i, turn):
                        dve.wait_ge(ident_in, b + 1)
                        v.tensor_scalar(nm[i][:, 0:S], Cb[i][:, 0:S], 0.0, BIG, ALU.is_equal, ALU.mult).then_inc(mask_ready, 1)

                    def source_max(b, i, h):
                        if h == 0:
                            dve.wait_ge(mask_ready, b + 1)
                            v.memset(marks[:, 2:3], 0.0)
                        dve.wait_ge(max_done, b * 4 + h + 2)
                        v.memset(marks[:, 3:4], 0.0)
                        ins = v.tensor_tensor_reduce(out=junk[:, 0:SPAD], in0=as_bc[:, h, :], in1=nm[i], scale=1.0, scalar=NEG_HUGE,
                                                     op0=ALU.subtract, op1=ALU.max, accum_out=mx[:, i, 0, h:h + 1])
                        ins.then_inc(max_done, 1)

                    def shifts(b, i):
                        dve.wait_ge(max_done, b * 4 + 6)
                        adv = asd[:, bass.ds(b, 1), H:2 * H].rearrange("p o h -> p (o h)")
                        v.tensor_tensor(mx[:, i, 1, :], mx[:, i, 0, :], adv, ALU.add).then_inc(shift_step, 1)
                        dve.wait_ge(shift_step, b * 2 + 1)
                        v.scalar_tensor_tensor(mx[:, i, 1, :], mx[:, i, 1, :], SLOPE, mx[:, i, 1, :], ALU.mult, ALU.max).then_inc(shift_step, 1)
                        dve.wait_ge(shift_step, b * 2 + 2)
                        v.scalar_tensor_tensor(mx[:, i, 2, :], adv, SLOPE, mx[:, i, 1, :], ALU.mult, ALU.subtract).then_inc(shifted, 1)

                    def body(b, i, turn, last=False):
                        shifts(b, i)
                        for h in range(H):
                            dve.wait_ge(relu_done, b * 4 + h + 1)
                            if h == 0:
                                dve.wait_ge(logs_ready, b + 1)
                                dve.wait_ge(shifted, b + 1)
                            v.scalar_tensor_tensor(u[h % 2], u[h % 2], mx[:, i, 2, h:h + 1], Cb[i], ALU.add, ALU.add).then_inc(sum_done, 1)
                            if h == 1 and not last:
                                mask(b + 1, 1 - i, turn)
                            if h and not last:
                                source_max(b + 1, 1 - i, h - 1)
                        if not last:
                            source_max(b + 1, 1 - i, 3)

                    mask(0, 0, 0)
                    for h in range(H):
                        source_max(0, 0, h)
                    body(0, 0, 0)
                    with dve.Fori(0, NT // 2 - 1) as m:
                        body(m * 2 + 1, 1, m)
                        body(m * 2 + 2, 0, m + 1)
                    body(NT - 2, 1, NT // 2 - 1)
                    body(NT - 1, 0, NT // 2, last=True)

                @block.scalar
                def _(act):
                    act.sem_inc(turned, 2)
                    act.sem_inc(used, 2)
                    for h in range(2, H):
                        last = a.activation(Z[32 * h:32 * h + 32, :], as_bc[32 * h:32 * h + 32, h, :], ACT.Copy, scale=SLOPE)
                    last.then_inc(half_scaled, 1)
                    a.preload_act_table_set("natural_log_exp_and_others")

                    def logs(b, i, turn):
                        act.wait_ge(mask_ready, b + 1)
                        act.wait_ge(acc_done, b + 1)
                        a.activation(Cb[i][:, 0:S], Cb[i][:, 0:S], ACT.Ln, bias=tiny[:, 0:1]).then_inc(ln_ready, 1)

                    def relu(b, h, half):
                        if half == 0:
                            act.wait_ge(turned, b * 4 + h + 1)
                        sources = slice(half * SPAD // 2, (half + 1) * SPAD // 2)
                        ins = a.activation(u[h % 2][:, sources], as_bc[:, h, sources], ACT.Relu, scale=1.0 - SLOPE,
                                           bias=ad8[:, bass.ds(b * 4 + h, 1)])
                        if half:
                            ins.then_inc(relu_done, 1)

                    def body(b, i, turn, first=False, last=False):
                        for h in range(H):
                            for g in range(5):
                                if g < 2 and h < 3:
                                    relu(b, h + 1, g)
                                elif g < 2 and not last:
                                    relu(b + 1, 0, g)
                                if h == 2 and g == 3 and not last:
                                    logs(b + 1, 1 - i, turn)
                                j = (5 * h + g) % 2
                                act.wait_ge(scores_done, b * 20 + 5 * h + g + 1)
                                act.wait_ge(used, b * 20 + 5 * h + g + 1)
                                n = TG * (STAIL if last else P)
                                a.activation(PT[j][:, 0:n], psT[j][:, 0:n], ACT.Exp).then_inc(exp_done, 1)
                            if h == 0 and not first:
                                take_sums(b - 1, 1 - i)
                        if not first:
                            put_back(b - 1, 1 - i)

                    def take_sums(b, i):
                        act.wait_ge(used, b * 20 + 22)
                        a.activation(aggS[i][:, :], psum[0:C + 1, 4 + i, :], ACT.Copy).then_inc(sums_out, 1)

                    def put_back(b, i):
                        act.wait_ge(back, b + 1)
                        a.activation(nb[:, bass.ds(b, 1), :].rearrange("p o n -> p (o n)"), psum[:, 6, 0:H * (C + 1)], ACT.Copy).then_inc(sums_in, 1)

                    logs(0, 0, 0)
                    relu(0, 0, 0)
                    relu(0, 0, 1)
                    body(0, 0, 0, first=True)
                    with act.Fori(0, NT // 2 - 1) as m:
                        body(m * 2 + 1, 1, m)
                        body(m * 2 + 2, 0, m + 1)
                    body(NT - 2, 1, NT // 2 - 1)
                    body(NT - 1, 0, NT // 2, last=True)
                    take_sums(NT - 1, 0)
                    put_back(NT - 1, 0)

                @block.tensor
                def _(pe):
                    pe.sem_inc(exp_done, 2)
                    pe.sem_inc(sums_out, 2)
                    pe.sem_inc(sums_in, 2)
                    pe.wait_ge(own_terms, 1)

                    def scores(b, h, g, w=P):
                        j = (5 * h + g) % 2
                        pe.wait_ge(exp_done, b * 20 + 5 * h + g + 1)
                        if g == 0:
                            pe.wait_ge(sum_done, b * 4 + h + 2)
                        for k in range(TG):
                            o = psT[j][:, k * w:(k + 1) * w]
                            s0 = (g * TG + k) * P
                            pt.matmul(o, u[h % 2][0:w, s0:s0 + P], ident[0:w, 0:w], is_transpose=True, start=True, stop=False)
                            last = pt.matmul(o, A3[:, s0:s0 + P], head_rows[:, h, 0:w], start=False, stop=True)
                        last.then_inc(scores_done, 1)

                    def weigh(b, i, h, g, w=P):
                        j = (5 * h + g) % 2
                        if h == 0 and g == 0:
                            pe.wait_ge(sums_out, b + 1)
                        pe.wait_ge(exp_done, b * 20 + 5 * h + g + 3)
                        for k in range(TG):
                            s = g * TG + k
                            last = pt.matmul(psum[0:C + 1, 4 + i, h * P:h * P + w], haug[:, s, h, :], PT[j][:, k * w:(k + 1) * w],
                                             start=s == 0, stop=s == NT - 1)
                        last.then_inc(used, 1)

                    def turn_back(b, i):
                        pe.wait_ge(sums_out, b + 3)
                        pe.wait_ge(sums_in, b + 2)
                        pt.matmul(psum[0:1, 7, 0:1], onesb[:, 0:1], onesb[:, 0:1], start=True, stop=True)
                        for h in range(H):
                            last = pt.transpose(psum[:, 6, h * (C + 1):(h + 1) * (C + 1)], aggS[i][:, h * P:(h + 1) * P],
                                                ident[0:C + 1, 0:C + 1])
                        last.then_inc(back, 1)

                    def body(b, i, turn, first=False, w=P):
                        for h in range(H):
                            for g in range(5):
                                scores(b, h, g, w)
                                if h or g:
                                    weigh(b, i, (5 * h + g - 1) // 5, (g - 1) % 5, w)
                                elif not first:
                                    weigh(b - 1, 1 - i, 3, 4)
                            pt.matmul(psum[0:1, 7, 0:1], onesb[:, 0:1], onesb[:, 0:1], start=True, stop=True, skip_group_check=True).then_inc(turned, 1)
                            if h == 2 and not first:
                                turn_back(b - 1, 1 - i)

                    body(0, 0, 0, first=True)
                    with pe.Fori(0, NT // 2 - 1) as m:
                        body(m * 2 + 1, 1, m)
                        body(m * 2 + 2, 0, m + 1)
                    body(NT - 2, 1, NT // 2 - 1)
                    body(NT - 1, 0, NT // 2, w=STAIL)
                    weigh(NT - 1, 0, 3, 4, STAIL)
                    turn_back(NT - 1, 0)

        def each(n, w=CW):
            return [(c, c * w, min(w, n - c * w)) for c in range(-(-n // w))]

        def bc_vec(k, n=NT):
            return vec[:, k:k + 1, :].to_broadcast([P, n, D])

        HEAD = 4

        def split(dve):
            for k0, k1 in ((0, HEAD), (HEAD, NT)):
                link(dve, "dve", v.tensor_copy(G[:, k0:k1, 0, :], hn[:, k0:k1, :]))
                link(dve, "dve", v.tensor_tensor(rest[:, k0:k1, :], hn[:, k0:k1, :], G[:, k0:k1, 0, :], ALU.subtract))
                link(dve, "dve", v.tensor_copy(G[:, k0:k1, 1, :], rest[:, k0:k1, :]))
                v.tensor_tensor(G[:, k0:k1, 2, :], rest[:, k0:k1, :], G[:, k0:k1, 1, :], ALU.subtract).then_inc(split_done, 1)

        USES = [7, 6, 6, 6]

        def stream_counts(sp, k, rows, residues):
            def load(t_, i, m, n_rows=P):
                use = m + k * USES[i]
                if not (k == 0 and isinstance(m, int) and m == 0):
                    sp.wait_ge(ring_used[i], use)
                sp.dma_start(ring[i][0:n_rows, :], rows[bass.ds(t_ * P, n_rows), :]).then_inc(ring_in[i], 16)

            for i in range(4):
                load(i, i, 0)
            with sp.Fori(1, 6) as m:
                for i in range(4):
                    load(m * 4 + i, i, m)
            load(NT - 1, 0, 6, STAIL)
            with sp.If(large_counts(sp) > 0):
                summed(sp, k)
                if k == 0:
                    sp.sem_inc(res_used, 1)

                def load_residue(t_, n_rows=P):
                    sp.wait_ge(res_used, t_ + k * NT + 1)
                    sp.sem_inc(res_step, 1)
                    sp.dma_start(ring[1][0:n_rows, :], residues[bass.ds(t_ * P, n_rows), :]).then_inc(res_in, 16)

                with sp.Fori(0, NT - 1) as t_:
                    load_residue(t_)
                load_residue(NT - 1, STAIL)
                sp.wait_ge(res_used, (k + 1) * NT + 1)

        def sum_edges(pe, k, self_loops=False):
            def tile(t_, i, m, first=False, last=False):
                rows = STAIL if last else P
                use = m + k * USES[i]
                pe.wait_ge(ring_in[i], use * 16 + 16)

                def part_of(part):
                    return G[0:rows, NT - 1, part, :] if last else G[:, bass.ds(t_, 1), part, :].rearrange("p o d -> p (o d)")

                def own():
                    for part in range(3):
                        ins = pt.matmul(psum_flat[:, bass.ds(t_ * P, rows)], part_of(part), identb[0:rows, 0:rows], start=False, stop=False)
                    return ins

                if self_loops and last:
                    own()
                for part in range(3):
                    for c, c0, cw in each(S):
                        ins = pt.matmul(psum[:, c, 0:cw], part_of(part), ring[i][0:rows, c0:c0 + cw], start=first and part == 0,
                                        stop=last and part == 2)
                if self_loops and not last:
                    ins = own()
                ins.then_inc(ring_used[i], 1)

            pe.wait_ge(split_done, 2 * k + 1)
            for i in range(HEAD):
                tile(i, i, 0, first=i == 0)
            pe.wait_ge(split_done, 2 * k + 2)
            with pe.Fori(1, 6) as m:
                for i in range(4):
                    tile(m * 4 + i, i, m)
            tile(NT - 1, 0, 6, last=True)
            with pe.If(large_counts(pe) > 0):
                def add_residue(t_, rows=P):
                    pe.wait_ge(res_in, t_ * 16 + k * NT * 16 + 16)
                    for part in range(3):
                        g = G[0:rows, NT - 1, part, :] if rows < P else G[:, bass.ds(t_, 1), part, :].rearrange("p o d -> p (o d)")
                        for c, c0, cw in each(S):
                            ins = pt.matmul(psum[:, c, 0:cw], g, ring[1][0:rows, c0:c0 + cw], start=False, stop=True, skip_group_check=True)
                    ins.then_inc(res_used, 1)

                with pe.Fori(0, NT - 1) as t_:
                    add_residue(t_)
                add_residue(NT - 1, STAIL)
            pt.matmul(psum[0:1, 7, 0:1], onesb[:, 0:1], onesb[:, 0:1], start=True, stop=True).then_inc(sums_done, 1)

        def summed(eng, k):
            eng.wait_ge(ring_used[0], 7 * (k + 1))

        def all_summed(eng, k):
            eng.wait_ge(sums_done, k + 1)

        def large_counts(eng):
            return eng.value_load(flag_i[0:1, 0:1], min_val=0, max_val=1)

        def phase_attention_end():
            x_in, zeroed, root_in, root_out, flag_made, ovf_summed = (sem("t_" + n) for n in ("x_in", "zeroed", "root_in", "root_out", "flag", "ovf_summed"))
            with nc.Block() as block:
                @block.sync
                def _(sp):
                    load_x(sp, zeroed, x_in)
                    sp.dma_start(TT[:, 0:S], types_d).then_inc(tt_in, 16)

                @block.gpsimd
                def _(pool):
                    gp.memset(x[:, NT - 1, :], 0.0).then_inc(zeroed, 1)
                    gp.memset(TT[:, S:SPAD], 0.0)
                    for k in range(2):
                        pool.wait_ge(root_in, k + 1)
                        gp.tensor_tensor(rstd[:, :], rstd[:, :], mhalf[:, :], ALU.pow).then_inc(root_out, 1)

                @block.tensor
                def _(pe):
                    pe.wait_ge(ovf_summed, 1)
                    pt.matmul(psum[0:1, 2, 0:1], flag_f[:, 0:1], ones[:, 0:1], start=True, stop=True).then_inc(flag_made, 1)

                @block.vector
                def _(dve):
                    v.tensor_reduce(flag_f[:, 0:1], ovf[:, :], AX.X, ALU.add).then_inc(ovf_summed, 1)
                    att = nb[:, :, :].rearrange("p t (h c) -> p t h c", h=H)
                    link(dve, "dve", v.tensor_scalar(rden[:, :, :], att[:, :, :, C], 1e-16, None, ALU.add))
                    link(dve, "dve", v.reciprocal(rden[:, :, :], rden[:, :, :]))
                    for h in range(H):
                        last = v.tensor_tensor(att_o[:, :, h * C:(h + 1) * C], att[:, :, h, 0:C],
                                               rden[:, :, h:h + 1].to_broadcast([P, NT, C]), ALU.mult)
                    link(dve, "dve", last)
                    link(dve, "dve", v.tensor_tensor(att_o, att_o, bc_vec(0), ALU.add))
                    layer_stats(dve, att_o, root_in, root_out, 1)
                    link(dve, "dve", v.tensor_tensor(att_o, att_o, over_features(mv[:, :, 0]), ALU.subtract))
                    link(dve, "dve", v.tensor_tensor(att_o, att_o, over_features(rstd[:, :]), ALU.mult))
                    link(dve, "dve", v.tensor_tensor(att_o, att_o, bc_vec(1), ALU.mult))
                    link(dve, "dve", v.tensor_tensor(att_o, att_o, bc_vec(2), ALU.add))
                    dve.wait_ge(x_in, 32)
                    link(dve, "dve", v.scalar_tensor_tensor(x, att_o, 0.0, x, ALU.max, ALU.add))
                    layer_stats(dve, x, root_in, root_out, 2)
                    dve.wait_ge(flag_made, 1)
                    v.tensor_scalar(flag_i[:, :], psum[0:1, 2, 0:1], 0.0, None, ALU.is_gt)

        def phase_residue():
            names = ("rows_in", "left", "stored", "turned", "taken")
            rows_in, left, stored, turned, took = (sem("r_" + n) for n in names)
            W = 64
            NB = S // W
            BANKS = [(0, 16), (16, 32), (32, 48), (48, 49)]
            exact = FA[0:W, 0:S]
            rounded = FB[0:W, :].bitcast(BF16)[:, 0:S]
            left_t = FC[0:W, :].bitcast(BF16)[:, 0:S].rearrange("p (t d) -> p t d", d=W)
            with nc.Block() as block:
                @block.scalar
                def _(act):
                    with act.If(large_counts(act) > 0):
                        act.sem_inc(stored, 32)
                        with act.Fori(0, NB) as b:
                            rows = bass.ds(act.snap(b * W), W)
                            act.wait_ge(stored, b * 32 + 32)
                            act.dma_start(exact, rows32[rows, :]).then_inc(rows_in, 16)
                            act.dma_start(rounded, rows16[rows, :]).then_inc(rows_in, 16)
                            act.wait_ge(left, b + 1)
                            act.dma_start(residue[rows, :], rounded).then_inc(stored, 16)
                            act.wait_ge(took, b * 4 + 4)
                            act.dma_start(residue_turned[:, rows].rearrange("(t p) d -> p t d", p=W), left_t).then_inc(stored, 16)
                        act.wait_ge(stored, 32 * (NB + 1))

                @block.vector
                def _(dve):
                    with dve.If(large_counts(dve) > 0):
                        with dve.Fori(0, NB) as b:
                            dve.wait_ge(rows_in, b * 32 + 32)
                            v.tensor_tensor(rounded, exact, rounded, ALU.subtract).then_inc(left, 1)
                            for g, (t0, t1) in enumerate(BANKS):
                                dve.wait_ge(turned, b * 4 + g + 1)
                                v.tensor_copy(left_t[:, t0:t1, :], psum[0:W, g, :].bitcast(BF16)[:, 0:(t1 - t0) * W].rearrange("p (t d) -> p t d", d=W)).then_inc(took, 1)

                @block.tensor
                def _(pe):
                    with pe.If(large_counts(pe) > 0):
                        with pe.Fori(0, NB) as b:
                            pe.wait_ge(left, b + 1)
                            pt.matmul(psum[0:1, 7, 0:1], onesb[:, 0:1], onesb[:, 0:1], start=True, stop=True)
                            for g, (t0, t1) in enumerate(BANKS):
                                for k in range(t0, t1):
                                    last = pt.transpose(psum[0:W, g, :].bitcast(BF16)[:, (k - t0) * W:(k - t0 + 1) * W], rounded[:, k * W:(k + 1) * W],
                                                        identb[0:W, 0:W])
                                last.then_inc(turned, 1)

        def phase_gated():
            names = ("h_by_f", "h_out", "sum_out_act", "sum_out_dve", "msg", "msg_out", "gates", "rz", "pre", "cand", "new", "back", "added", "root_in", "root_out", "zero", "deg", "deg_out", "diag")
            (h_by_f, h_out, sum_act, sum_dve, msg, msg_out, gates, rz, pre, cand, new, back, added, root_in, root_out, zero, deg, deg_out, diag_ready) = (sem("g_" + n) for n in names)
            dst_deg, src_deg, dinv_in, dinv_out = (sem("g_" + n) for n in ("dst_deg", "src_deg", "dinv_in", "dinv_out"))
            norm_shift, hn_normed = sem("g_norm_shift"), [sem("g_normed_dve"), sem("g_normed_act")]
            with nc.Block() as block:
                @block.sync
                def _(sp):
                    stream_counts(sp, 0, turned16, residue_turned)

                @block.gpsimd
                def _(pool):
                    pool.wait_ge(dinv_in, 1)
                    gp.tensor_tensor(dinv[:, :], dinv[:, :], mhalf[:, :], ALU.pow).then_inc(dinv_out, 1)
                    pool.wait_ge(deg, 7)
                    gp.memset(FB[:, S:SPAD], 0.0).then_inc(zero, 1)
                    pool.wait_ge(root_in, 1)
                    gp.tensor_tensor(rstd[:, :], rstd[:, :], mhalf[:, :], ALU.pow).then_inc(root_out, 1)

                @block.tensor
                def _(pe):
                    pe.wait_ge(tt_in, 16)
                    for k in range(NT):
                        last = pt.matmul(psum[:, 7, k:k + 1], TT[:, k * P:(k + 1) * P], ones[0:NTYPE, 0:1], start=True, stop=True)
                    last.then_inc(dst_deg, 1)
                    for c, c0, cw in each(SPAD):
                        normed_chunk(pe, hn_normed, c)
                        for k in range(cw // P):
                            last = pt.transpose(psum[:, c, k * P:(k + 1) * P], hn[:, 4 * c + k, :], ident[:, :])
                        last.then_inc(h_by_f, 1)
                    pe.wait_ge(diag_ready, 1)
                    for c, c0, cw in each(SPAD):
                        pe.wait_ge(h_out, c + 1)
                        pt.matmul(psum[:, c, 0:cw], ones[:, :], FB[:, c0:c0 + cw], start=True, stop=True).then_inc(deg, 1)
                    pe.wait_ge(deg_out, 7)
                    sum_edges(pe, 0)
                    pe.wait_ge(sum_act, 4)
                    pe.wait_ge(sum_dve, 3)
                    for c, c0, cw in each(S):
                        pt.matmul(psum[:, c, 0:cw], WT[:, 0, :], FB[:, c0:c0 + cw], start=True, stop=False)
                        pt.matmul(psum[:, c, 0:cw], embx[:, :], TT[:, c0:c0 + cw], start=False, stop=True).then_inc(msg, 1)
                    pe.wait_ge(msg_out, 7)
                    def gate(c, c0, cw):
                        if c >= 2:
                            pe.wait_ge(added, c - 1)
                        b0 = 4 * (c % 2)
                        m_, h_ = FC[:, c0:c0 + cw], FA[:, c0:c0 + cw]
                        for k in range(2):
                            pt.matmul(psum[:, b0 + k, 0:cw], WT[:, 1 + k, :], m_, start=True, stop=False)
                            pt.matmul(psum[:, b0 + k, 0:cw], WT[:, 4 + k, :], h_, start=False, stop=True)
                        pt.matmul(psum[:, b0 + 2, 0:cw], WT[:, 3, :], m_, start=True, stop=True)
                        pt.matmul(psum[:, b0 + 3, 0:cw], WT[:, 6, :], h_, start=True, stop=True).then_inc(gates, 1)

                    def by_node(c, c0, cw):
                        pe.wait_ge(new, c + 1)
                        for k in range(-(-cw // P)):
                            last = pt.transpose(psum[:, 4 * (c % 2), k * P:(k + 1) * P], FB[:, c0 + k * P:c0 + (k + 1) * P], ident[:, :])
                        last.then_inc(back, 1)

                    pe.wait_ge(zero, 1)
                    for c, c0, cw in each(S):
                        gate(c, c0, cw)
                        if c:
                            by_node(*each(S)[c - 1])
                    by_node(*each(S)[6])
                    pe.wait_ge(added, 6)
                    for k in range(NT):
                        last = pt.matmul(psum[:, 7, k:k + 1], acc[:, k * P:(k + 1) * P], ones[:, 0:1], start=True, stop=True)
                    last.then_inc(src_deg, 1)

                @block.scalar
                def _(act):
                    norm_relu_act(act, norm_shift, hn_normed)
                    for c, c0, cw in each(SPAD):
                        act.wait_ge(h_by_f, c + 1)
                        a.activation(FA[:, c0:c0 + cw], psum[:, c, 0:cw], ACT.Copy).then_inc(h_out, 1)
                    for c, c0, cw in each(SPAD):
                        act.wait_ge(deg, c + 1)
                        a.activation(DB[:, c0:c0 + cw], psum[:, c, 0:cw], ACT.Copy).then_inc(deg_out, 1)
                    all_summed(act, 0)
                    for c, c0, cw in each(S)[0::2]:
                        a.activation(FB[:, c0:c0 + cw], psum[:, c, 0:cw], ACT.Copy).then_inc(sum_act, 1)
                    for c, c0, cw in each(S):
                        act.wait_ge(msg, c + 1)
                        a.activation(FC[:, c0:c0 + cw], psum[:, c, 0:cw], ACT.Copy).then_inc(msg_out, 1)
                    for c, c0, cw in each(S):
                        act.wait_ge(gates, c + 1)
                        if c:
                            act.wait_ge(new, c)
                        b0 = 4 * (c % 2)
                        a.activation(gr[:, 0:cw], psum[:, b0, 0:cw], ACT.Sigmoid, bias=col[:, 12:13])
                        a.activation(gz[:, 0:cw], psum[:, b0 + 1, 0:cw], ACT.Sigmoid, bias=col[:, 13:14]).then_inc(rz, 1)
                        act.wait_ge(pre, c + 1)
                        a.activation(gn[:, 0:cw], gn[:, 0:cw], ACT.Tanh, bias=col[:, 2:3]).then_inc(cand, 1)

                @block.vector
                def _(dve):
                    dve.wait_ge(dst_deg, 1)
                    v.tensor_scalar(dinv[:, :], psum[:, 7, 0:NT], 1.0, None, ALU.add).then_inc(dinv_in, 1)
                    norm_relu(dve, norm_shift, hn_normed)
                    dve.wait_ge(dinv_out, 1)
                    link(dve, "dve", v.tensor_tensor(col[:, 12:14], col[:, 0:2], col[:, 3:5], ALU.add))
                    v.tensor_tensor(FB.rearrange("p (t d) -> p t d", d=P), ident[:, :].unsqueeze(1).to_broadcast([P, NT, P]),
                                    dinv[:, :].unsqueeze(2).to_broadcast([P, NT, P]), ALU.mult).then_inc(diag_ready, 1)
                    split(dve)
                    all_summed(dve, 0)
                    for c, c0, cw in each(S)[1::2]:
                        v.tensor_copy(FB[:, c0:c0 + cw], psum[:, c, 0:cw]).then_inc(sum_dve, 1)
                    for c, c0, cw in each(S):
                        b0 = 4 * (c % 2)
                        dve.wait_ge(rz, c + 1)
                        link(dve, "dve", v.scalar_tensor_tensor(gn[:, 0:cw], psum[:, b0 + 3, 0:cw], col[:, 5:6], gr[:, 0:cw], ALU.add, ALU.mult))
                        v.tensor_tensor(gn[:, 0:cw], gn[:, 0:cw], psum[:, b0 + 2, 0:cw], ALU.add).then_inc(pre, 1)
                        dve.wait_ge(cand, c + 1)
                        link(dve, "dve", v.tensor_tensor(gr[:, 0:cw], FA[:, c0:c0 + cw], gn[:, 0:cw], ALU.subtract))
                        link(dve, "dve", v.tensor_tensor(gr[:, 0:cw], gr[:, 0:cw], gz[:, 0:cw], ALU.mult))
                        v.tensor_tensor(FB[:, c0:c0 + cw], gr[:, 0:cw], gn[:, 0:cw], ALU.add).then_inc(new, 1)
                        dve.wait_ge(back, c + 1)
                        xs = x[:, 4 * c:4 * c + -(-cw // P), :].rearrange("p t d -> p (t d)")
                        n_ = -(-cw // P) * P
                        v.tensor_tensor(xs, xs, psum[:, b0, 0:n_], ALU.add).then_inc(added, 1)
                        if c:
                            tile_stats(dve, added, c - 1)
                    tile_stats(dve, added, 6)
                    layer_stats(dve, x, root_in, root_out, 1, counted=True)
                    dve.wait_ge(src_deg, 1)
                    link(dve, "dve", v.tensor_scalar(rdeg[:, :], psum[:, 7, 0:NT], -1.0, 1.0, ALU.add, ALU.max))
                    v.reciprocal(rdeg[:, :], rdeg[:, :])

        def phase_conv():
            names = ("h_by_f", "h_out", "mlp", "mlp_out", "bn_in", "bn_out", "normed", "conv", "scaled", "sum_out", "biased", "back", "added", "root_in", "root_out", "shifted")
            (h_by_f, h_out, mlp, mlp_out, bn_in, bn_out, normed, conv, scaled, sum_out, biased, back, added, root_in, root_out, shifted) = (sem("c_" + n) for n in names)

            def batch_norm(dve, n, g, b, made=None):
                for c, c0, cw in each(N):
                    if made is not None:
                        dve.wait_ge(made, c + 1)
                    v.bn_stats(bn6[:, c, :], FB[:, c0:c0 + cw])
                link(dve, "dve", v.memset(marks[:, 3:4], 0.0))
                link(dve, "dve", v.bn_aggr(mv[:, 0, :], bn6[:, 0:7, :].rearrange("p c k -> p (c k)")))
                v.tensor_scalar(col[:, 18:19], mv[:, 0, 1:2], EPS, None, ALU.add).then_inc(bn_in, 1)
                dve.wait_ge(bn_out, n)
                link(dve, "dve", v.tensor_tensor(col[:, 20:21], col[:, 18:19], col[:, g:g + 1], ALU.mult))
                link(dve, "dve", v.tensor_tensor(col[:, 19:20], col[:, 20:21], mv[:, 0, 0:1], ALU.mult))
                v.tensor_tensor(col[:, 21:22], col[:, b:b + 1], col[:, 19:20], ALU.subtract).then_inc(shifted, 1)

            norm_shift, hn_normed = sem("c_norm_shift"), [sem("c_normed_dve"), sem("c_normed_act")]
            with nc.Block() as block:
                @block.sync
                def _(sp):
                    stream_counts(sp, 1, turned16, residue_turned)

                @block.gpsimd
                def _(pool):
                    for k in range(2):
                        pool.wait_ge(bn_in, k + 1)
                        gp.tensor_tensor(col[:, 18:19], col[:, 18:19], mhalf[:, 0:1], ALU.pow).then_inc(bn_out, 1)
                    pool.wait_ge(root_in, 1)
                    gp.tensor_tensor(rstd[:, :], rstd[:, :], mhalf[:, :], ALU.pow).then_inc(root_out, 1)

                @block.tensor
                def _(pe):
                    for c, c0, cw in each(SPAD):
                        normed_chunk(pe, hn_normed, c)
                        for k in range(cw // P):
                            last = pt.transpose(psum[:, c, k * P:(k + 1) * P], hn[:, 4 * c + k, :], ident[:, :])
                        last.then_inc(h_by_f, 1)
                    for c, c0, cw in each(SPAD):
                        pe.wait_ge(h_out, c + 1)
                        pt.matmul(psum[:, c, 0:cw], WT[:, 10, :], FA[:, c0:c0 + cw], start=True, stop=True).then_inc(mlp, 1)
                    for c, c0, cw in each(SPAD):
                        pe.wait_ge(normed, c + 1)
                        for k in range(cw // P):
                            last = pt.matmul(psum[:, c, k * P:(k + 1) * P], FA[:, c0 + k * P:c0 + (k + 1) * P], WT[:, 11, :], start=True, stop=True)
                        last.then_inc(conv, 1)
                    pe.wait_ge(scaled, 7)
                    sum_edges(pe, 1, self_loops=True)
                    for c, c0, cw in each(SPAD):
                        pe.wait_ge(normed, 7 + c + 1)
                        for k in range(cw // P):
                            last = pt.transpose(psum[:, c, k * P:(k + 1) * P], FA[:, c0 + k * P:c0 + (k + 1) * P], ident[:, :])
                        last.then_inc(back, 1)

                @block.scalar
                def _(act):
                    norm_relu_act(act, norm_shift, hn_normed)
                    for c, c0, cw in each(SPAD):
                        act.wait_ge(h_by_f, c + 1)
                        a.activation(FA[:, c0:c0 + cw], psum[:, c, 0:cw], ACT.Copy).then_inc(h_out, 1)
                    for c, c0, cw in each(SPAD):
                        act.wait_ge(mlp, c + 1)
                        a.activation(FB[:, c0:c0 + cw], psum[:, c, 0:cw], ACT.Identity, bias=col[:, 6:7]).then_inc(mlp_out, 1)
                    act.wait_ge(mlp_out, 7)
                    act.wait_ge(shifted, 1)
                    for c, c0, cw in each(SPAD):
                        a.activation(FA[:, c0:c0 + cw], FB[:, c0:c0 + cw], ACT.Relu, scale=col[:, 20:21], bias=col[:, 21:22]).then_inc(normed, 1)
                    for c, c0, cw in each(S):
                        act.wait_ge(sum_out, c + 1)
                        a.activation(FB[:, c0:c0 + cw], FB[:, c0:c0 + cw], ACT.Identity, bias=col[:, 9:10]).then_inc(biased, 1)
                    act.wait_ge(biased, 7)
                    act.wait_ge(shifted, 2)
                    for c, c0, cw in each(SPAD):
                        a.activation(FA[:, c0:c0 + cw], FB[:, c0:c0 + cw], ACT.Relu, scale=col[:, 20:21], bias=col[:, 21:22]).then_inc(normed, 1)

                @block.vector
                def _(dve):
                    norm_relu(dve, norm_shift, hn_normed)
                    dve.wait_ge(mlp_out, 7)
                    batch_norm(dve, 1, 7, 8)
                    for c, c0, cw in each(SPAD):
                        k0, n_ = 4 * c, cw // P
                        dve.wait_ge(conv, c + 1)
                        v.tensor_tensor(hn[:, k0:k0 + n_, :], psum[:, c, 0:cw].rearrange("p (t d) -> p t d", d=D),
                                        dinv[:, k0:k0 + n_].unsqueeze(2).to_broadcast([P, n_, D]), ALU.mult).then_inc(scaled, 1)
                    dve.wait_ge(scaled, 7)
                    split(dve)
                    all_summed(dve, 1)
                    for c, c0, cw in each(S):
                        v.tensor_tensor(FB[:, c0:c0 + cw], psum[:, c, 0:cw], DB[:, c0:c0 + cw], ALU.mult).then_inc(sum_out, 1)
                    batch_norm(dve, 2, 10, 11, biased)
                    for c, c0, cw in each(SPAD):
                        dve.wait_ge(back, c + 1)
                        xs = x[:, 4 * c:4 * c + cw // P, :].rearrange("p t d -> p (t d)")
                        v.tensor_tensor(xs, xs, psum[:, c, 0:cw], ALU.add).then_inc(added, 1)
                        if c:
                            tile_stats(dve, added, c - 1)
                    tile_stats(dve, added, 6)
                    layer_stats(dve, x, root_in, root_out, 1, counted=True)

        def phase_mean():
            names = ("h_by_f", "h_out", "lin", "lin_out", "sum_out_act", "sum_out_dve", "out_ready", "out_st")
            h_by_f, h_out, lin, lin_out, sum_act, sum_dve, out_ready, out_st = (sem("m_" + n) for n in names)
            norm_shift, hn_normed = sem("m_norm_shift"), [sem("m_normed_dve"), sem("m_normed_act")]
            with nc.Block() as block:
                @block.sync
                def _(sp):
                    stream_counts(sp, 2, rows16, residue)
                    stream_counts(sp, 3, rows16, residue)
                    sp.wait_ge(out_ready, 1)
                    sp.dma_start(out[0:(NT - 1) * P, :].rearrange("(t p) d -> p t d", p=P), hn[:, 0:NT - 1, :]).then_inc(out_st, 16)
                    sp.dma_start(out[(NT - 1) * P:N, :], hn[0:TAIL, NT - 1, :]).then_inc(out_st, 16)
                    sp.wait_ge(out_st, 32)

                @block.tensor
                def _(pe):
                    for c, c0, cw in each(SPAD):
                        normed_chunk(pe, hn_normed, c)
                        for k in range(cw // P):
                            last = pt.transpose(psum[:, c, k * P:(k + 1) * P], hn[:, 4 * c + k, :], ident[:, :])
                        last.then_inc(h_by_f, 1)

                    def linear(src, w):
                        for c, c0, cw in each(SPAD):
                            for k in range(cw // P):
                                last = pt.matmul(psum[:, c, k * P:(k + 1) * P], src[:, c0 + k * P:c0 + (k + 1) * P], WT[:, w, :], start=True, stop=True)
                            last.then_inc(lin, 1)

                    pe.wait_ge(h_out, 7)
                    linear(FA, 7)
                    for k in range(2):
                        pe.wait_ge(lin_out, 7 * (k + 1))
                        sum_edges(pe, 2 + k)
                        pe.wait_ge(sum_act, 4 * (k + 1))
                        pe.wait_ge(sum_dve, 3 * (k + 1))
                        linear(FB, 8 + k)

                @block.scalar
                def _(act):
                    norm_relu_act(act, norm_shift, hn_normed)
                    for c, c0, cw in each(SPAD):
                        act.wait_ge(h_by_f, c + 1)
                        a.activation(FA[:, c0:c0 + cw], psum[:, c, 0:cw], ACT.Copy).then_inc(h_out, 1)
                    for k in range(2):
                        all_summed(act, 2 + k)
                        for c, c0, cw in each(S)[0::2]:
                            a.activation(FB[:, c0:c0 + cw], psum[:, c, 0:cw], ACT.Relu).then_inc(sum_act, 1)

                @block.vector
                def _(dve):
                    norm_relu(dve, norm_shift, hn_normed)
                    for k in range(3):
                        for c, c0, cw in each(SPAD):
                            k0, n_ = 4 * c, cw // P
                            o, src = hn[:, k0:k0 + n_, :], psum[:, c, 0:cw].rearrange("p (t d) -> p t d", d=D)
                            dve.wait_ge(lin, 7 * k + c + 1)
                            if k == 0:
                                v.tensor_tensor(o, src, bc_vec(3, n_), ALU.add).then_inc(lin_out, 1)
                            else:
                                v.tensor_tensor(o, src, rdeg[:, k0:k0 + n_].unsqueeze(2).to_broadcast([P, n_, D]), ALU.mult).then_inc(lin_out, 1)
                        dve.wait_ge(lin_out, 7 * (k + 1))
                        if k:
                            link(dve, "dve", v.tensor_tensor(hn, hn, bc_vec(3 + k), ALU.add))
                        if k == 2:
                            v.tensor_tensor(hn, hn, x, ALU.add).then_inc(out_ready, 1)
                            break
                        split(dve)
                        all_summed(dve, 2 + k)
                        for c, c0, cw in each(S)[1::2]:
                            v.tensor_scalar(FB[:, c0:c0 + cw], psum[:, c, 0:cw], 0.0, None, ALU.max).then_inc(sum_dve, 1)

        acc_done, shift_step, shifted = sem("a_acc_done"), sem("a_shift_step"), sem("a_shifted")
        tt_in = sem("types_in")
        res_step = sem("residue_step")
        split_done, sums_done, res_in, res_used = sem("split_done"), sem("sums_done"), sem("residue_in"), sem("residue_used")
        ring_in = [sem(f"ring_in{i}") for i in range(4)]
        ring_used = [sem(f"ring_used{i}") for i in range(4)]
        phase_counts()
        phase_nodes()
        phase_attention()
        phase_attention_end()
        phase_residue()
        phase_gated()
        phase_conv()
        phase_mean()


_IN = ["x", "src", "dst", "edge_type_9", "L0_gnn_W", "L0_gnn_a_src", "L0_gnn_a_dst", "L0_gnn_bias", "L0_gnn_gamma", "L0_gnn_beta",
       "L1_gnn_W_msg", "L1_gnn_b_msg", "L1_gnn_edge_embed", "L1_gnn_W_ih", "L1_gnn_W_hh", "L1_gnn_b_ih", "L1_gnn_b_hh",
       "L2_gnn_W_mlp", "L2_gnn_b_mlp", "L2_gnn_gamma1", "L2_gnn_beta1", "L2_gnn_W_conv", "L2_gnn_b_conv", "L2_gnn_gamma2", "L2_gnn_beta2",
       "L3_gnn_W1", "L3_gnn_b1", "L3_gnn_W2", "L3_gnn_b2", "L3_gnn_W3", "L3_gnn_b3"]


def kernel(**inputs):
    import concourse.bacc as _bacc
    from concourse.bass_utils import run_bass_kernel_spmd as _run
    nc = _bacc.Bacc("TRN2", target_bir_lowering=False, num_devices=1)
    arrays, aps = {}, {}
    for name in _IN:
        a = np.ascontiguousarray(inputs[name])
        arrays[f"in_{name}"] = a
        aps[name] = nc.dram_tensor(f"in_{name}", a.shape, mybir.dt.from_np(a.dtype), kind="ExternalInput").ap()
    out = nc.dram_tensor("out_x", (N, D), F32, kind="ExternalOutput").ap()
    gnn_program(nc, aps, out)
    r = _run(nc, [arrays], core_ids=[0])
    return r.results[0]["out_x"]
```
